# Optimizing a Trainium2 kernel written in Bass

```python
import numpy as np
import jax
import jax.numpy as jnp

def _softmax(x, axis=-1):
    return jax.nn.softmax(x, axis=axis)

def _gelu(x):
    return jax.nn.gelu(x, approximate=True)

def _silu(x):
    return jax.nn.silu(x)

def _sigmoid(x):
    return jax.nn.sigmoid(x)

def _layernorm(x, axis=-1, eps=1e-05):
    m = jnp.mean(x, axis=axis, keepdims=True)
    v = jnp.var(x, axis=axis, keepdims=True)
    return (x - m) / jnp.sqrt(v + eps)

def _scatter_add(tgt, idx, src, axis=0):
    return tgt.at[idx].add(src)

def _segment_sum(src, seg, n):
    return jax.ops.segment_sum(src, seg, n)
kernel_name = 'mk_cond_seq_d4_seqx_r4_17102b'

def setup_inputs(seed: int=0):
    np.random.seed(seed)
    _w = jnp.asarray

    def _rec_inputs():
        import jax
        import jax.numpy as jnp
        _rk = jax.random.key(seed)
        x = -0.0002928 + 1 * jax.random.normal(jax.random.fold_in(_rk, 1), (128, 64, 256), jnp.float32)
        _lenS = 64 - jax.random.randint(jax.random.fold_in(_rk, 7), (128,), 0, max(1, 64 // 4) + 1, jnp.int32)
        _lenS2 = 64 - jax.random.randint(jax.random.fold_in(_rk, 8), (128,), 0, max(1, 64 // 4) + 1, jnp.int32)
        itok_B_0_7 = jax.random.randint(jax.random.fold_in(_rk, 11), (128,), 0, 8, jnp.int32)
        itok_B_34_63 = jax.random.randint(jax.random.fold_in(_rk, 13), (128,), 34, 64, jnp.int32)
        fside_Bx16xSxS_0 = -1.47943e-05 + 1.00017 * jax.random.normal(jax.random.fold_in(_rk, 14), (128, 16, 64, 64), jnp.float32)
        condB_safetyscore = -0.927215 + 0.920279 * jax.random.normal(jax.random.fold_in(_rk, 15), (128,), jnp.float32)
        itok_B_0_2 = jax.random.randint(jax.random.fold_in(_rk, 16), (128,), 0, 3, jnp.int32)
        _validS = jnp.arange(64)[None, :] < _lenS[:, None]
        _validS2 = jnp.arange(64)[None, :] < _lenS2[:, None]
        _causal = jnp.tril(jnp.ones((64, 64), dtype=bool))
        mask_Bx1xSxS_bk0 = jnp.logical_not(jnp.broadcast_to(_validS[:, None, None, :], (128, 1, 64, 64)))
        return (x, itok_B_0_7, itok_B_34_63, fside_Bx16xSxS_0, condB_safetyscore, itok_B_0_2, mask_Bx1xSxS_bk0)
    x, itok_B_0_7, itok_B_34_63, fside_Bx16xSxS_0, condB_safetyscore, itok_B_0_2, mask_Bx1xSxS_bk0 = _rec_inputs()

    def _L0_cond_setup():
        import jax, jax.numpy as jnp
        import numpy as np
        E, H, I = (8, 256, 1024)
        B, S = (4, 256)
        LN_EPS = 1e-12
        key = jax.random.key(seed)
        ks = jax.random.split(key, 8)
        x = jax.random.normal(ks[0], (B, S, H), dtype=jnp.float32)
        expert_idx = jax.random.randint(ks[1], (B,), 0, E, dtype=jnp.int64)
        Wi = jax.random.normal(ks[2], (E, H, I), dtype=jnp.float32) * 0.02
        bi = jnp.zeros((E, I), dtype=jnp.float32)
        Wo = jax.random.normal(ks[3], (E, I, H), dtype=jnp.float32) * 0.02
        bo = jnp.zeros((E, H), dtype=jnp.float32)
        gamma = jnp.ones((E, H), dtype=jnp.float32)
        beta = jnp.zeros((E, H), dtype=jnp.float32)
        return {'input_tensor': x, 'expert_idx': expert_idx, 'Wi': Wi, 'bi': bi, 'Wo': Wo, 'bo': bo, 'gamma': gamma, 'beta': beta}
    _L0_cond_all = _L0_cond_setup()
    _L0_cond_in = {k: v for k, v in _L0_cond_all.items() if k in ('Wi', 'bi', 'Wo', 'bo', 'gamma', 'beta')}
    del _L0_cond_all

    def _L1_cond_setup():
        import jax, jax.numpy as jnp
        import numpy as np
        import math
        D_MODEL = 256
        N_HEAD = 16
        HEAD_DIM = D_MODEL // N_HEAD
        D_FF = 1024
        NUM_STEPS = 100.0
        RESCALE = 4000.0
        EPS = 1e-05

        def _sin_emb(t):
            half = D_MODEL // 2
            x = t.astype(jnp.float32) / NUM_STEPS * RESCALE
            freqs = jnp.exp(jnp.arange(half, dtype=jnp.float32) * (-math.log(10000.0) / (half - 1)))
            e = x[:, None] * freqs[None, :]
            return jnp.concatenate([jnp.sin(e), jnp.cos(e)], axis=-1)

        def _ln(x):
            m = jnp.mean(x, axis=-1, keepdims=True)
            v = jnp.var(x, axis=-1, keepdims=True)
            return (x - m) / jnp.sqrt(v + EPS)

        def _gelu2(x):
            return x * jax.nn.sigmoid(1.702 * x)
        key = jax.random.key(seed)
        ks = jax.random.split(key, 24)
        B, S, D, F = (4, 128, D_MODEL, D_FF)
        std = 0.02
        inp = {'src': jax.random.normal(ks[0], (B, S, D), dtype=jnp.float32), 'src_mask': jax.random.randint(ks[1], (B, 1, S, S), 0, 2).astype(bool), 'timestep': jax.random.randint(ks[2], (B,), 0, 100, dtype=jnp.int32), 'attention_bias': jax.random.normal(ks[3], (B, N_HEAD, S, S), dtype=jnp.float32), 'W_ada': jax.random.normal(ks[4], (D, 2 * D), dtype=jnp.float32) * std, 'b_ada': jnp.zeros((2 * D,), dtype=jnp.float32), 'Wq': jax.random.normal(ks[5], (D, D), dtype=jnp.float32) * std, 'bq': jnp.zeros((D,), dtype=jnp.float32), 'Wk': jax.random.normal(ks[6], (D, D), dtype=jnp.float32) * std, 'bk': jnp.zeros((D,), dtype=jnp.float32), 'Wv': jax.random.normal(ks[7], (D, D), dtype=jnp.float32) * std, 'bv': jnp.zeros((D,), dtype=jnp.float32), 'Wo': jax.random.normal(ks[8], (D, D), dtype=jnp.float32) * std, 'bo': jnp.zeros((D,), dtype=jnp.float32), 'W1': jax.random.normal(ks[9], (D, F), dtype=jnp.float32) * std, 'b1': jnp.zeros((F,), dtype=jnp.float32), 'W2': jax.random.normal(ks[10], (F, D), dtype=jnp.float32) * std, 'b2': jnp.zeros((D,), dtype=jnp.float32), 'g2': jnp.ones((D,), dtype=jnp.float32), 'beta2': jnp.zeros((D,), dtype=jnp.float32)}
        return inp
    _L1_cond_all = _L1_cond_setup()
    _L1_cond_in = {k: v for k, v in _L1_cond_all.items() if k in ('W_ada', 'b_ada', 'Wq', 'bq', 'Wk', 'bk', 'Wv', 'bv', 'Wo', 'bo', 'W1', 'b1', 'W2', 'b2', 'g2', 'beta2')}
    del _L1_cond_all

    def _L2_cond_setup():
        import jax, jax.numpy as jnp
        import numpy as np
        TEMPERATURE = 1.0
        ACT_THRESHOLD = 0.1
        MAX_ACT = 1.0
        SAFETY_KNOB = 1.0
        EPS = 1e-08

        def gram_schmidt(X):
            r = X.shape[1]
            Q = X
            for i in range(r):
                q = Q[:, i]
                q = q / (jnp.linalg.norm(q) + EPS)
                Q = Q.at[:, i].set(q)
                coeffs = q @ Q[:, i + 1:]
                Q = Q.at[:, i + 1:].add(-jnp.outer(q, coeffs))
            return Q
        key = jax.random.key(seed)
        ks = jax.random.split(key, 8)
        B, S, D, R = (8, 1024, 256, 32)
        init_std = 0.02
        return {'hidden_states': jax.random.normal(ks[0], (B, S, D), jnp.float32), 'safety_score': jax.random.normal(ks[1], (B,), jnp.float32), 'U': jax.random.normal(ks[2], (D, R), jnp.float32) * init_std, 'V': jax.random.normal(ks[3], (D, R), jnp.float32) * init_std, 'safety_bias': jnp.zeros((D,), jnp.float32), 'gate_w1': jax.random.normal(ks[4], (D // 4, D), jnp.float32) * (1.0 / np.sqrt(D)), 'gate_b1': jnp.zeros((D // 4,), jnp.float32), 'gate_w2': jax.random.normal(ks[5], (1, D // 4), jnp.float32) * (1.0 / np.sqrt(D // 4)), 'gate_b2': jnp.zeros((1,), jnp.float32), 'resp_w': jax.random.normal(ks[6], (D, R), jnp.float32) * (1.0 / np.sqrt(R)), 'resp_b': jnp.zeros((D,), jnp.float32)}
    _L2_cond_all = _L2_cond_setup()
    _L2_cond_in = {k: v for k, v in _L2_cond_all.items() if k in ('U', 'V', 'safety_bias', 'gate_w1', 'gate_b1', 'gate_w2', 'gate_b2', 'resp_w', 'resp_b')}
    del _L2_cond_all

    def _L3_cond_setup():
        import jax, jax.numpy as jnp
        import numpy as np
        H = 256
        EPS = 1e-05

        def _gelu(x):
            return jax.nn.gelu(x, approximate=False)
        key = jax.random.key(seed)
        ks = jax.random.split(key, 16)
        s = 1.0 / np.sqrt(H)
        inp = {'x': jax.random.normal(ks[0], (64, 256, H), dtype=jnp.float32), 'condition': jax.random.randint(ks[1], (64,), 0, 3), 'w1_nr': jax.random.normal(ks[2], (H, H), dtype=jnp.float32) * s, 'b1_nr': jnp.zeros((H,), dtype=jnp.float32), 'w2_nr': jax.random.normal(ks[3], (H, H), dtype=jnp.float32) * s, 'b2_nr': jnp.zeros((H,), dtype=jnp.float32), 'w1_tsr': jax.random.normal(ks[4], (H, H), dtype=jnp.float32) * s, 'b1_tsr': jnp.zeros((H,), dtype=jnp.float32), 'w2_tsr': jax.random.normal(ks[5], (H, H), dtype=jnp.float32) * s, 'b2_tsr': jnp.zeros((H,), dtype=jnp.float32), 'w1_sr': jax.random.normal(ks[6], (H, 2 * H), dtype=jnp.float32) * s, 'b1_sr': jnp.zeros((2 * H,), dtype=jnp.float32), 'w2_sr': jax.random.normal(ks[7], (2 * H, H), dtype=jnp.float32) * (1.0 / np.sqrt(2 * H)), 'b2_sr': jnp.zeros((H,), dtype=jnp.float32), 'w3_sr': jax.random.normal(ks[8], (H, H), dtype=jnp.float32) * s, 'b3_sr': jnp.zeros((H,), dtype=jnp.float32), 'gamma': jnp.ones((H,), dtype=jnp.float32), 'beta': jnp.zeros((H,), dtype=jnp.float32)}
        return inp
    _L3_cond_all = _L3_cond_setup()
    _L3_cond_in = {k: v for k, v in _L3_cond_all.items() if k in ('w1_nr', 'b1_nr', 'w2_nr', 'b2_nr', 'w1_tsr', 'b1_tsr', 'w2_tsr', 'b2_tsr', 'w1_sr', 'b1_sr', 'w2_sr', 'b2_sr', 'w3_sr', 'b3_sr', 'gamma', 'beta')}
    del _L3_cond_all
    return {'x': x, 'itok_B_0_7': itok_B_0_7, 'itok_B_34_63': itok_B_34_63, 'fside_Bx16xSxS_0': fside_Bx16xSxS_0, 'condB_safetyscore': condB_safetyscore, 'itok_B_0_2': itok_B_0_2, 'mask_Bx1xSxS_bk0': mask_Bx1xSxS_bk0, 'L0_cond_Wi': _L0_cond_in['Wi'], 'L0_cond_bi': _L0_cond_in['bi'], 'L0_cond_Wo': _L0_cond_in['Wo'], 'L0_cond_bo': _L0_cond_in['bo'], 'L0_cond_gamma': _L0_cond_in['gamma'], 'L0_cond_beta': _L0_cond_in['beta'], 'L1_cond_W_ada': _L1_cond_in['W_ada'], 'L1_cond_b_ada': _L1_cond_in['b_ada'], 'L1_cond_Wq': _L1_cond_in['Wq'], 'L1_cond_bq': _L1_cond_in['bq'], 'L1_cond_Wk': _L1_cond_in['Wk'], 'L1_cond_bk': _L1_cond_in['bk'], 'L1_cond_Wv': _L1_cond_in['Wv'], 'L1_cond_bv': _L1_cond_in['bv'], 'L1_cond_Wo': _L1_cond_in['Wo'], 'L1_cond_bo': _L1_cond_in['bo'], 'L1_cond_W1': _L1_cond_in['W1'], 'L1_cond_b1': _L1_cond_in['b1'], 'L1_cond_W2': _L1_cond_in['W2'], 'L1_cond_b2': _L1_cond_in['b2'], 'L1_cond_g2': _L1_cond_in['g2'], 'L1_cond_beta2': _L1_cond_in['beta2'], 'L2_cond_U': _L2_cond_in['U'], 'L2_cond_V': _L2_cond_in['V'], 'L2_cond_safety_bias': _L2_cond_in['safety_bias'], 'L2_cond_gate_w1': _L2_cond_in['gate_w1'], 'L2_cond_gate_b1': _L2_cond_in['gate_b1'], 'L2_cond_gate_w2': _L2_cond_in['gate_w2'], 'L2_cond_gate_b2': _L2_cond_in['gate_b2'], 'L2_cond_resp_w': _L2_cond_in['resp_w'], 'L2_cond_resp_b': _L2_cond_in['resp_b'], 'L3_cond_w1_nr': _L3_cond_in['w1_nr'], 'L3_cond_b1_nr': _L3_cond_in['b1_nr'], 'L3_cond_w2_nr': _L3_cond_in['w2_nr'], 'L3_cond_b2_nr': _L3_cond_in['b2_nr'], 'L3_cond_w1_tsr': _L3_cond_in['w1_tsr'], 'L3_cond_b1_tsr': _L3_cond_in['b1_tsr'], 'L3_cond_w2_tsr': _L3_cond_in['w2_tsr'], 'L3_cond_b2_tsr': _L3_cond_in['b2_tsr'], 'L3_cond_w1_sr': _L3_cond_in['w1_sr'], 'L3_cond_b1_sr': _L3_cond_in['b1_sr'], 'L3_cond_w2_sr': _L3_cond_in['w2_sr'], 'L3_cond_b2_sr': _L3_cond_in['b2_sr'], 'L3_cond_w3_sr': _L3_cond_in['w3_sr'], 'L3_cond_b3_sr': _L3_cond_in['b3_sr'], 'L3_cond_gamma': _L3_cond_in['gamma'], 'L3_cond_beta': _L3_cond_in['beta']}

def reference(x, itok_B_0_7, itok_B_34_63, fside_Bx16xSxS_0, condB_safetyscore, itok_B_0_2, mask_Bx1xSxS_bk0, L0_cond_Wi, L0_cond_bi, L0_cond_Wo, L0_cond_bo, L0_cond_gamma, L0_cond_beta, L1_cond_W_ada, L1_cond_b_ada, L1_cond_Wq, L1_cond_bq, L1_cond_Wk, L1_cond_bk, L1_cond_Wv, L1_cond_bv, L1_cond_Wo, L1_cond_bo, L1_cond_W1, L1_cond_b1, L1_cond_W2, L1_cond_b2, L1_cond_g2, L1_cond_beta2, L2_cond_U, L2_cond_V, L2_cond_safety_bias, L2_cond_gate_w1, L2_cond_gate_b1, L2_cond_gate_w2, L2_cond_gate_b2, L2_cond_resp_w, L2_cond_resp_b, L3_cond_w1_nr, L3_cond_b1_nr, L3_cond_w2_nr, L3_cond_b2_nr, L3_cond_w1_tsr, L3_cond_b1_tsr, L3_cond_w2_tsr, L3_cond_b2_tsr, L3_cond_w1_sr, L3_cond_b1_sr, L3_cond_w2_sr, L3_cond_b2_sr, L3_cond_w3_sr, L3_cond_b3_sr, L3_cond_gamma, L3_cond_beta):
    import jax
    import jax.numpy as jnp

    def _L0_cond_ref(input_tensor, expert_idx, Wi, bi, Wo, bo, gamma, beta):
        import jax, jax.numpy as jnp
        import numpy as np
        E, H, I = (8, 256, 1024)
        B, S = (4, 256)
        LN_EPS = 1e-12
        Wi_b = Wi[expert_idx]
        bi_b = bi[expert_idx]
        Wo_b = Wo[expert_idx]
        bo_b = bo[expert_idx]
        g_b = gamma[expert_idx]
        be_b = beta[expert_idx]
        h = jax.nn.gelu(jnp.einsum('bsh,bhi->bsi', input_tensor, Wi_b) + bi_b[:, None, :], approximate=False)
        o = jnp.einsum('bsi,bih->bsh', h, Wo_b) + bo_b[:, None, :]
        r = o + input_tensor
        mu = jnp.mean(r, axis=-1, keepdims=True)
        var = jnp.mean(jnp.square(r - mu), axis=-1, keepdims=True)
        y = (r - mu) * jax.lax.rsqrt(var + LN_EPS)
        return y * g_b[:, None, :] + be_b[:, None, :]

    def _L1_cond_ref(src, src_mask, timestep, attention_bias, W_ada, b_ada, Wq, bq, Wk, bk, Wv, bv, Wo, bo, W1, b1, W2, b2, g2, beta2):
        import jax, jax.numpy as jnp
        import numpy as np
        import math
        D_MODEL = 256
        N_HEAD = 16
        HEAD_DIM = D_MODEL // N_HEAD
        D_FF = 1024
        NUM_STEPS = 100.0
        RESCALE = 4000.0
        EPS = 1e-05

        def _sin_emb(t):
            half = D_MODEL // 2
            x = t.astype(jnp.float32) / NUM_STEPS * RESCALE
            freqs = jnp.exp(jnp.arange(half, dtype=jnp.float32) * (-math.log(10000.0) / (half - 1)))
            e = x[:, None] * freqs[None, :]
            return jnp.concatenate([jnp.sin(e), jnp.cos(e)], axis=-1)

        def _ln(x):
            m = jnp.mean(x, axis=-1, keepdims=True)
            v = jnp.var(x, axis=-1, keepdims=True)
            return (x - m) / jnp.sqrt(v + EPS)

        def _gelu2(x):
            return x * jax.nn.sigmoid(1.702 * x)
        B, S, D = src.shape
        emb = jax.nn.silu(_sin_emb(timestep)) @ W_ada + b_ada
        scale, shift = jnp.split(emb[:, None, :], 2, axis=-1)
        x = _ln(src) * (1.0 + scale) + shift
        q = (x @ Wq + bq).reshape(B, S, N_HEAD, HEAD_DIM).transpose(0, 2, 1, 3)
        k = (x @ Wk + bk).reshape(B, S, N_HEAD, HEAD_DIM).transpose(0, 2, 1, 3)
        v = (x @ Wv + bv).reshape(B, S, N_HEAD, HEAD_DIM).transpose(0, 2, 1, 3)
        scores = jnp.einsum('bhqd,bhkd->bhqk', q / math.sqrt(HEAD_DIM), k)
        scores = scores + attention_bias
        scores = jnp.where(src_mask, -jnp.inf, scores.astype(jnp.float32))
        probs = jax.nn.softmax(scores, axis=-1).astype(v.dtype)
        ctx = jnp.einsum('bhqk,bhkd->bhqd', probs, v)
        ctx = ctx.transpose(0, 2, 1, 3).reshape(B, S, D)
        x = x + (ctx @ Wo + bo)
        h = _ln(x) * g2 + beta2
        ff = _gelu2(h @ W1 + b1) @ W2 + b2
        return x + ff

    def _L2_cond_ref(hidden_states, safety_score, U, V, safety_bias, gate_w1, gate_b1, gate_w2, gate_b2, resp_w, resp_b):
        import jax, jax.numpy as jnp
        import numpy as np
        TEMPERATURE = 1.0
        ACT_THRESHOLD = 0.1
        MAX_ACT = 1.0
        SAFETY_KNOB = 1.0
        EPS = 1e-08

        def gram_schmidt(X):
            r = X.shape[1]
            Q = X
            for i in range(r):
                q = Q[:, i]
                q = q / (jnp.linalg.norm(q) + EPS)
                Q = Q.at[:, i].set(q)
                coeffs = q @ Q[:, i + 1:]
                Q = Q.at[:, i + 1:].add(-jnp.outer(q, coeffs))
            return Q
        R = resp_w.shape[1]
        U_o = gram_schmidt(U)
        V_o = gram_schmidt(V)
        basis = U_o @ V_o.T
        pooled = hidden_states.mean(axis=1)
        h1 = jax.nn.relu(pooled @ gate_w1.T + gate_b1)
        base_act = jax.nn.sigmoid(h1 @ gate_w2.T + gate_b2)
        mod = jax.nn.sigmoid(safety_score[:, None] / TEMPERATURE)
        knob = jnp.clip(jnp.asarray(SAFETY_KNOB, hidden_states.dtype), ACT_THRESHOLD, MAX_ACT)
        strength = (base_act * mod * knob)[:, None, :]
        proj = hidden_states @ basis
        feats = proj @ basis.T[:, :R]
        response = feats @ resp_w.T + resp_b + safety_bias
        return hidden_states + strength * response

    def _L3_cond_ref(x, condition, w1_nr, b1_nr, w2_nr, b2_nr, w1_tsr, b1_tsr, w2_tsr, b2_tsr, w1_sr, b1_sr, w2_sr, b2_sr, w3_sr, b3_sr, gamma, beta):
        import jax, jax.numpy as jnp
        import numpy as np
        H = 256
        EPS = 1e-05

        def _gelu(x):
            return jax.nn.gelu(x, approximate=False)
        out_nr = _gelu(jnp.einsum('bth,hk->btk', x, w1_nr) + b1_nr)
        out_nr = jnp.einsum('bth,hk->btk', out_nr, w2_nr) + b2_nr
        out_tsr = _gelu(jnp.einsum('bth,hk->btk', x, w1_tsr) + b1_tsr)
        out_tsr = jnp.einsum('bth,hk->btk', out_tsr, w2_tsr) + b2_tsr
        h = _gelu(jnp.einsum('bth,hk->btk', x, w1_sr) + b1_sr)
        h = _gelu(jnp.einsum('bth,hk->btk', h, w2_sr) + b2_sr)
        out_sr = jnp.einsum('bth,hk->btk', h, w3_sr) + b3_sr
        c = condition[:, None, None]
        out = jnp.where(c == 0, out_nr, jnp.where(c == 1, out_tsr, jnp.where(c == 2, out_sr, jnp.zeros_like(x))))
        y = x + out
        mu = jnp.mean(y, axis=-1, keepdims=True)
        var = jnp.mean((y - mu) ** 2, axis=-1, keepdims=True)
        return (y - mu) * jax.lax.rsqrt(var + EPS) * gamma + beta
    x = _L0_cond_ref(x, itok_B_0_7, L0_cond_Wi, L0_cond_bi, L0_cond_Wo, L0_cond_bo, L0_cond_gamma, L0_cond_beta)
    x = _L1_cond_ref(x, mask_Bx1xSxS_bk0, itok_B_34_63, fside_Bx16xSxS_0, L1_cond_W_ada, L1_cond_b_ada, L1_cond_Wq, L1_cond_bq, L1_cond_Wk, L1_cond_bk, L1_cond_Wv, L1_cond_bv, L1_cond_Wo, L1_cond_bo, L1_cond_W1, L1_cond_b1, L1_cond_W2, L1_cond_b2, L1_cond_g2, L1_cond_beta2)
    x = _L2_cond_ref(x, condB_safetyscore, L2_cond_U, L2_cond_V, L2_cond_safety_bias, L2_cond_gate_w1, L2_cond_gate_b1, L2_cond_gate_w2, L2_cond_gate_b2, L2_cond_resp_w, L2_cond_resp_b)
    x = _L3_cond_ref(x, itok_B_0_2, L3_cond_w1_nr, L3_cond_b1_nr, L3_cond_w2_nr, L3_cond_b2_nr, L3_cond_w1_tsr, L3_cond_b1_tsr, L3_cond_w2_tsr, L3_cond_b2_tsr, L3_cond_w1_sr, L3_cond_b1_sr, L3_cond_w2_sr, L3_cond_b2_sr, L3_cond_w3_sr, L3_cond_b3_sr, L3_cond_gamma, L3_cond_beta)
    return x

_drawn_inputs = setup_inputs


def setup_inputs(seed=0):
    import zlib

    import numpy as np

    out = dict(_drawn_inputs(seed))
    spreads = {'L0_cond_bi': (0.0, 0.1),
     'L0_cond_bo': (0.0, 0.1),
     'L0_cond_gamma': (1.0, 0.2),
     'L0_cond_beta': (0.0, 0.1),
     'L1_cond_b_ada': (0.0, 0.1),
     'L1_cond_bq': (0.0, 0.8),
     'L1_cond_bk': (0.0, 2.0),
     'L1_cond_bv': (0.0, 0.271),
     'L1_cond_bo': (0.0, 0.1),
     'L1_cond_b1': (0.0, 0.1),
     'L1_cond_b2': (0.0, 0.1),
     'L1_cond_g2': (1.0, 0.6),
     'L1_cond_beta2': (0.0, 0.666),
     'L2_cond_safety_bias': (0.0, 0.424),
     'L2_cond_gate_b1': (0.0, 2.0),
     'L2_cond_resp_b': (0.0, 0.394),
     'L3_cond_b1_nr': (0.0, 0.27),
     'L3_cond_b2_nr': (0.0, 0.1),
     'L3_cond_b1_tsr': (0.0, 0.268),
     'L3_cond_b2_tsr': (0.0, 0.1),
     'L3_cond_b1_sr': (0.0, 0.361),
     'L3_cond_b2_sr': (0.0, 0.1),
     'L3_cond_b3_sr': (0.0, 0.1),
     'L3_cond_gamma': (1.0, 0.2),
     'L3_cond_beta': (0.0, 0.1)}
    factors = {'fside_Bx16xSxS_0': 3.519,
     'L1_cond_Wq': 8.0,
     'L1_cond_Wk': 8.0,
     'L2_cond_V': 64.0,
     'L2_cond_gate_w1': 8.0,
     'L2_cond_gate_w2': 8.0}
    for name, (base, spread) in spreads.items():
        noise = np.random.default_rng([zlib.crc32(name.encode()), seed]).standard_normal(out[name].shape)
        drawn = base * np.exp(spread * noise) if base else spread * noise
        out[name] = jnp.asarray(drawn.astype(out[name].dtype))
    for name, factor in factors.items():
        out[name] = (out[name] * factor).astype(out[name].dtype)
    return out
```

```python
from contextlib import ExitStack

import numpy as np

import concourse.bass as bass
from concourse import mybir

F32 = mybir.dt.float32
F32R = mybir.dt.float32r
I32 = mybir.dt.int32
U8 = mybir.dt.uint8
ACT = mybir.ActivationFunctionType
ALU = mybir.AluOpType
X = mybir.AxisListType.X

P = 128
B, S, D = 128, 64, 256
E, FF = 8, 1024
NH, HD = 16, 16
R = 32
QS = 4
PAIRS = QS * S // P
TQ = QS * S
KC = D // P
FC = FF // P
NQ = B // QS
CLS = 4
A_TILES = NQ + E
C_TILES = NQ + CLS
A_SLOTS = QS * (A_TILES + 1)
C_SLOTS = QS * (C_TILES + 1)
ROWS = B + QS
MASKED = -1e30

CONST = {}
_n = 0
for _name, _w in (("ident", P), ("before", P), ("ones", P), ("slot", A_SLOTS), ("slot4", A_SLOTS),
                  ("quads", NQ), ("class", E), ("less", E * E), ("freq", 1), ("head", 2), ("sample", 1),
                  ("later", R)):
    CONST[_name] = (_n, _n + _w)
    _n += _w
CONST_W = _n

COLS = {}
_n = 0
for _name, _w in (("L0_cond_bi", E * FC), ("L1_cond_bq", KC), ("L1_cond_bk", KC), ("L1_cond_b1", FC),
                  ("L1_cond_g2", KC), ("L1_cond_beta2", KC), ("L3_cond_b1_nr", KC), ("L3_cond_b1_tsr", KC),
                  ("L3_cond_b1_sr", 2 * KC), ("L3_cond_b2_sr", KC)):
    COLS[_name] = (_n, _n + _w)
    _n += _w
COLS_W = _n

ROWS_OF = {}
_n = 0
for _name, _w in (("L1_cond_bv", 1),
                  ("L1_cond_bo", 1), ("L1_cond_b2", 1), ("L2_cond_resp_b", 1), ("L2_cond_safety_bias", 1),
                  ("L3_cond_b2_nr", 1), ("L3_cond_b2_tsr", 1), ("L3_cond_b3_sr", 1), ("L3_cond_gamma", 1),
                  ("L3_cond_beta", 1)):
    ROWS_OF[_name] = (_n, _n + _w)
    _n += _w
ROWS_W = _n

EROWS = ("L0_cond_bo", "L0_cond_gamma", "L0_cond_beta")
WB = (("L1_cond_Wq", KC, D), ("L1_cond_Wk", KC, D), ("L1_cond_Wv", KC, D), ("L1_cond_Wo", KC, D),
      ("L1_cond_W1", KC, FF), ("L1_cond_W2", FC, D))
WC = (("L3_cond_w1_nr", KC, D), ("L3_cond_w2_nr", KC, D), ("L3_cond_w1_tsr", KC, D), ("L3_cond_w2_tsr", KC, D),
      ("L3_cond_w1_sr", KC, 2 * D), ("L3_cond_w2_sr", 2 * KC, D), ("L3_cond_w3_sr", KC, D))
STAGE = 2048
B_STAGES = (WB[0:4], WB[4:5], WB[5:6])
C_STAGES = (WC[0:4], WC[4:6], WC[6:7])
BRANCHES = (("L3_cond_w1_nr", "L3_cond_w2_nr", None), ("L3_cond_w1_tsr", "L3_cond_w2_tsr", None),
            ("L3_cond_w1_sr", "L3_cond_w2_sr", "L3_cond_w3_sr"))
OUT_BIAS = ("L3_cond_b2_nr", "L3_cond_b2_tsr", "L3_cond_b3_sr")
HALF_TURN = float(np.nextafter(np.float32(np.pi), np.float32(0)))
TURN1 = 6.28125
TURN2 = float(np.float32(round((2 * np.pi - TURN1) * 2 ** 20) / 2 ** 20))
TURN3 = 2 * np.pi - TURN1 - TURN2
ROUNDER = 1.5 * 2 ** 23


def constants():
    c = np.zeros((P, CONST_W), np.float32)

    def put(name, a):
        c[:, CONST[name][0]:CONST[name][1]] = a

    i = np.arange(P)
    put("ident", np.eye(P))
    put("before", i[:, None] < i[None, :])
    put("ones", 1.0)
    put("slot", np.arange(A_SLOTS))
    put("slot4", np.arange(A_SLOTS) % QS)
    put("quads", [-1.0] + [QS * j for j in range(1, NQ)])
    put("class", np.arange(E))
    put("less", (np.arange(E)[None, :] < np.arange(E)[:, None]).reshape(1, -1))
    put("freq", np.exp(np.arange(P, dtype=np.float32) * np.float32(-np.log(10000.0) / (P - 1)))[:, None])
    put("head", np.stack([(i // HD) % 2 == 0, (i // HD) % 2 == 1], 1) * HD ** -0.5)
    put("sample", (i - B)[:, None])
    put("later", np.where((i % R)[:, None] > np.arange(R)[None, :], -1.0, 0.0))
    return c


def build(nc, inp, const, out):
    ctx = ExitStack()
    with ctx:
        def sb(name, shape, dt=F32):
            return ctx.enter_context(nc.sbuf_tensor(name, shape, dt))

        def sem(name):
            return ctx.enter_context(nc.semaphore(name))

        x_rows = inp["x"]
        l0_out = nc.dram_tensor("l0_out", (ROWS, S, D), F32, kind="Internal").ap()
        l2_out = nc.dram_tensor("l2_out", (B, S, D), F32, kind="Internal").ap()
        emb_dram = nc.dram_tensor("emb_dram", (B, 2 * D), F32, kind="Internal").ap()

        cst = sb("cst", [P, CONST_W])
        idx = sb("idx", [P, 2], I32)
        idxf = sb("idxf", [P, 2])
        cols_in = sb("cols_in", [COLS_W, P])
        cols = sb("cols", [P, COLS_W])
        rows = sb("rows", [P, ROWS_W, D])
        resp_bias = sb("resp_bias", [P, D])
        bq_head = sb("bq_head", [P, KC, 2])

        def k(name):
            return cst[:, CONST[name][0]:CONST[name][1]]

        def col(name, j):
            c0 = COLS[name][0] + j
            return cols[:, c0:c0 + 1]

        def row(name, rep=PAIRS):
            r0 = ROWS_OF[name][0]
            return rows[:, r0:r0 + 1, :].to_broadcast([P, rep, D])

        ident = k("ident")

        onehot = sb("onehot", [P, 2, E])
        quads = sb("quads", [P, E])
        start = sb("start", [P, E])
        end = sb("end", [P, E])
        slot_e = sb("slot_e", [P, E])
        slot_of = sb("slot_of", [P, 1])
        start_i = sb("start_i", [1, 2, E], I32)
        end_i = sb("end_i", [1, 2, E], I32)
        src_i = sb("src_i", [1, 2, A_SLOTS], I32)
        dst_i = sb("dst_i", [1, 2, A_SLOTS], I32)

        wb_hi = sb("wb_hi", [P, sum(a * b for _, a, b in WB)], F32R)
        wb_lo = sb("wb_lo", [P, sum(a * b for _, a, b in WB)], F32R)
        wc_hi = sb("wc_hi", [P, sum(a * b for _, a, b in WC)], F32R)
        wc_lo = sb("wc_lo", [P, sum(a * b for _, a, b in WC)], F32R)
        stage = sb("stage", [P, 2, STAGE])
        m_hi = sb("m_hi", [P, KC, D], F32R)
        m_lo = sb("m_lo", [P, KC, D], F32R)

        def views(parts, hi, lo):
            v, n = {}, 0
            for name, a, b in parts:
                v[name] = [t[:, n:n + a * b].rearrange("p (k n) -> p k n", k=a) for t in (hi, lo)]
                n += a * b
            return v

        w = {**views(WB, wb_hi, wb_lo), **views(WC, wc_hi, wc_lo)}
        wi = [t[:, 0:STAGE].rearrange("p (k n) -> p k n", k=KC) for t in (wc_hi, wc_lo)]
        wo = [t[:, STAGE:2 * STAGE].rearrange("p (k n) -> p k n", k=FC) for t in (wc_hi, wc_lo)]

        xin = sb("xin", [P, PAIRS, D])
        xb = sb("xb", [P, PAIRS, D])
        xh = sb("xh", [P, KC, TQ], F32R)
        xl = sb("xl", [P, KC, TQ], F32R)
        hid = sb("hid", [P, FC, TQ])
        hid_h = sb("hid_h", [P, FC, TQ], F32R)
        hid_l = sb("hid_l", [P, FC, TQ], F32R)
        res = sb("res", [P, PAIRS, D])
        stats = sb("stats", [P, PAIRS, 6])
        mv = sb("mv", [P, PAIRS, 2])
        vare = sb("vare", [P, PAIRS])
        rstd = sb("rstd", [P, PAIRS])
        minus_half = sb("minus_half", [P, PAIRS])
        half = sb("half", [P, 1])
        masked = sb("masked", [P, 1, 1])
        yout = sb("yout", [P, PAIRS, D])

        shared = sb("shared", [P, 3 * E * D])
        erows = shared[:, :].rearrange("p (w e d) -> p w e d", w=3, e=E)
        at = [0]

        def part(n):
            at[0] += n
            return shared[:, at[0] - n:at[0]]

        prob_t = part(4 * PAIRS * KC * P).rearrange("p (n r q) -> p n r q", r=4, q=P)
        qm = part(KC * 2 * TQ).rearrange("p (c h t) -> p c h t", c=KC, h=2)
        kt = part(KC * TQ).rearrange("p (c t) -> p c t", c=KC)
        vblk = part(PAIRS * 2 * D).rearrange("p (a b d) -> p a b d", a=PAIRS, b=2)
        x1b = part(PAIRS * D).rearrange("p (a d) -> p a d", a=PAIRS)
        xn = part(PAIRS * D).rearrange("p (a d) -> p a d", a=PAIRS)
        x2 = part(PAIRS * D).rearrange("p (a d) -> p a d", a=PAIRS)
        x1 = res

        ada = sb("ada", [P, PAIRS, 2 * D])
        xm = sb("xm", [P, PAIRS, D])
        mask8 = sb("mask8", [P, B // 2, S], U8)
        maskf = sb("maskf", [P, PAIRS, S])
        bias = stage[:, 0, :].rearrange("p (a n) -> p a n", a=PAIRS)
        att = stage[:, 1, :].rearrange("p (a n) -> p a n", a=PAIRS)
        amax = sb("amax", [P, PAIRS, NH])
        asum = sb("asum", [P, PAIRS, NH])
        ctx_h = sb("ctx_h", [P, KC, TQ], F32R)
        ctx_l = sb("ctx_l", [P, KC, TQ], F32R)
        ht = sb("ht", [P, KC, TQ])
        ht_h = sb("ht_h", [P, KC, TQ], F32R)
        ht_l = sb("ht_l", [P, KC, TQ], F32R)
        pooled = sb("pooled", [P, KC, QS])
        gate1 = sb("gate1", [S, TQ])
        expz = sb("expz", [P, PAIRS])
        den = sb("den", [P, PAIRS])
        strength = sb("strength", [P, PAIRS])

        hflat = hid[:, :, :].rearrange("p f t -> p (f t)")
        over = hflat[:, 0:E * NQ].rearrange("p (e q) -> p e q", e=E)
        prior = hflat[:, 256:256 + E * E].rearrange("p (e f) -> p e f", e=E)
        placed = hflat[:, 320:320 + A_SLOTS]
        srow = hflat[0:1, 512:512 + A_SLOTS]
        sempty = hflat[0:1, 704:704 + A_SLOTS]
        tstep = hflat[:, 1920:1920 + P].bitcast(I32)
        tf, tq, tr = (hflat[:, 896 + n * P:896 + (n + 1) * P] for n in range(3))
        ang = hflat[:, 1280:1408]
        turns = hflat[:, 1408:1664].rearrange("p (a n) -> p a n", a=2)
        wrap = hflat[:, 1664:1920].rearrange("p (a n) -> p a n", a=2)
        w_ada = ada
        b_ada = xm[:, :, :].rearrange("p a d -> p (a d)")
        emb = ht[:, :, :].rearrange("p a d -> p (a d)")
        uv = sb("uv", [P, KC, 2 * R])
        uvt = hflat[0:2 * R, 256:512]
        sel = sb("sel", [2 * R, 2, R])
        junk = hflat[0:2 * R, 0:D]
        qv = hflat[0:R, 512:512 + D]
        c_t = junk[0:R, :]
        basis_t = xm
        resp_in = sb("resp_in", [P, KC, R])
        resp_t = gate1[0:R, :]
        gs = sb("gs", [2 * R, 8])
        gw1_in = xb[0:S, 0, :]
        gw1_t = sb("gw1_t", [P, KC, S])
        gw2_t = sb("gw2_t", [S, 1])
        gb1 = sb("gb1", [S, 1])
        gb2 = sb("gb2", [P, 1])
        safety = sb("safety", [P, B])
        modden = sb("modden", [P, B // 2])

        ps = ctx.enter_context(nc.psum_tensor("ps", [P, 8, 512], F32))

        def bank(n, shape=None, **kw):
            return ps[:, n, :] if shape is None else ps[:, n, :].rearrange(shape, **kw)

        names = """const_in idx_in cols_in_in rows_in erows_in small_in stage_in_0 stage_in_1 stage_hi stage_lo
            uv_in mask_in setup_dve setup_act routed_onehot routed_ps routed_placed route_ready
            cols_ps gw1_ps uv_ps turned half_ready
            wrap_ready silu_ready emb_ps emb_done emb_out
            gs_sel gs_row gs_norm2 gs_dot gs_norm gs_shift gs_square gs_inverse gs_factor gs_step gs_done
            m_ps m_sb m_hi_ready m_ready safety_exp vblk_zero
            a_w_in a_w_hi a_w_lo a_x_in a_xT a_xh a_xl a_xb a_fc1 a_gelu a_hi a_split a_fc2 a_res a_stat a_var
            a_rstd a_norm a_gain a_y a_out
            b_x_in b_ada_in b_bias_in b_bias b_mask b_stat b_var b_rstd b_norm b_scaled b_xm b_xb b_xT b_xh b_xl
            b_qkv b_q b_v b_score b_added b_max b_sub b_exp b_sum b_rsum b_prob b_pT b_pTs b_pv b_ctxh b_ctxl
            b_wo b_x1 b_stat2 b_var2 b_rstd2 b_xn b_x1b b_xnT b_hth b_ht b_htl b_fc1 b_gelu b_hi b_split b_fc2
            b_x2 b_x2T b_x2h b_x2l b_pool b_gate1 b_gate1s b_gate2 b_expz b_strength b_resp b_corr b_x3 b_out
            c_x_in c_xT c_xh c_xl c_xb c_out_ps c_res c_stat c_var c_rstd c_norm c_gain c_y c_out""".split()
        sems = {}
        for n in names:
            sems[n] = sem(n)
        for c in range(len(BRANCHES)):
            for n in ("fc1", "gelu", "hi", "split"):
                sems[f"c_{n}_{c}"] = sem(f"c_{n}_{c}")
        for n in ("fc2", "gelu2", "hi2", "split2"):
            sems[f"c_{n}"] = sem(f"c_{n}")
        s = sems
        block = ctx.enter_context(nc.Block())

        def apart(eng, value):
            value = eng.to_reg(value)
            eng.wait_ge(s["const_in"], 16)
            return value

        def passes(pe, o, lhs, rhs, first, last):
            pe.matmul(o, lhs[0], rhs[0], start=first, stop=False)
            pe.matmul(o, lhs[0], rhs[1], start=False, stop=False)
            return pe.matmul(o, lhs[1], rhs[0], start=False, stop=last)

        def bounds(eng, which, e):
            tiles = A_TILES if which == 0 else C_TILES
            a = eng.value_load(start_i[0:1, which, bass.ds(e, 1)], min_val=0, max_val=tiles - 1)
            z = eng.value_load(end_i[0:1, which, bass.ds(e, 1)], min_val=1, max_val=tiles)
            return a, z

        def total(eng, which):
            last = (E if which == 0 else CLS) - 1
            return eng.value_load(end_i[0:1, which, last:last + 1], min_val=1,
                                  max_val=A_TILES if which == 0 else C_TILES)

        def stage_dmas(n):
            return 16 * sum(len(names) for names in (B_STAGES + C_STAGES)[n % 2:n + 1:2])

        @block.sync
        def _(sp):
            sp.dma_start(cst[:, :], const).then_inc(s["const_in"], 16)
            sp.dma_start(idx[:, 0:1], inp["itok_B_0_7"].rearrange("(b o) -> b o", o=1)).then_inc(s["idx_in"], 16)
            sp.dma_start(idx[:, 1:2], inp["itok_B_0_2"].rearrange("(b o) -> b o", o=1)).then_inc(s["idx_in"], 16)
            for name, (a, z) in COLS.items():
                src = inp[name]
                src = (src.rearrange("e (f p) -> (e f) p", p=P) if len(src.shape) == 2
                       else src.rearrange("(f p) -> f p", p=P))
                sp.dma_start(cols_in[a:z, :], src).then_inc(s["cols_in_in"], 16)
            for name, (a, z) in ROWS_OF.items():
                src = inp[name]
                src = src if len(src.shape) == 2 else src.rearrange("(o d) -> o d", o=1)
                sp.dma_start(rows[:, a:z, :], src.partition_broadcast(P)).then_inc(s["rows_in"], 16)
            sp.dma_start(uv[:, :, 0:R], inp["L2_cond_U"].rearrange("(c p) r -> p c r", p=P)).then_inc(s["uv_in"], 16)
            sp.dma_start(uv[:, :, R:2 * R], inp["L2_cond_V"].rearrange("(c p) r -> p c r", p=P)).then_inc(s["uv_in"], 16)
            sp.dma_start(tstep[:, :], inp["itok_B_34_63"].partition_broadcast(P)).then_inc(s["small_in"], 16)
            sp.dma_start(w_ada[:, :, :], inp["L1_cond_W_ada"].rearrange("(c p) n -> p c n", p=P)).then_inc(s["small_in"], 16)
            sp.dma_start(b_ada, inp["L1_cond_b_ada"].partition_broadcast(P)).then_inc(s["small_in"], 16)
            sp.dma_start(resp_in[:, :, :], inp["L2_cond_resp_w"].rearrange("(c p) r -> p c r", p=P)).then_inc(s["small_in"], 16)
            sp.dma_start(gw1_in, inp["L2_cond_gate_w1"]).then_inc(s["small_in"], 16)
            sp.dma_start(gw2_t[:, :], inp["L2_cond_gate_w2"].rearrange("o n -> n o")).then_inc(s["small_in"], 16)
            sp.dma_start(gb1[:, :], inp["L2_cond_gate_b1"].rearrange("(n o) -> n o", o=1)).then_inc(s["small_in"], 16)
            sp.dma_start(gb2[:, :], inp["L2_cond_gate_b2"].partition_broadcast(P)).then_inc(s["small_in"], 16)
            sp.dma_start(safety[:, :], inp["condB_safetyscore"].partition_broadcast(P)).then_inc(s["small_in"], 16)
            for n, name in enumerate(EROWS):
                sp.dma_start(erows[:, n, :, :], inp[name].partition_broadcast(P)).then_inc(s["erows_in"], 16)
            for b2 in range(2):
                sp.dma_start(mask8[b2 * S:(b2 + 1) * S, :, :],
                             inp["mask_Bx1xSxS_bk0"].rearrange("(n b) o q k -> b q (n o) k", b=2)[b2])\
                    .then_inc(s["mask_in"], 16)
            sp.wait_ge(s["emb_done"], 1)
            sp.dma_start(emb_dram, emb).then_inc(s["emb_out"], 16)

            def load_stage(n, names):
                if n >= 2:
                    sp.wait_ge(s["stage_lo"], n - 1)
                at = 0
                for name, a, b in names:
                    sp.dma_start(stage[:, n % 2, at:at + a * b].rearrange("p (k n) -> p k n", k=a),
                                 inp[name].rearrange("(k p) n -> p k n", p=P)).then_inc(s[f"stage_in_{n % 2}"], 16)
                    at += a * b
            for n, names in enumerate(B_STAGES):
                load_stage(n, names)

            sp.wait_ge(s["route_ready"], 2)
            sp.wait_ge(s["stage_lo"], len(B_STAGES))

            def a_load(g):
                for j in range(QS):
                    n = sp.value_load(src_i[0:1, 0, bass.ds(g * QS + j, 1)], min_val=0, max_val=B - 1)
                    sp.dma_start(xin[(j % 2) * S:(j % 2 + 1) * S, j // 2, :],
                                 x_rows[bass.ds(n, 1)].rearrange("a s d -> (a s) d")).then_inc(s["a_x_in"], 16)

            def a_store(g):
                sp.wait_ge(s["a_y"], g + 1)
                for j in range(QS):
                    n = sp.value_load(dst_i[0:1, 0, bass.ds(g * QS + j, 1)], min_val=0, max_val=ROWS - 1)
                    sp.dma_start(l0_out[bass.ds(n, 1)].rearrange("a s d -> (a s) d"),
                                 yout[(j % 2) * S:(j % 2 + 1) * S, j // 2, :]).then_inc(s["a_out"], 16)

            a_load(0)
            with sp.Fori(0, E) as e:
                g0, g1 = bounds(sp, 0, e)
                with sp.Fori(g0, g1) as g:
                    sp.wait_ge(s["a_xT"], g + 1)
                    sp.wait_ge(s["a_xb"], g + 1)
                    a_load(g + 1)
                    a_store(g)

            n_a = total(sp, 0)
            sp.wait_ge(s["a_out"], n_a * (16 * QS))
            sp.wait_ge(s["emb_out"], 16)

            def b_load(i):
                sp.dma_start(xin[:, :, :], l0_out[bass.ds(i * QS, QS)].rearrange("(a b) s d -> (b s) a d", b=2))\
                    .then_inc(s["b_x_in"], 16)
                for p in range(PAIRS):
                    for b2 in range(2):
                        sp.dma_start(ada[b2 * S:(b2 + 1) * S, p, :],
                                     emb_dram[bass.ds(i * QS + 2 * p + b2, 1), :].to_broadcast([S, 2 * D]))\
                            .then_inc(s["b_ada_in"], 16)

            def b_load_bias(i):
                for p in range(PAIRS):
                    for b2 in range(2):
                        sp.dma_start(bias[b2 * S:(b2 + 1) * S, p, :].rearrange("q (h k) -> q h k", h=NH),
                                     inp["fside_Bx16xSxS_0"][bass.ds(i * QS + 2 * p + b2, 1)]
                                     .rearrange("a h q k -> q (a h) k")).then_inc(s["b_bias_in"], 16)

            def b_store(i):
                sp.wait_ge(s["b_x3"], i + 1)
                sp.dma_start(l2_out[bass.ds(i * QS, QS)].rearrange("(a b) s d -> (b s) a d", b=2), yout[:, :, :])\
                    .then_inc(s["b_out"], 16)

            b_load(0)
            b_load_bias(0)

            def b_next_loads(i):
                sp.wait_ge(s["b_xm"], i + 1)
                b_load(i + 1)
                sp.wait_ge(s["b_added"], 2 * i + 2)
                b_load_bias(i + 1)

            b_next_loads(0)
            with sp.Fori(1, NQ - 1) as i:
                b_next_loads(i)
                b_store(i - 1)
            b_store(NQ - 2)
            b_store(NQ - 1)

            sp.wait_ge(s["b_out"], 16 * NQ)
            for n, names in enumerate(C_STAGES):
                load_stage(n + len(B_STAGES), names)

            def c_load(g):
                for j in range(QS):
                    n = sp.value_load(src_i[0:1, 1, bass.ds(g * QS + j, 1)], min_val=0, max_val=B - 1)
                    sp.dma_start(xin[(j % 2) * S:(j % 2 + 1) * S, j // 2, :],
                                 l2_out[bass.ds(n, 1)].rearrange("a s d -> (a s) d")).then_inc(s["c_x_in"], 16)

            def c_store(g):
                sp.wait_ge(s["c_y"], g + 1)
                for j in range(QS):
                    n = sp.value_load(dst_i[0:1, 1, bass.ds(g * QS + j, 1)], min_val=0, max_val=ROWS - 1)
                    sp.dma_start(out[bass.ds(n, 1)].rearrange("a s d -> (a s) d"),
                                 yout[(j % 2) * S:(j % 2 + 1) * S, j // 2, :]).then_inc(s["c_out"], 16)

            c_load(0)
            n_c = total(sp, 1)
            with sp.Fori(0, n_c) as g:
                sp.wait_ge(s["c_xT"], g + 1)
                sp.wait_ge(s["c_xb"], g + 1)
                c_load(g + 1)
                c_store(g)
            sp.wait_ge(s["c_x_in"], apart(sp, (n_c + 1) * (16 * QS)))
            sp.wait_ge(s["c_out"], apart(sp, n_c * (16 * QS)))

        @block.tensor
        def _(pe):
            pe.wait_ge(s["const_in"], 16)
            pe.wait_ge(s["cols_in_in"], 16 * len(COLS))
            pe.transpose(ps[:, 7, 0:COLS_W], cols_in[:, :], ident[0:COLS_W, 0:COLS_W]).then_inc(s["cols_ps"], 1)

            for which in range(2):
                pe.wait_ge(s["routed_onehot"], which + 1)
                pe.matmul(ps[:, 0, 0:E], k("before"), onehot[:, which, :], start=True, stop=True)
                pe.matmul(ps[:, 1, 0:E], k("ones"), onehot[:, which, :], start=True, stop=True)\
                    .then_inc(s["routed_ps"], 1)
                pe.wait_ge(s["routed_placed"], which + 1)
                pe.matmul(ps[0:1, 2, 0:A_SLOTS], k("sample"), placed, start=True, stop=True)\
                    .then_inc(s["routed_ps"], 1)

            pe.wait_ge(s["small_in"], 16 * 9)
            for c in range(KC):
                pe.transpose(ps[:, 3, c * S:(c + 1) * S], gw1_in[:, c * P:(c + 1) * P], ident[0:S, 0:S])
            for c in range(KC):
                last = pe.transpose(ps[0:R, 5, c * P:(c + 1) * P], resp_in[:, c, :], ident)
            last.then_inc(s["gw1_ps"], 1)
            pe.wait_ge(s["uv_in"], 32)
            for c in range(KC):
                last = pe.transpose(ps[0:2 * R, 4, c * P:(c + 1) * P], uv[:, c, :], ident)
            last.then_inc(s["uv_ps"], 1)

            pe.wait_ge(s["silu_ready"], 1)
            pe.wait_ge(s["turned"], 4)
            for c in range(KC):
                last = pe.matmul(bank(6), wrap[:, c, :], w_ada[:, c, :], start=(c == 0), stop=(c == KC - 1))
            last.then_inc(s["emb_ps"], 1)

            with pe.Fori(0, R) as i:
                pe.wait_ge(s["gs_sel"], apart(pe, i + 1))
                pe.matmul(ps[0:2 * R, 0, 0:D], sel[:, :, :], uvt[:, :], start=True, stop=True).then_inc(s["gs_row"], 1)

            pe.wait_ge(s["gs_done"], 1)
            for c in range(KC):
                last = pe.matmul(ps[:, 1, c * D:(c + 1) * D], qv[:, c * P:(c + 1) * P], uvt[0:R, :],
                                 start=True, stop=True)
            last.then_inc(s["m_ps"], 1)
            pe.wait_ge(s["m_sb"], 1)
            for c in range(KC):
                last = pe.matmul(ps[0:R, 2, 0:D], basis_t[:, c, 0:R], basis_t[:, c, :],
                                 start=(c == 0), stop=(c == KC - 1))
            last.then_inc(s["m_ps"], 1)
            pe.wait_ge(s["m_sb"], 2)
            for c in range(KC):
                last = pe.matmul(ps[:, 3, c * D:(c + 1) * D], c_t[:, c * P:(c + 1) * P], resp_t,
                                 start=True, stop=True)
            last.then_inc(s["m_ps"], 1)
            pe.wait_ge(s["m_ready"], 1)

            def turn(src, dst):
                for p in range(PAIRS):
                    for c in range(KC):
                        last = pe.transpose(dst[:, c, p * P:(p + 1) * P], src[:, p, c * P:(c + 1) * P], ident)
                return last

            def hidden(o, wt, xs, f):
                n = len(xs)
                for c in range(n):
                    last = passes(pe, o, [t[:, c, f * P:(f + 1) * P] for t in wt], xs[c], c == 0, c == n - 1)
                return last

            def tokens_out(o, xs, wt, c, n):
                for p in range(PAIRS):
                    last = passes(pe, o[:, p, :], [t[:, c, p * P:(p + 1) * P] for t in xs],
                                  [t[:, c, :] for t in wt], c == 0 and p == 0, c == n - 1 and p == PAIRS - 1)
                return last

            xs = [[xh[:, c, :], xl[:, c, :]] for c in range(KC)]
            xT = bank(0, "p (c n) -> p c n", c=KC)

            def a_turn(g):
                pe.wait_ge(s["a_x_in"], g * (16 * QS) + 16 * QS)
                turn(xin, xT).then_inc(s["a_xT"], 1)

            o_ps = bank(5, "p (a n) -> p a n", a=PAIRS)
            a_turn(0)
            with pe.Fori(0, E) as e:
                pe.wait_ge(s["a_w_lo"], 2 * e + 2)
                g0, g1 = bounds(pe, 0, e)
                with pe.Fori(g0, g1) as g:
                    pe.wait_ge(s["a_xl"], g + 1)
                    for f in range(FC):
                        last = hidden(ps[:, 1 + f // 2, (f % 2) * TQ:(f % 2 + 1) * TQ], wi, xs, f)
                        if f % 2 == 1:
                            last.then_inc(s["a_fc1"], 1)
                    a_turn(g + 1)
                    pe.wait_ge(s["a_res"], g)
                    for c in range(FC):
                        if c % 2 == 0:
                            pe.wait_ge(s["a_split"], g * (FC // 2) + c // 2 + 1)
                        last = tokens_out(o_ps, [hid_h, hid_l], wo, c, FC)
                    last.then_inc(s["a_fc2"], 1)

            scores = ps[:, 0:4, :]
            q_ps, k_ps, v_ps = bank(0, "p (c n) -> p c n", c=KC), bank(1, "p (c n) -> p c n", c=KC), \
                bank(2, "p (a n) -> p a n", a=PAIRS)
            xT7 = bank(7, "p (c n) -> p c n", c=KC)
            ctx_ps = bank(4, "p (c n) -> p c n", c=KC)
            wo_ps = bank(5, "p (a n) -> p a n", a=PAIRS)
            y_ps = bank(6, "p (a n) -> p a n", a=PAIRS)
            r_ps = bank(4, "p (a n) -> p a n", a=PAIRS)

            def b_front(i):
                pe.wait_ge(s["b_xm"], i + 1)
                turn(xm, xT7).then_inc(s["b_xT"], 1)
                pe.wait_ge(s["b_xl"], i + 1)
                for f in range(KC):
                    hidden(q_ps[:, f, :], w["L1_cond_Wq"], xs, f)
                for f in range(KC):
                    last = hidden(k_ps[:, f, :], w["L1_cond_Wk"], xs, f)
                last.then_inc(s["b_qkv"], 1)
                for c in range(KC):
                    last = tokens_out(v_ps, [xh, xl], w["L1_cond_Wv"], c, KC)
                last.then_inc(s["b_qkv"], 1)
                pe.wait_ge(s["b_q"], 2 * i + 2)
                pe.wait_ge(s["b_v"], i + 1)
                for p in range(PAIRS):
                    for c in range(KC):
                        for par in range(2):
                            for b2 in range(2):
                                t0 = p * P + b2 * S
                                for r in range(4):
                                    last = pe.matmul(
                                        scores[b2 * S:(b2 + 1) * S, r,
                                               (p * 4 + c * 2 + par) * S:(p * 4 + c * 2 + par + 1) * S],
                                        qm[r * 32:(r + 1) * 32, c, par, t0:t0 + S],
                                        kt[r * 32:(r + 1) * 32, c, t0:t0 + S], start=True, stop=True)
                last.then_inc(s["b_score"], 1)

            def b_ffn(i):
                pe.wait_ge(s["b_htl"], i + 1)
                for f in range(FC):
                    if f % 2 == 0 and f >= 4:
                        pe.wait_ge(s["b_gelu"], i * (FC // 2) + f // 2 - 1)
                    last = hidden(ps[:, 4 + f // 2 % 2, (f % 2) * TQ:(f % 2 + 1) * TQ], w["L1_cond_W1"],
                                  [[ht_h[:, c, :], ht_l[:, c, :]] for c in range(KC)], f)
                    if f % 2 == 1:
                        last.then_inc(s["b_fc1"], 1)
                for c in range(FC):
                    if c % 2 == 0:
                        pe.wait_ge(s["b_split"], i * (FC // 2) + c // 2 + 1)
                    last = tokens_out(y_ps, [hid_h, hid_l], w["L1_cond_W2"], c, FC)
                last.then_inc(s["b_fc2"], 1)

            def b_back(i):
                for p in range(PAIRS):
                    pe.wait_ge(s["b_prob"], 2 * i + p + 1)
                    for c in range(KC):
                        for r in range(4):
                            last = pe.transpose(ps[:, p * KC + c, r * P:(r + 1) * P],
                                                att[:, p, (c * 4 + r) * P:(c * 4 + r + 1) * P], ident)
                    last.then_inc(s["b_pT"], 1)
                for p in range(PAIRS):
                    pe.wait_ge(s["b_pTs"], 2 * i + p + 1)
                    for c in range(KC):
                        for b2 in range(2):
                            for r in range(4):
                                last = pe.matmul(ctx_ps[r * 32:(r + 1) * 32, c, p * P + b2 * S:p * P + (b2 + 1) * S],
                                                 vblk[:, p, b2, c * P + r * 32:c * P + (r + 1) * 32],
                                                 prob_t[:, p * KC + c, r, b2 * S:(b2 + 1) * S],
                                                 start=True, stop=True)
                last.then_inc(s["b_pv"], 1)
                pe.wait_ge(s["b_ctxl"], i + 1)
                for c in range(KC):
                    last = tokens_out(wo_ps, [ctx_h, ctx_l], w["L1_cond_Wo"], c, KC)
                last.then_inc(s["b_wo"], 1)

            def b_turn_ffn(i):
                pe.wait_ge(s["b_xn"], i + 1)
                turn(xn, xT7).then_inc(s["b_xnT"], 1)

            def b_last(i):
                pe.wait_ge(s["b_x2"], i + 1)
                turn(x2, xT7).then_inc(s["b_x2T"], 1)
                pe.wait_ge(s["b_x2l"], i + 1)
                for c in range(KC):
                    last = tokens_out(r_ps, [xh, xl], [m_hi, m_lo], c, KC)
                last.then_inc(s["b_resp"], 1)
                pe.wait_ge(s["b_pool"], i + 1)
                for c in range(KC):
                    last = pe.matmul(ps[0:S, 7, 0:QS], gw1_t[:, c, :], pooled[:, c, :],
                                     start=(c == 0), stop=(c == KC - 1))
                last.then_inc(s["b_gate1"], 1)
                pe.wait_ge(s["b_gate1s"], i + 1)
                for p in range(PAIRS):
                    last = pe.matmul(ps[:, 5, p:p + 1], gate1[:, p * P:(p + 1) * P], gw2_t[:, :],
                                     start=True, stop=True)
                last.then_inc(s["b_gate2"], 1)

            n_a = total(pe, 0)
            pe.wait_ge(s["a_out"], apart(pe, n_a * (16 * QS)))
            pe.wait_ge(s["vblk_zero"], 1)
            with pe.Fori(0, NQ) as i:
                b_front(i)
                b_back(i)
                b_turn_ffn(i)
                b_ffn(i)
                b_last(i)
                pe.wait_ge(s["b_x3"], i + 1)

            pe.wait_ge(s["stage_lo"], len(B_STAGES) + len(C_STAGES))

            def c_turn(g):
                pe.wait_ge(s["c_x_in"], g * (16 * QS) + 16 * QS)
                turn(xin, xT).then_inc(s["c_xT"], 1)

            c_turn(0)
            for c, (w1, w2, w3) in enumerate(BRANCHES):
                g0, g1 = bounds(pe, 1, c)
                n1 = w[w1][0].shape[2] // P
                with pe.Fori(0, pe.snap(g1 - g0)) as t:
                    g = g0 + t
                    pe.wait_ge(s["c_xl"], g + 1)
                    for f in range(n1):
                        last = hidden(ps[:, 1 + f // 2, (f % 2) * TQ:(f % 2 + 1) * TQ], w[w1], xs, f)
                        if f % 2 == 1:
                            last.then_inc(s[f"c_fc1_{c}"], 1)
                    c_turn(g + 1)
                    src = [hid_h, hid_l]
                    if w3:
                        for f in range(KC):
                            for kc in range(n1):
                                if f == 0 and kc % 2 == 0:
                                    pe.wait_ge(s[f"c_split_{c}"], t * (n1 // 2) + kc // 2 + 1)
                                last = passes(pe, ps[:, 4, f * TQ:(f + 1) * TQ],
                                              [u[:, kc, f * P:(f + 1) * P] for u in w[w2]],
                                              [hid_h[:, kc, :], hid_l[:, kc, :]], kc == 0, kc == n1 - 1)
                        last.then_inc(s["c_fc2"], 1)
                        src = [hid_h[:, 4:6, :], hid_l[:, 4:6, :]]
                        pe.wait_ge(s["c_split2"], t + 1)
                    else:
                        pe.wait_ge(s[f"c_split_{c}"], t * (n1 // 2) + 1)
                    pe.wait_ge(s["c_res"], g)
                    for kc in range(KC):
                        last = tokens_out(o_ps, src, w[w3 or w2], kc, KC)
                    last.then_inc(s["c_out_ps"], 1)
            g0, g1 = bounds(pe, 1, CLS - 1)
            with pe.Fori(g0, g1) as g:
                pe.wait_ge(s["c_xl"], g + 1)
                c_turn(g + 1)

        @block.scalar
        def _(act):
            act.wait_ge(s["wrap_ready"], 1)
            act.activation(wrap, wrap, ACT.Sin).then_inc(s["setup_act"], 1)
            act.wait_ge(s["setup_act"], 1)
            act.activation(wrap, wrap, ACT.Silu).then_inc(s["silu_ready"], 1)
            act.wait_ge(s["small_in"], 16 * 9)
            act.activation(safety[:, :], safety[:, :], ACT.Exp, scale=-1.0).then_inc(s["safety_exp"], 1)
            with act.Fori(0, R) as i:
                act.wait_ge(s["gs_row"], i + 1)
                act.activation(ps[0:2 * R, 1, 0:D], ps[0:2 * R, 0, 0:D], ACT.Square, accum_out=gs[:, 0:1])\
                    .then_inc(s["gs_norm2"], 1)
            act.wait_ge(s["m_ps"], 3)
            act.activation(m_hi[:, :, :], bank(3, "p (c n) -> p c n", c=KC), ACT.Copy).then_inc(s["m_hi_ready"], 1)

            def split_stage(n, names, hi_v):
                act.wait_ge(s[f"stage_in_{n % 2}"], stage_dmas(n))
                width = sum(a * b for _, a, b in names)
                act.activation(hi_v, stage[:, n % 2, 0:width], ACT.Copy).then_inc(s["stage_hi"], 1)

            for n, names in enumerate(B_STAGES):
                split_stage(n, names, wb_hi[:, n * STAGE:(n + 1) * STAGE])

            def a_xhi(g):
                act.wait_ge(s["a_xT"], g + 1)
                act.activation(xh[:, :, :], bank(0, "p (c n) -> p c n", c=KC), ACT.Copy).then_inc(s["a_xh"], 1)

            a_xhi(0)
            with act.Fori(0, E) as e:
                g0, g1 = bounds(act, 0, e)
                act.wait_ge(s["a_w_in"], e * 32 + 32)
                act.wait_ge(s["a_fc1"], g0 * (FC // 2))
                act.activation(wc_hi[:, 0:STAGE], stage[:, 0, :], ACT.Copy).then_inc(s["a_w_hi"], 1)
                act.wait_ge(s["a_fc2"], g0)
                act.activation(wc_hi[:, STAGE:2 * STAGE], stage[:, 1, :], ACT.Copy).then_inc(s["a_w_hi"], 1)
                with act.Fori(g0, g1) as g:
                    for f in range(FC):
                        if f % 2 == 0:
                            act.wait_ge(s["a_fc1"], g * (FC // 2) + f // 2 + 1)
                        last = act.activation(hid[:, f, :], ps[:, 1 + f // 2, (f % 2) * TQ:(f % 2 + 1) * TQ], ACT.Gelu,
                                              bias=cols[:, bass.ds(e * FC + f, 1)])
                        if f % 2 == 1:
                            last.then_inc(s["a_gelu"], 1)
                    a_xhi(g + 1)

            n_a = total(act, 0)
            act.wait_ge(s["a_out"], n_a * (16 * QS))

            def b_act_front(i):
                act.wait_ge(s["b_xT"], i + 1)
                act.activation(xh[:, :, :], bank(7, "p (c n) -> p c n", c=KC), ACT.Copy).then_inc(s["b_xh"], 1)
                act.wait_ge(s["b_qkv"], 2 * i + 1)
                for c in range(KC):
                    for par in range(2):
                        last = act.activation(qm[:, c, par, :], ps[:, 0, c * TQ:(c + 1) * TQ], ACT.Identity,
                                              scale=k("head")[:, par:par + 1], bias=bq_head[:, c, par:par + 1])
                last.then_inc(s["b_q"], 1)
                for c in range(KC):
                    last = act.activation(kt[:, c, :], ps[:, 1, c * TQ:(c + 1) * TQ], ACT.Identity,
                                          bias=col("L1_cond_bk", c))
                last.then_inc(s["b_q"], 1)

            def b_act_exp(i):
                for p in range(PAIRS):
                    act.wait_ge(s["b_sub"], 2 * i + p + 1)
                    act.activation(att[:, p, :], att[:, p, :], ACT.Exp).then_inc(s["b_exp"], 1)

            def b_act_back(i):
                for p in range(PAIRS):
                    act.wait_ge(s["b_pT"], 2 * i + p + 1)
                    act.activation(prob_t[:, p * KC:(p + 1) * KC, :, :],
                                   ps[:, p * KC:(p + 1) * KC, :].rearrange("q c (r n) -> q c r n", r=4),
                                   ACT.Copy).then_inc(s["b_pTs"], 1)
                act.wait_ge(s["b_pv"], i + 1)
                act.activation(ctx_h[:, :, :], bank(4, "p (c n) -> p c n", c=KC), ACT.Copy)\
                    .then_inc(s["b_ctxh"], 1)

            def b_act_ht(i):
                act.wait_ge(s["b_xnT"], i + 1)
                for c in range(KC):
                    last = act.activation(ht_h[:, c, :], ps[:, 7, c * TQ:(c + 1) * TQ], ACT.Identity,
                                          scale=col("L1_cond_g2", c), bias=col("L1_cond_beta2", c))
                last.then_inc(s["b_hth"], 1)

            def b_act_ffn(i):
                for f in range(FC):
                    if f % 2 == 0:
                        act.wait_ge(s["b_fc1"], i * (FC // 2) + f // 2 + 1)
                    last = act.activation(hid[:, f, :], ps[:, 4 + f // 2 % 2, (f % 2) * TQ:(f % 2 + 1) * TQ],
                                          ACT.Gelu_apprx_sigmoid, bias=col("L1_cond_b1", f))
                    if f % 2 == 1:
                        last.then_inc(s["b_gelu"], 1)

            def b_act_last(i):
                act.wait_ge(s["b_x2T"], i + 1)
                act.activation(xh[:, :, :], bank(7, "p (c n) -> p c n", c=KC), ACT.Copy).then_inc(s["b_x2h"], 1)
                act.wait_ge(s["b_gate1"], i + 1)
                act.activation(gate1[:, :].rearrange("n (b s) -> n b s", b=QS),
                               ps[0:S, 7, 0:QS].rearrange("n (b o) -> n b o", o=1).to_broadcast([S, QS, S]),
                               ACT.Relu, scale=1.0 / S, bias=gb1[:, 0:1]).then_inc(s["b_gate1s"], 1)
                act.wait_ge(s["b_gate2"], i + 1)
                act.activation(expz[:, :], ps[:, 5, 0:PAIRS], ACT.Exp, scale=-1.0, bias=gb2[:, 0:1])\
                    .then_inc(s["b_expz"], 1)

            with act.Fori(0, NQ) as i:
                b_act_front(i)
                b_act_exp(i)
                b_act_back(i)
                b_act_ht(i)
                b_act_ffn(i)
                b_act_last(i)

            at = 0
            for n, names in enumerate(C_STAGES):
                width = sum(a * b for _, a, b in names)
                split_stage(n + len(B_STAGES), names, wc_hi[:, at:at + width])
                at += width

            def c_xhi(g):
                act.wait_ge(s["c_xT"], g + 1)
                act.activation(xh[:, :, :], bank(0, "p (c n) -> p c n", c=KC), ACT.Copy).then_inc(s["c_xh"], 1)

            c_xhi(0)
            for c, (w1, w2, w3) in enumerate(BRANCHES):
                g0, g1 = bounds(act, 1, c)
                n1 = w[w1][0].shape[2] // P
                b1 = w1.replace("w1", "b1")
                with act.Fori(0, act.snap(g1 - g0)) as t:
                    for f in range(n1):
                        if f % 2 == 0:
                            act.wait_ge(s[f"c_fc1_{c}"], t * (n1 // 2) + f // 2 + 1)
                        last = act.activation(hid[:, f, :], ps[:, 1 + f // 2, (f % 2) * TQ:(f % 2 + 1) * TQ], ACT.Gelu,
                                              bias=col(b1, f))
                        if f % 2 == 1:
                            last.then_inc(s[f"c_gelu_{c}"], 1)
                    c_xhi(g0 + t + 1)
                    if w3:
                        act.wait_ge(s["c_fc2"], t + 1)
                        for f in range(KC):
                            last = act.activation(hid[:, 4 + f, :], ps[:, 4, f * TQ:(f + 1) * TQ], ACT.Gelu,
                                                  bias=col("L3_cond_b2_sr", f))
                        last.then_inc(s["c_gelu2"], 1)
            g0, g1 = bounds(act, 1, CLS - 1)
            with act.Fori(g0, g1) as g:
                c_xhi(g + 1)

        @block.vector
        def _(dve):
            done = [0]

            def then(ins):
                done[0] += 1
                ins.then_inc(s["setup_dve"], 1)
                dve.wait_ge(s["setup_dve"], done[0])

            dve.wait_ge(s["const_in"], 16)
            dve.wait_ge(s["idx_in"], 32)
            then(dve.tensor_copy(idxf[:, :], idx[:, :]))
            then(dve.tensor_scalar(idxf[:, 0:1], idxf[:, 0:1], 0.0, float(E - 1), ALU.max, ALU.min))
            for which in range(2):
                hot = onehot[:, which, :]
                then(dve.tensor_scalar(hot, k("class"), idxf[:, which:which + 1], None, ALU.is_equal))
                if which == 1:
                    then(dve.tensor_reduce(slot_of[:, :], hot[:, 0:CLS - 1], X, ALU.add))
                    then(dve.tensor_scalar(hot[:, CLS - 1:CLS], slot_of[:, :], -1.0, 1.0, ALU.mult, ALU.add))
                    then(dve.memset(hot[:, CLS:E], 0.0))
                dve.sem_inc(s["routed_onehot"], 1)
                dve.wait_ge(s["routed_ps"], 2 * which + 1)
                then(dve.tensor_tensor(over, ps[:, 1, 0:E].rearrange("p (e o) -> p e o", o=1).to_broadcast([P, E, NQ]),
                                       k("quads").rearrange("p (o q) -> p o q", o=1).to_broadcast([P, E, NQ]),
                                       ALU.is_gt))
                then(dve.tensor_reduce(quads[:, :], over, X, ALU.add))
                then(dve.tensor_tensor(prior, k("less").rearrange("p (e f) -> p e f", e=E),
                                       quads[:, :].rearrange("p (o f) -> p o f", o=1).to_broadcast([P, E, E]),
                                       ALU.mult))
                then(dve.tensor_reduce(start[:, :], prior, X, ALU.add))
                then(dve.tensor_tensor(end[:, :], start[:, :], quads[:, :], ALU.add))
                then(dve.scalar_tensor_tensor(slot_e[:, :], start[:, :], float(QS), ps[:, 0, 0:E], ALU.mult, ALU.add))
                then(dve.tensor_tensor(slot_e[:, :], slot_e[:, :], hot, ALU.mult))
                then(dve.tensor_reduce(slot_of[:, :], slot_e[:, :], X, ALU.add))
                dve.tensor_scalar(placed, k("slot"), slot_of[:, 0:1], None, ALU.is_equal)\
                    .then_inc(s["routed_placed"], 1)
                dve.tensor_copy(start_i[:, which, :], start[0:1, :])
                dve.tensor_copy(end_i[:, which, :], end[0:1, :])
                dve.wait_ge(s["routed_ps"], 2 * which + 2)
                then(dve.tensor_copy(srow, ps[0:1, 2, 0:A_SLOTS]))
                then(dve.tensor_scalar(sempty, srow, -0.5, None, ALU.is_gt))
                then(dve.tensor_tensor(sempty, sempty, k("slot4")[0:1, :], ALU.mult))
                dve.tensor_scalar(src_i[:, which, :], srow, float(B), float(B - 1), ALU.add, ALU.min)
                dve.scalar_tensor_tensor(dst_i[:, which, :], srow, float(B), sempty, ALU.add, ALU.add)\
                    .then_inc(s["route_ready"], 1)

            dve.wait_ge(s["cols_ps"], 1)
            then(dve.tensor_copy(cols[:, :], ps[:, 7, 0:COLS_W]))
            dve.wait_ge(s["gw1_ps"], 1)
            dve.tensor_copy(gw1_t[:, :, :], ps[:, 3, 0:KC * S].rearrange("p (c n) -> p c n", c=KC))\
                .then_inc(s["turned"], 1)
            dve.tensor_copy(resp_t, ps[0:R, 5, 0:D]).then_inc(s["turned"], 1)
            dve.wait_ge(s["uv_ps"], 1)
            dve.tensor_copy(uvt[:, :], ps[0:2 * R, 4, 0:D]).then_inc(s["turned"], 1)
            for c in range(KC):
                last = dve.tensor_scalar(bq_head[:, c, :], k("head"), col("L1_cond_bq", c), None, ALU.mult)
            last.then_inc(s["turned"], 1)
            dve.wait_ge(s["rows_in"], 16 * len(ROWS_OF))
            dve.tensor_tensor(resp_bias[:, :], row("L2_cond_resp_b", 1)[:, 0, :], row("L2_cond_safety_bias", 1)[:, 0, :],
                              ALU.add)
            dve.tensor_scalar(gb2[:, :], gb2[:, :], -1.0, None, ALU.mult)
            dve.wait_ge(s["small_in"], 16 * 9)
            then(dve.tensor_copy(tf, tstep[:, :]))
            then(dve.tensor_scalar(tq, tf, 0.01, None, ALU.mult))
            then(dve.scalar_tensor_tensor(tr, tq, -64.0, tf, ALU.mult, ALU.add))
            then(dve.scalar_tensor_tensor(tr, tq, -32.0, tr, ALU.mult, ALU.add))
            then(dve.scalar_tensor_tensor(tr, tq, -4.0, tr, ALU.mult, ALU.add))
            then(dve.scalar_tensor_tensor(tq, tr, 0.01, tq, ALU.mult, ALU.add))
            then(dve.tensor_scalar(tq, tq, 4000.0, None, ALU.mult))
            then(dve.tensor_scalar(ang, tq, k("freq"), None, ALU.mult))
            for half_n, shift in enumerate((0.0, 0.25)):
                n, v = turns[:, half_n, :], wrap[:, half_n, :]
                then(dve.tensor_scalar(n, ang, 0.5 / np.pi, shift, ALU.mult, ALU.add))
                then(dve.tensor_scalar(n, n, ROUNDER, None, ALU.add))
                then(dve.tensor_scalar(n, n, -ROUNDER, None, ALU.add))
                then(dve.scalar_tensor_tensor(v, n, -TURN1, ang, ALU.mult, ALU.add))
                then(dve.scalar_tensor_tensor(v, n, -TURN2, v, ALU.mult, ALU.add))
                then(dve.scalar_tensor_tensor(v, n, -TURN3, v, ALU.mult, ALU.add))
                then(dve.tensor_scalar(v, v, 2 * np.pi * shift, None, ALU.add))
                then(dve.tensor_scalar(v, v, HALF_TURN, -HALF_TURN, ALU.min, ALU.max))
            dve.sem_inc(s["wrap_ready"], 1)
            dve.wait_ge(s["emb_ps"], 1)
            then(dve.tensor_tensor(emb, bank(6), b_ada, ALU.add))
            dve.tensor_scalar(emb[:, 0:D], emb[:, 0:D], 1.0, None, ALU.add).then_inc(s["emb_done"], 1)

            dve.wait_ge(s["safety_exp"], 1)
            for b2 in range(2):
                then(dve.tensor_scalar(modden[b2 * S:(b2 + 1) * S, :],
                                       safety[b2 * S:(b2 + 1) * S, :].rearrange("p (n b) -> p n b", b=2)[:, :, b2],
                                       1.0, None, ALU.add))

            with dve.Fori(0, R) as i:
                dve.tensor_copy(sel[:, :, :], ident[0:2 * R, 0:2 * R].rearrange("p (a j) -> p a j", a=2)
                                [:, :, bass.ds(i, 1)].to_broadcast([2 * R, 2, R])).then_inc(s["gs_sel"], 1)
                dve.wait_ge(s["gs_norm2"], i + 1)
                dve.tensor_tensor_reduce(junk[:, :], ps[0:2 * R, 0, 0:D], uvt[:, :], 1.0, 0.0, ALU.mult, ALU.add,
                                         gs[:, 1:2]).then_inc(s["gs_dot"], 1)
                dve.wait_ge(s["gs_norm"], i + 1)
                dve.tensor_scalar(gs[:, 3:4], gs[:, 2:3], 1e-8, None, ALU.add).then_inc(s["gs_shift"], 1)
                dve.wait_ge(s["gs_shift"], i + 1)
                dve.tensor_tensor(gs[:, 4:5], gs[:, 3:4], gs[:, 3:4], ALU.mult).then_inc(s["gs_square"], 1)
                dve.wait_ge(s["gs_square"], i + 1)
                dve.reciprocal(gs[:, 5:6], gs[:, 4:5]).then_inc(s["gs_inverse"], 1)
                dve.wait_ge(s["gs_inverse"], i + 1)
                dve.wait_ge(s["gs_dot"], i + 1)
                dve.scalar_tensor_tensor(gs[:, 6:7], gs[:, 1:2], gs[:, 5:6], k("later")[0:2 * R, bass.ds(i, 1)],
                                         ALU.mult, ALU.mult).then_inc(s["gs_factor"], 1)
                dve.wait_ge(s["gs_factor"], i + 1)
                dve.scalar_tensor_tensor(uvt[:, :], ps[0:2 * R, 0, 0:D], gs[:, 6:7], uvt[:, :], ALU.mult, ALU.add)\
                    .then_inc(s["gs_step"], 1)
                dve.wait_ge(s["gs_step"], i + 1)
            then(dve.tensor_tensor_reduce(junk[:, :], uvt[:, :], uvt[:, :], 1.0, 0.0, ALU.mult, ALU.add, gs[:, 0:1]))
            dve.sem_inc(s["gs_dot"], 1)
            dve.wait_ge(s["gs_norm"], R + 1)
            then(dve.tensor_scalar(gs[:, 3:4], gs[:, 2:3], 1e-8, None, ALU.add))
            then(dve.reciprocal(gs[:, 4:5], gs[:, 3:4]))
            then(dve.tensor_scalar(uvt[:, :], uvt[:, :], gs[:, 4:5], None, ALU.mult))
            dve.tensor_copy(qv[:, :], uvt[R:2 * R, :]).then_inc(s["gs_done"], 1)

            dve.wait_ge(s["m_ps"], 1)
            dve.tensor_copy(basis_t[:, :, :], ps[:, 1, :].rearrange("p (c n) -> p c n", c=KC)).then_inc(s["m_sb"], 1)
            dve.wait_ge(s["m_ps"], 2)
            dve.tensor_copy(c_t, ps[0:R, 2, 0:D]).then_inc(s["m_sb"], 1)
            dve.wait_ge(s["m_hi_ready"], 1)
            dve.tensor_tensor(m_lo[:, :, :], ps[:, 3, :].rearrange("p (c n) -> p c n", c=KC),
                              m_hi[:, :, :].bitcast(F32), ALU.subtract).then_inc(s["m_ready"], 1)

            def split_lo(n, names, lo_v, hi_v):
                dve.wait_ge(s["stage_hi"], n + 1)
                width = sum(a * b for _, a, b in names)
                dve.tensor_tensor(lo_v, stage[:, n % 2, 0:width], hi_v.bitcast(F32), ALU.subtract)\
                    .then_inc(s["stage_lo"], 1)

            for n, names in enumerate(B_STAGES):
                split_lo(n, names, wb_lo[:, n * STAGE:(n + 1) * STAGE], wb_hi[:, n * STAGE:(n + 1) * STAGE])

            def low(out_t, whole, high):
                return dve.tensor_tensor(out_t, whole, high.bitcast(F32), ALU.subtract)

            def split_hidden(j, sem_hi, n_hi, sem_split, at=None):
                f = slice(2 * j, 2 * j + 2) if at is None else slice(at, at + 2)
                dve.tensor_copy(hid_h[:, f, :], hid[:, f, :]).then_inc(sem_hi, 1)
                dve.wait_ge(sem_hi, n_hi)
                low(hid_l[:, f, :], hid[:, f, :], hid_h[:, f, :]).then_inc(sem_split, 1)

            def layer_stats(src, sem_stat, n_stat, sem_var, eps):
                for p in range(PAIRS):
                    last = dve.bn_stats(stats[:, p, :], src[:, p, :])
                last.then_inc(sem_stat, 1)
                dve.wait_ge(sem_stat, apart(dve, n_stat - 1))
                for p in range(PAIRS):
                    last = dve.bn_aggr(mv[:, p, :], stats[:, p, :])
                last.then_inc(sem_stat, 1)
                dve.wait_ge(sem_stat, n_stat)
                dve.tensor_scalar(vare[:, :], mv[:, :, 1], eps, None, ALU.add).then_inc(sem_var, 1)

            xT_ps = bank(0, "p (c n) -> p c n", c=KC)
            o_ps = bank(5, "p (a n) -> p a n", a=PAIRS)

            def a_xlo(g):
                dve.wait_ge(s["a_xh"], g + 1)
                low(xl[:, :, :], xT_ps, xh[:, :, :]).then_inc(s["a_xl"], 1)

            a_xlo(0)
            with dve.Fori(0, E) as e:
                g0, g1 = bounds(dve, 0, e)
                for n in range(2):
                    dve.wait_ge(s["a_w_hi"], 2 * e + n + 1)
                    v = slice(n * STAGE, (n + 1) * STAGE)
                    low(wc_lo[:, v], stage[:, n, :], wc_hi[:, v]).then_inc(s["a_w_lo"], 1)
                with dve.Fori(g0, g1) as g:
                    for j in range(FC // 2):
                        dve.wait_ge(s["a_gelu"], g * (FC // 2) + j + 1)
                        split_hidden(j, s["a_hi"], g * (FC // 2) + j + 1, s["a_split"])
                    a_xlo(g + 1)
                    dve.wait_ge(s["a_fc2"], g + 1)
                    dve.wait_ge(s["a_xb"], g + 1)
                    dve.wait_ge(s["a_norm"], g)
                    dve.tensor_tensor(res[:, :, :], o_ps, xb[:, :, :], ALU.add).then_inc(s["a_res"], 1)
                    dve.wait_ge(s["a_res"], g + 1)
                    layer_stats(res, s["a_stat"], 2 * g + 2, s["a_var"], 1e-12)

            n_a = total(dve, 0)
            dve.wait_ge(s["a_out"], n_a * (16 * QS))
            dve.memset(vblk, 0.0).then_inc(s["vblk_zero"], 1)
            dve.wait_ge(s["vblk_zero"], 1)
            xT7 = bank(7, "p (c n) -> p c n", c=KC)
            heads = lambda t, n: t.rearrange("q a (h d) -> q a h d", h=n)

            def normalise(dst, src):
                for p in range(PAIRS):
                    last = dve.tensor_scalar(dst[:, p, :], src[:, p, :], mv[:, p, 0:1], rstd[:, p:p + 1],
                                             ALU.subtract, ALU.mult)
                return last

            def b_ln1(i):
                dve.wait_ge(s["b_x_in"], 16 * i + 16)
                layer_stats(xin, s["b_stat"], 2 * i + 2, s["b_var"], 1e-5)
                dve.wait_ge(s["b_rstd"], i + 1)
                normalise(xm, xin).then_inc(s["b_norm"], 1)

            def b_values(i):
                dve.wait_ge(s["b_xh"], i + 1)
                low(xl[:, :, :], xT7, xh[:, :, :]).then_inc(s["b_xl"], 1)
                dve.wait_ge(s["b_qkv"], 2 * i + 2)
                bv = row("L1_cond_bv").rearrange("q a (g h d) -> q a g h d", g=NH // 2, h=2)
                vp = bank(2, "q (a g h d) -> q a g h d", a=PAIRS, g=NH // 2, h=2)
                vb = vblk.rearrange("q a b (g h d) -> q a b g h d", g=NH // 2, h=2)
                for b2 in range(2):
                    for par in range(2):
                        here, to = slice(b2 * S, (b2 + 1) * S), slice(par * S, (par + 1) * S)
                        last = dve.tensor_tensor(vb[to, :, b2, :, par, :], vp[here, :, :, par, :],
                                                 bv[here, :, :, par, :], ALU.add)
                last.then_inc(s["b_v"], 1)

            def b_softmax_in(i):
                dve.wait_ge(s["b_score"], i + 1)
                for p in range(PAIRS):
                    dve.wait_ge(s["b_bias"], 2 * i + p + 1)
                    v = lambda t: t[:, p, :].rearrange("q (c r n) -> q r c n", c=KC, r=4)
                    dve.tensor_tensor(v(att), ps[:, 0:4, p * TQ:(p + 1) * TQ].rearrange("q r (c n) -> q r c n", c=KC),
                                      v(bias), ALU.add).then_inc(s["b_added"], 1)
                    dve.wait_ge(s["b_added"], 2 * i + p + 1)
                    dve.tensor_reduce(amax[:, p, :], att[:, p, :].rearrange("q (h k) -> q h k", h=NH), X, ALU.max)\
                        .then_inc(s["b_max"], 1)
                for p in range(PAIRS):
                    dve.wait_ge(s["b_max"], 2 * i + p + 1)
                    v = att[:, p, :].rearrange("q (h k) -> q h k", h=NH)
                    dve.tensor_tensor(v, v, amax[:, p, :].rearrange("q (h o) -> q h o", o=1).to_broadcast([P, NH, S]),
                                      ALU.subtract).then_inc(s["b_sub"], 1)

            def b_softmax_sum(i):
                for p in range(PAIRS):
                    dve.wait_ge(s["b_exp"], 2 * i + p + 1)
                    dve.tensor_reduce(asum[:, p, :], att[:, p, :].rearrange("q (h k) -> q h k", h=NH), X, ALU.add)\
                        .then_inc(s["b_sum"], 1)
                    dve.wait_ge(s["b_sum"], 2 * i + p + 1)
                    dve.reciprocal(asum[:, p, :], asum[:, p, :]).then_inc(s["b_rsum"], 1)

            def b_ctx(i):
                dve.wait_ge(s["b_ctxh"], i + 1)
                low(ctx_l[:, :, :], bank(4, "p (c n) -> p c n", c=KC), ctx_h[:, :, :]).then_inc(s["b_ctxl"], 1)

            def b_ln2(i):
                dve.wait_ge(s["b_wo"], i + 1)
                dve.wait_ge(s["b_xb"], i + 1)
                dve.tensor_tensor(x1[:, :, :], bank(5, "p (a n) -> p a n", a=PAIRS), xb[:, :, :], ALU.add)\
                    .then_inc(s["b_x1"], 1)
                dve.wait_ge(s["b_x1"], i + 1)
                layer_stats(x1, s["b_stat2"], 2 * i + 2, s["b_var2"], 1e-5)
                dve.wait_ge(s["b_rstd2"], i + 1)
                normalise(xn, x1).then_inc(s["b_xn"], 1)

            def b_ffn_in(i):
                dve.wait_ge(s["b_hth"], i + 1)
                for c in range(KC):
                    last = dve.tensor_scalar(ht[:, c, :], xT7[:, c, :], col("L1_cond_g2", c), col("L1_cond_beta2", c),
                                             ALU.mult, ALU.add)
                last.then_inc(s["b_ht"], 1)
                dve.wait_ge(s["b_ht"], i + 1)
                low(ht_l[:, :, :], ht[:, :, :], ht_h[:, :, :]).then_inc(s["b_htl"], 1)

            def b_ffn(i):
                for j in range(FC // 2):
                    dve.wait_ge(s["b_gelu"], i * (FC // 2) + j + 1)
                    split_hidden(j, s["b_hi"], i * (FC // 2) + j + 1, s["b_split"])

            def b_l2_in(i):
                dve.wait_ge(s["b_fc2"], i + 1)
                dve.wait_ge(s["b_x1b"], i + 1)
                dve.tensor_tensor(x2, bank(6, "p (a n) -> p a n", a=PAIRS), x1b, ALU.add).then_inc(s["b_x2"], 1)
                dve.wait_ge(s["b_x2h"], i + 1)
                low(xl[:, :, :], xT7, xh[:, :, :]).then_inc(s["b_x2l"], 1)
                dve.tensor_reduce(pooled[:, :, :], xT7.rearrange("p c (b s) -> p c b s", b=QS), X, ALU.add)\
                    .then_inc(s["b_pool"], 1)

            def b_l2_out(i):
                dve.wait_ge(s["b_resp"], i + 1)
                dve.wait_ge(s["b_out"], 16 * i)
                dve.tensor_tensor(yout[:, :, :], bank(4, "p (a n) -> p a n", a=PAIRS),
                                  resp_bias[:, :].rearrange("p (o d) -> p o d", o=1).to_broadcast([P, PAIRS, D]),
                                  ALU.add).then_inc(s["b_corr"], 1)
                dve.wait_ge(s["b_expz"], i + 1)
                dve.scalar_tensor_tensor(den[:, :], expz[:, :], 1.0, modden[:, bass.ds(i * PAIRS, PAIRS)],
                                         ALU.add, ALU.mult).then_inc(s["b_strength"], 1)
                dve.wait_ge(s["b_strength"], 2 * i + 1)
                dve.reciprocal(strength[:, :], den[:, :]).then_inc(s["b_strength"], 1)
                dve.wait_ge(s["b_strength"], 2 * i + 2)
                dve.wait_ge(s["b_corr"], i + 1)
                for p in range(PAIRS):
                    last = dve.scalar_tensor_tensor(yout[:, p, :], yout[:, p, :], strength[:, p:p + 1], x2[:, p, :],
                                                    ALU.mult, ALU.add)
                last.then_inc(s["b_x3"], 1)

            with dve.Fori(0, NQ) as i:
                b_ln1(i)
                b_values(i)
                b_softmax_in(i)
                b_softmax_sum(i)
                b_ctx(i)
                b_ln2(i)
                b_ffn_in(i)
                b_ffn(i)
                b_l2_in(i)
                b_l2_out(i)

            at = 0
            for n, names in enumerate(C_STAGES):
                width = sum(a * b for _, a, b in names)
                split_lo(n + len(B_STAGES), names, wc_lo[:, at:at + width], wc_hi[:, at:at + width])
                at += width

            def c_xlo(g):
                dve.wait_ge(s["c_xh"], g + 1)
                low(xl[:, :, :], xT_ps, xh[:, :, :]).then_inc(s["c_xl"], 1)

            def c_finish(g, with_ps):
                dve.wait_ge(s["c_xb"], g + 1)
                dve.wait_ge(s["c_norm"], g)
                if with_ps:
                    dve.wait_ge(s["c_out_ps"], g + 1)
                    dve.tensor_tensor(res[:, :, :], o_ps, xb[:, :, :], ALU.add).then_inc(s["c_res"], 1)
                else:
                    dve.tensor_copy(res[:, :, :], xb[:, :, :]).then_inc(s["c_res"], 1)
                dve.wait_ge(s["c_res"], g + 1)
                layer_stats(res, s["c_stat"], 2 * g + 2, s["c_var"], 1e-5)

            c_xlo(0)
            for c, (w1, w2, w3) in enumerate(BRANCHES):
                g0, g1 = bounds(dve, 1, c)
                n1 = w[w1][0].shape[2] // P
                with dve.Fori(0, dve.snap(g1 - g0)) as t:
                    g = g0 + t
                    for j in range(n1 // 2):
                        dve.wait_ge(s[f"c_gelu_{c}"], t * (n1 // 2) + j + 1)
                        split_hidden(j, s[f"c_hi_{c}"], t * (n1 // 2) + j + 1, s[f"c_split_{c}"])
                    c_xlo(g + 1)
                    if w3:
                        dve.wait_ge(s["c_gelu2"], t + 1)
                        split_hidden(0, s["c_hi2"], t + 1, s["c_split2"], at=4)
                    c_finish(g, True)
            g0, g1 = bounds(dve, 1, CLS - 1)
            with dve.Fori(g0, g1) as g:
                c_xlo(g + 1)
                c_finish(g, False)

        @block.gpsimd
        def _(pool):
            pool.memset(minus_half[:, :], -0.5).then_inc(s["half_ready"], 1)
            pool.memset(half[:, :], 0.5).then_inc(s["half_ready"], 1)
            pool.memset(masked[:, :, :], MASKED).then_inc(s["half_ready"], 1)
            pool.wait_ge(s["half_ready"], 3)
            with pool.Fori(0, R) as i:
                pool.wait_ge(s["gs_norm2"], i + 1)
                pool.tensor_tensor(gs[:, 2:3], gs[:, 0:1], half[0:2 * R, :], ALU.pow).then_inc(s["gs_norm"], 1)
            pool.wait_ge(s["gs_dot"], R + 1)
            pool.tensor_tensor(gs[:, 2:3], gs[:, 0:1], half[0:2 * R, :], ALU.pow).then_inc(s["gs_norm"], 1)

            def inverse_root(sem_var, n, sem_rstd):
                pool.wait_ge(sem_var, n)
                pool.tensor_tensor(rstd[:, :], vare[:, :], minus_half[:, :], ALU.pow).then_inc(sem_rstd, 1)

            def finish(pre, g, gain, offset, prior_out):
                inverse_root(s[pre + "_var"], g + 1, s[pre + "_rstd"])
                pool.wait_ge(s[pre + "_rstd"], apart(pool, g + 1))
                pool.wait_ge(s[pre + "_out"], prior_out)
                for p in range(PAIRS):
                    last = pool.tensor_scalar(yout[:, p, :], res[:, p, :], mv[:, p, 0:1], rstd[:, p:p + 1],
                                              ALU.subtract, ALU.mult)
                last.then_inc(s[pre + "_norm"], 1)
                pool.wait_ge(s[pre + "_norm"], g + 1)
                pool.tensor_tensor(yout[:, :, :], yout[:, :, :], gain, ALU.mult).then_inc(s[pre + "_gain"], 1)
                pool.wait_ge(s[pre + "_gain"], g + 1)
                pool.tensor_tensor(yout[:, :, :], yout[:, :, :], offset, ALU.add).then_inc(s[pre + "_y"], 1)

            def a_weights(e):
                pool.wait_ge(s["a_w_lo"], 2 * e)
                pool.dma_start(stage[:, 0, :].rearrange("p (k n) -> p k n", k=KC),
                               inp["L0_cond_Wi"][bass.ds(e, 1)].rearrange("a (k p) n -> p (a k) n", p=P))\
                    .then_inc(s["a_w_in"], 16)
                pool.dma_start(stage[:, 1, :].rearrange("p (k n) -> p k n", k=FC),
                               inp["L0_cond_Wo"][bass.ds(e, 1)].rearrange("a (k p) n -> p (a k) n", p=P))\
                    .then_inc(s["a_w_in"], 16)

            def a_tiles(e):
                def erow(n):
                    return erows[:, n, bass.ds(e, 1), :].to_broadcast([P, PAIRS, D])
                g0, g1 = bounds(pool, 0, e)
                with pool.Fori(g0, g1) as g:
                    pool.wait_ge(s["a_x_in"], g * (16 * QS) + 16 * QS)
                    pool.wait_ge(s["a_res"], g)
                    pool.tensor_tensor(xb[:, :, :], xin[:, :, :], erow(0), ALU.add).then_inc(s["a_xb"], 1)
                    finish("a", g, erow(1), erow(2), g * (16 * QS))

            pool.wait_ge(s["erows_in"], 16 * 3)
            pool.wait_ge(s["turned"], 4)
            pool.wait_ge(s["stage_lo"], len(B_STAGES))
            pool.wait_ge(s["route_ready"], 2)
            a_weights(0)
            with pool.Fori(0, E - 1) as e:
                a_weights(e + 1)
                a_tiles(e)
            a_tiles(E - 1)

            n_a = total(pool, 0)
            pool.wait_ge(s["a_out"], apart(pool, n_a * (16 * QS)))
            pool.wait_ge(s["mask_in"], 32)

            def b_masks(i):
                pool.tensor_copy(maskf[:, :, :], mask8[:, bass.ds(i * PAIRS, PAIRS), :]).then_inc(s["b_mask"], 1)
                pool.wait_ge(s["b_mask"], 2 * i + 1)
                pool.tensor_tensor(maskf[:, :, :], maskf[:, :, :], masked[:, :, :].to_broadcast([P, PAIRS, S]),
                                   ALU.mult).then_inc(s["b_mask"], 1)
                pool.wait_ge(s["b_mask"], 2 * i + 2)
                pool.wait_ge(s["b_bias_in"], i * (16 * QS) + 16 * QS)
                for p in range(PAIRS):
                    v = bias[:, p, :].rearrange("q (h k) -> q h k", h=NH)
                    pool.tensor_tensor(v, v, maskf[:, p:p + 1, :].to_broadcast([P, NH, S]), ALU.add)\
                        .then_inc(s["b_bias"], 1)

            def b_modulate(i):
                inverse_root(s["b_var"], i + 1, s["b_rstd"])
                pool.wait_ge(s["b_norm"], i + 1)
                pool.wait_ge(s["b_ada_in"], i * (16 * QS) + 16 * QS)
                pool.tensor_tensor(xm[:, :, :], xm[:, :, :], ada[:, :, 0:D], ALU.mult).then_inc(s["b_scaled"], 1)
                pool.wait_ge(s["b_scaled"], i + 1)
                pool.tensor_tensor(xm[:, :, :], xm[:, :, :], ada[:, :, D:2 * D], ALU.add).then_inc(s["b_xm"], 1)
                pool.wait_ge(s["b_xm"], i + 1)
                pool.tensor_tensor(xb[:, :, :], xm[:, :, :], row("L1_cond_bo"), ALU.add).then_inc(s["b_xb"], 1)

            def b_probs(i):
                for p in range(PAIRS):
                    pool.wait_ge(s["b_rsum"], 2 * i + p + 1)
                    v = att[:, p, :].rearrange("q (h k) -> q h k", h=NH)
                    pool.tensor_tensor(v, v, asum[:, p, :].rearrange("q (h o) -> q h o", o=1).to_broadcast([P, NH, S]),
                                       ALU.mult).then_inc(s["b_prob"], 1)

            def b_base(i):
                pool.wait_ge(s["b_x1"], i + 1)
                inverse_root(s["b_var2"], i + 1, s["b_rstd2"])
                pool.tensor_tensor(x1b, x1[:, :, :], row("L1_cond_b2"), ALU.add).then_inc(s["b_x1b"], 1)

            with pool.Fori(0, NQ) as i:
                b_modulate(i)
                b_masks(i)
                b_probs(i)
                b_base(i)

            def c_tile(g, bias_row):
                pool.wait_ge(s["c_x_in"], apart(pool, g * (16 * QS) + 16 * QS))
                pool.wait_ge(s["c_res"], g)
                if bias_row is None:
                    pool.tensor_copy(xb[:, :, :], xin[:, :, :]).then_inc(s["c_xb"], 1)
                else:
                    pool.tensor_tensor(xb[:, :, :], xin[:, :, :], bias_row, ALU.add).then_inc(s["c_xb"], 1)
                finish("c", g, row("L3_cond_gamma"), row("L3_cond_beta"), g * (16 * QS))

            for c in range(CLS):
                g0, g1 = bounds(pool, 1, c)
                with pool.Fori(g0, g1) as g:
                    c_tile(g, row(OUT_BIAS[c]) if c < len(OUT_BIAS) else None)


def kernel(**inputs):
    import concourse.bacc as bacc
    from concourse.bass_utils import run_bass_kernel_spmd

    nc = bacc.Bacc("TRN2", target_bir_lowering=False, num_devices=1)
    arrays, aps = {}, {}
    for name, a in inputs.items():
        a = np.ascontiguousarray(a)
        arrays[name] = a
        aps[name] = nc.dram_tensor(name, a.shape, mybir.dt.from_np(a.dtype), kind="ExternalInput").ap()
    arrays["const"] = constants()
    const = nc.dram_tensor("const", (P, CONST_W), F32, kind="ExternalInput").ap()
    out = nc.dram_tensor("out", (ROWS, S, D), F32, kind="ExternalOutput").ap()
    build(nc, aps, const, out)
    r = run_bass_kernel_spmd(nc, [arrays], core_ids=[0])
    return r.results[0]["out"][:B]
```

```python
from contextlib import ExitStack

import numpy as np

import concourse.bass as bass
from concourse import mybir

F32 = mybir.dt.float32
F32R = mybir.dt.float32r
I32 = mybir.dt.int32
U8 = mybir.dt.uint8
ACT = mybir.ActivationFunctionType
ALU = mybir.AluOpType
X = mybir.AxisListType.X

P = 128
B, S, D = 128, 64, 256
E, FF = 8, 1024
NH, HD = 16, 16
R = 32
QS = 4
PAIRS = QS * S // P
TQ = QS * S
KC = D // P
FC = FF // P
NQ = B // QS
CLS = 4
A_TILES = NQ + E
C_TILES = NQ + CLS
A_SLOTS = QS * (A_TILES + 1)
C_SLOTS = QS * (C_TILES + 1)
ROWS = B + QS
MASKED = -1e30

CONST = {}
_n = 0
for _name, _w in (("ident", P), ("before", P), ("ones", P), ("slot", A_SLOTS), ("slot4", A_SLOTS),
                  ("quads", NQ), ("class", E), ("less", E * E), ("freq", 1), ("head", 2), ("sample", 1),
                  ("later", A_TILES), ("pick", 2 * A_TILES)):
    CONST[_name] = (_n, _n + _w)
    _n += _w
CONST_W = _n

COLS = {}
_n = 0
for _name, _w in (("L0_cond_bi", E * FC), ("L1_cond_bq", KC), ("L1_cond_bk", KC), ("L1_cond_b1", FC),
                  ("L1_cond_g2", KC), ("L1_cond_beta2", KC), ("L3_cond_b1_nr", KC), ("L3_cond_b1_tsr", KC),
                  ("L3_cond_b1_sr", 2 * KC), ("L3_cond_b2_sr", KC)):
    COLS[_name] = (_n, _n + _w)
    _n += _w
COLS_W = _n

ROWS_OF = {}
_n = 0
for _name, _w in (("L1_cond_bv", 1),
                  ("L1_cond_bo", 1), ("L1_cond_b2", 1), ("L2_cond_resp_b", 1), ("L2_cond_safety_bias", 1),
                  ("L3_cond_b2_nr", 1), ("L3_cond_b2_tsr", 1), ("L3_cond_b3_sr", 1), ("L3_cond_gamma", 1),
                  ("L3_cond_beta", 1)):
    ROWS_OF[_name] = (_n, _n + _w)
    _n += _w
ROWS_W = _n

EROWS = ("L0_cond_bo", "L0_cond_gamma", "L0_cond_beta")
WB = (("L1_cond_Wq", KC, D), ("L1_cond_Wk", KC, D), ("L1_cond_Wv", KC, D), ("L1_cond_Wo", KC, D),
      ("L1_cond_W1", KC, FF), ("L1_cond_W2", FC, D))
WC = (("L3_cond_w1_nr", KC, D), ("L3_cond_w2_nr", KC, D), ("L3_cond_w1_tsr", KC, D), ("L3_cond_w2_tsr", KC, D),
      ("L3_cond_w1_sr", KC, 2 * D), ("L3_cond_w2_sr", 2 * KC, D), ("L3_cond_w3_sr", KC, D))
STAGE = 2048
B_STAGES = (WB[0:4], WB[4:5], WB[5:6])
C_PARTS = (WC[0:3], WC[3:5], WC[5:7])
RAW = sum(a * b for _, a, b in C_PARTS[0])
BRANCHES = (("L3_cond_w1_nr", "L3_cond_w2_nr", None), ("L3_cond_w1_tsr", "L3_cond_w2_tsr", None),
            ("L3_cond_w1_sr", "L3_cond_w2_sr", "L3_cond_w3_sr"))
OUT_BIAS = ("L3_cond_b2_nr", "L3_cond_b2_tsr", "L3_cond_b3_sr")
HALF_TURN = float(np.nextafter(np.float32(np.pi), np.float32(0)))
TURN1 = 6.28125
TURN2 = float(np.float32(round((2 * np.pi - TURN1) * 2 ** 20) / 2 ** 20))
TURN3 = 2 * np.pi - TURN1 - TURN2
ROUNDER = 1.5 * 2 ** 23


def constants():
    c = np.zeros((P, CONST_W), np.float32)

    def put(name, a):
        c[:, CONST[name][0]:CONST[name][1]] = a

    i = np.arange(P)
    put("ident", np.eye(P))
    put("before", i[:, None] < i[None, :])
    put("ones", 1.0)
    put("slot", np.arange(A_SLOTS))
    put("slot4", np.arange(A_SLOTS) % QS)
    put("quads", [-1.0] + [QS * j for j in range(1, NQ)])
    put("class", np.arange(E))
    put("less", (np.arange(E)[None, :] < np.arange(E)[:, None]).reshape(1, -1))
    put("freq", np.exp(np.arange(P, dtype=np.float32) * np.float32(-np.log(10000.0) / (P - 1)))[:, None])
    put("head", np.stack([(i // HD) % 2 == 0, (i // HD) % 2 == 1], 1) * HD ** -0.5)
    put("sample", (i - B)[:, None])
    step = np.arange(A_TILES)
    put("later", np.where(((i % R)[:, None] > step[None, :]) & (step < R), -1.0, 0.0))
    put("pick", np.concatenate([(i[:, None] == a * R + step[None, :]) & (step < R) for a in range(2)], 1))
    return c


def build(nc, inp, const, out):
    ctx = ExitStack()
    with ctx:
        def sb(name, shape, dt=F32):
            return ctx.enter_context(nc.sbuf_tensor(name, shape, dt))

        def sem(name):
            return ctx.enter_context(nc.semaphore(name))

        x_rows = inp["x"]
        l0_out = nc.dram_tensor("l0_out", (ROWS, S, D), F32, kind="Internal").ap()
        l2_out = nc.dram_tensor("l2_out", (B, S, D), F32, kind="Internal").ap()
        emb_dram = nc.dram_tensor("emb_dram", (B, 2 * D), F32, kind="Internal").ap()

        cst = sb("cst", [P, CONST_W])
        idx = sb("idx", [P, 2], I32)
        idxf = sb("idxf", [P, 2])
        cols_in = sb("cols_in", [COLS_W, P])
        cols = sb("cols", [P, COLS_W])
        rows = sb("rows", [P, ROWS_W, D])
        resp_bias = sb("resp_bias", [P, D])
        bq_head = sb("bq_head", [P, KC, 2])

        def k(name):
            return cst[:, CONST[name][0]:CONST[name][1]]

        def col(name, j):
            c0 = COLS[name][0] + j
            return cols[:, c0:c0 + 1]

        def row(name, rep=PAIRS):
            r0 = ROWS_OF[name][0]
            return rows[:, r0:r0 + 1, :].to_broadcast([P, rep, D])

        ident = k("ident")

        onehot = sb("onehot", [P, 2, E])
        quads = sb("quads", [P, E])
        start = sb("start", [P, E])
        end = sb("end", [P, E])
        slot_e = sb("slot_e", [P, E])
        slot_of = sb("slot_of", [P, 1])
        start_i = sb("start_i", [1, 2, E], I32)
        end_i = sb("end_i", [1, 2, E], I32)
        src_i = sb("src_i", [1, 2, A_SLOTS], I32)
        dst_i = sb("dst_i", [1, 2, QS + A_SLOTS], I32)
        last_e = sb("last_e", [1, 1, A_TILES + 1], I32)

        wb_hi = sb("wb_hi", [P, sum(a * b for _, a, b in WB)], F32R)
        wb_lo = sb("wb_lo", [P, sum(a * b for _, a, b in WB)], F32R)
        wc_hi = sb("wc_hi", [P, sum(a * b for _, a, b in WC)], F32R)
        wc_lo = sb("wc_lo", [P, sum(a * b for _, a, b in WC)], F32R)
        stage = sb("stage", [P, 2, STAGE])
        m_hi = sb("m_hi", [P, KC, D], F32R)
        m_lo = sb("m_lo", [P, KC, D], F32R)

        def views(parts, hi, lo):
            v, n = {}, 0
            for name, a, b in parts:
                v[name] = [t[:, n:n + a * b].rearrange("p (k n) -> p k n", k=a) for t in (hi, lo)]
                n += a * b
            return v

        w = {**views(WB, wb_hi, wb_lo), **views(WC, wc_hi, wc_lo)}
        wi = [t[:, 0:STAGE].rearrange("p (k n) -> p k n", k=KC) for t in (wc_hi, wc_lo)]
        wo = [t[:, STAGE:2 * STAGE].rearrange("p (k n) -> p k n", k=FC) for t in (wc_hi, wc_lo)]

        xin = sb("xin", [P, PAIRS, D])
        xb = sb("xb", [P, PAIRS, D])
        xh = sb("xh", [P, KC, TQ], F32R)
        xl = sb("xl", [P, KC, TQ], F32R)
        hid = sb("hid", [P, FC, TQ])
        hid_h = sb("hid_h", [P, FC, TQ], F32R)
        hid_l = sb("hid_l", [P, FC, TQ], F32R)
        res = sb("res", [P, PAIRS, D])
        stats = sb("stats", [P, PAIRS, 6])
        mv = sb("mv", [P, PAIRS, 2])
        vare = sb("vare", [P, PAIRS])
        rstd = sb("rstd", [P, PAIRS])
        neg_mean = sb("neg_mean", [P, PAIRS])
        shift = sb("shift", [P, PAIRS])
        stats1 = sb("stats1", [P, PAIRS, 6])
        mv1 = sb("mv1", [P, PAIRS, 2])
        vare1 = sb("vare1", [P, PAIRS])
        rstd1 = sb("rstd1", [P, PAIRS])
        minus_half = sb("minus_half", [P, PAIRS])
        half = sb("half", [P, 1])
        masked = sb("masked", [P, 1, 1])
        yout = sb("yout", [P, PAIRS, D])

        shared = sb("shared", [P, 3 * E * D])
        erows = shared[:, :].rearrange("p (w e d) -> p w e d", w=3, e=E)
        at = [0]

        def part(n):
            at[0] += n
            return shared[:, at[0] - n:at[0]]

        prob_t = part(4 * PAIRS * KC * P).rearrange("p (n r q) -> p n r q", r=4, q=P)
        qm = part(KC * 2 * TQ).rearrange("p (c h t) -> p c h t", c=KC, h=2)
        kt = part(KC * TQ).rearrange("p (c t) -> p c t", c=KC)
        vblk = part(PAIRS * 2 * D).rearrange("p (a b d) -> p a b d", a=PAIRS, b=2)
        x1b = part(PAIRS * D).rearrange("p (a d) -> p a d", a=PAIRS)
        xn = part(PAIRS * D).rearrange("p (a d) -> p a d", a=PAIRS)
        x2 = part(PAIRS * D).rearrange("p (a d) -> p a d", a=PAIRS)
        x1 = res
        ctxn = xn

        ada = sb("ada", [P, PAIRS, 2 * D])
        xm = sb("xm", [P, PAIRS, D])
        mask8 = sb("mask8", [P, B // 2, S], U8)
        maskf = sb("maskf", [P, PAIRS, S])
        bias = stage[:, 0, :].rearrange("p (a n) -> p a n", a=PAIRS)
        att = stage[:, 1, :].rearrange("p (a n) -> p a n", a=PAIRS)
        amax = sb("amax", [P, PAIRS, NH])
        asum = sb("asum", [P, PAIRS, NH])
        ctx_h = sb("ctx_h", [P, KC, TQ], F32R)
        ctx_l = sb("ctx_l", [P, KC, TQ], F32R)
        ht = sb("ht", [P, KC, TQ])
        ht_h = sb("ht_h", [P, KC, TQ], F32R)
        ht_l = sb("ht_l", [P, KC, TQ], F32R)
        pooled = sb("pooled", [P, KC, QS])
        gate1 = sb("gate1", [S, TQ])
        expz = sb("expz", [P, PAIRS])
        den = sb("den", [P, PAIRS])
        strength = sb("strength", [P, PAIRS])

        hflat = hid[:, :, :].rearrange("p f t -> p (f t)")
        over = hflat[:, 0:E * NQ].rearrange("p (e q) -> p e q", e=E)
        prior = hflat[:, 256:256 + E * E].rearrange("p (e f) -> p e f", e=E)
        placed = hflat[:, 320:320 + A_SLOTS]
        ended = yout[0:1, :, :].rearrange("p a d -> p (a d)")[:, 0:E * (A_TILES + 1)]
        last_f = yout[0:1, :, :].rearrange("p a d -> p (a d)")[:, E * (A_TILES + 1):(E + 1) * (A_TILES + 1)]
        srow = hflat[0:1, 512:512 + A_SLOTS]
        sempty = hflat[0:1, 704:704 + A_SLOTS]
        tstep = hflat[:, 1920:1920 + P].bitcast(I32)
        tf, tq, tr = (hflat[:, 896 + n * P:896 + (n + 1) * P] for n in range(3))
        ang = hflat[:, 1280:1408]
        turns = hflat[:, 1408:1664].rearrange("p (a n) -> p a n", a=2)
        wrap = hflat[:, 1664:1920].rearrange("p (a n) -> p a n", a=2)
        w_ada = ada
        b_ada = xm[:, :, :].rearrange("p a d -> p (a d)")
        emb = ht[:, :, :].rearrange("p a d -> p (a d)")
        uv = sb("uv", [P, KC, 2 * R])
        uvt = xm[0:2 * R, 0, :]
        sel = sb("sel", [2 * R, 2, R])
        junk = xm[0:2 * R, 1, :]
        qv = x2[0:R, 0, :]
        c_t = x2[0:R, 1, :]
        basis_t = xm
        resp_in = sb("resp_in", [P, KC, R])
        resp_t = gate1[0:R, :]
        gs = sb("gs", [2 * R, 8])
        gw1_in = xb[0:S, 0, :]
        gw1_t = sb("gw1_t", [P, KC, S])
        gw2_t = sb("gw2_t", [S, 1])
        gb1 = sb("gb1", [S, 1])
        gb2 = sb("gb2", [P, 1])
        safety = sb("safety", [P, B])
        modden = sb("modden", [P, B // 2])

        ps = ctx.enter_context(nc.psum_tensor("ps", [P, 8, 512], F32))

        def bank(n, shape=None, **kw):
            return ps[:, n, :] if shape is None else ps[:, n, :].rearrange(shape, **kw)

        names = """const_in idx_in cols_in_in rows_in small_in stage_hi stage_lo
            mask_in setup_dve setup_act routed_onehot routed_ps routed_placed route_ready
            turned half_ready
            wrap_ready emb_done emb_out
            gs_sel gs_row gs_norm2 gs_dot gs_norm gs_step gs_done
            m_ps m_sb m_hi_ready m_ready vblk_zero
            a_w_in a_w_hi a_w_lo a_x_in a_xT a_xh a_xl a_xb a_fc1 a_gelu a_hi a_split a_fc2 a_res a_stat a_var
            a_rstd a_shift a_norm a_gain a_y a_out blank_xb blank_ps raw_in raw_hi raw_lo
            b_x_in b_ada_in b_bias_in b_bias b_mask b_stat b_var b_rstd b_norm b_scaled b_xm b_xb b_xT b_xh b_xl
            b_qkv b_q b_v b_score b_added b_max b_sub b_exp b_sum b_rsum b_ctx b_ctxT b_pT b_pTs b_pv b_ctxh b_ctxl
            b_wo b_x1 b_stat2 b_var2 b_rstd2 b_xn b_x1b b_xnT b_hth b_ht b_htl b_fc1 b_gelu b_hi b_split b_fc2
            b_x2 b_x2T b_x2h b_x2l b_pool b_gate1 b_gate1s b_gate2 b_expz b_strength b_resp b_corr b_x3 b_out
            c_x_in c_xT c_xh c_xl c_xb c_out_ps c_res c_stat c_var c_rstd c_shift c_norm c_gain c_y c_out stage_in_0 stage_in_1 gs_chain setup_ps""".split()
        sems = {}
        for n in names:
            sems[n] = sem(n)
        for c in range(len(BRANCHES)):
            for n in ("fc1", "gelu", "hi", "split"):
                sems[f"c_{n}_{c}"] = sem(f"c_{n}_{c}")
        for n in ("fc2", "gelu2", "hi2", "split2"):
            sems[f"c_{n}"] = sem(f"c_{n}")
        s = sems
        block = ctx.enter_context(nc.Block())
        hid_flat = hid[:, :, :].rearrange("p f t -> p (f t)")
        raw_cols = [slice(n * RAW, (n + 1) * RAW) for n in range(len(C_PARTS))]
        raws = [hid_flat[:, 0:RAW], stage[:, 1, 0:RAW], hid_flat[:, 0:RAW]]

        def apart(eng, value):
            value = eng.to_reg(value)
            eng.wait_ge(s["const_in"], 16)
            return value

        def passes(pe, o, lhs, rhs, first, last):
            pe.matmul(o, lhs[0], rhs[0], start=first, stop=False)
            pe.matmul(o, lhs[0], rhs[1], start=False, stop=False)
            return pe.matmul(o, lhs[1], rhs[0], start=False, stop=last)

        def bounds(eng, which, e):
            tiles = A_TILES if which == 0 else C_TILES
            a = eng.value_load(start_i[0:1, which, bass.ds(e, 1)], min_val=0, max_val=tiles - 1)
            z = eng.value_load(end_i[0:1, which, bass.ds(e, 1)], min_val=1, max_val=tiles)
            return a, z

        def total(eng, which):
            last = (E if which == 0 else CLS) - 1
            return eng.value_load(end_i[0:1, which, last:last + 1], min_val=1,
                                  max_val=A_TILES if which == 0 else C_TILES)

        def stage_dmas(n):
            return 16 * sum(len(names) for names in B_STAGES[n % 2:n + 1:2])

        @block.sync
        def _(sp):
            sp.dma_start(cst[:, :], const).then_inc(s["const_in"], 16)
            sp.dma_start(idx[:, 0:1], inp["itok_B_0_7"].rearrange("(b o) -> b o", o=1)).then_inc(s["idx_in"], 16)
            sp.dma_start(idx[:, 1:2], inp["itok_B_0_2"].rearrange("(b o) -> b o", o=1)).then_inc(s["idx_in"], 16)
            for name, (a, z) in COLS.items():
                src = inp[name]
                src = (src.rearrange("e (f p) -> (e f) p", p=P) if len(src.shape) == 2
                       else src.rearrange("(f p) -> f p", p=P))
                sp.dma_start(cols_in[a:z, :], src).then_inc(s["cols_in_in"], 16)
            for name, (a, z) in ROWS_OF.items():
                src = inp[name]
                src = src if len(src.shape) == 2 else src.rearrange("(o d) -> o d", o=1)
                sp.dma_start(rows[:, a:z, :], src.partition_broadcast(P)).then_inc(s["rows_in"], 16)
            sp.dma_start(uv[:, :, 0:R], inp["L2_cond_U"].rearrange("(c p) r -> p c r", p=P)).then_inc(s["small_in"], 16)
            sp.dma_start(uv[:, :, R:2 * R], inp["L2_cond_V"].rearrange("(c p) r -> p c r", p=P)).then_inc(s["small_in"], 16)
            sp.dma_start(tstep[:, :], inp["itok_B_34_63"].partition_broadcast(P)).then_inc(s["small_in"], 16)
            sp.dma_start(w_ada[:, :, :], inp["L1_cond_W_ada"].rearrange("(c p) n -> p c n", p=P)).then_inc(s["small_in"], 16)
            sp.dma_start(b_ada, inp["L1_cond_b_ada"].partition_broadcast(P)).then_inc(s["small_in"], 16)
            sp.dma_start(resp_in[:, :, :], inp["L2_cond_resp_w"].rearrange("(c p) r -> p c r", p=P)).then_inc(s["small_in"], 16)
            sp.dma_start(gw1_in, inp["L2_cond_gate_w1"]).then_inc(s["small_in"], 16)
            sp.dma_start(gw2_t[:, :], inp["L2_cond_gate_w2"].rearrange("o n -> n o")).then_inc(s["small_in"], 16)
            sp.dma_start(gb1[:, :], inp["L2_cond_gate_b1"].rearrange("(n o) -> n o", o=1)).then_inc(s["small_in"], 16)
            sp.dma_start(gb2[:, :], inp["L2_cond_gate_b2"].partition_broadcast(P)).then_inc(s["small_in"], 16)
            sp.dma_start(safety[:, :], inp["condB_safetyscore"].partition_broadcast(P)).then_inc(s["small_in"], 16)
            for n, name in enumerate(EROWS):
                sp.dma_start(erows[:, n, :, :], inp[name].partition_broadcast(P)).then_inc(s["rows_in"], 16)
            for b2 in range(2):
                sp.dma_start(mask8[b2 * S:(b2 + 1) * S, :, :],
                             inp["mask_Bx1xSxS_bk0"].rearrange("(n b) o q k -> b q (n o) k", b=2)[b2])\
                    .then_inc(s["mask_in"], 16)
            sp.wait_ge(s["emb_done"], 1)
            sp.dma_start(emb_dram, emb).then_inc(s["emb_out"], 16)

            def load_stage(n, names):
                if n >= 2:
                    sp.wait_ge(s["stage_lo"], n - 1)
                at = 0
                for name, a, b in names:
                    sp.dma_start(stage[:, n % 2, at:at + a * b].rearrange("p (k n) -> p k n", k=a),
                                 inp[name].rearrange("(k p) n -> p k n", p=P)).then_inc(s[f"stage_in_{n % 2}"], 16)
                    at += a * b
            for n, names in enumerate(B_STAGES):
                load_stage(n, names)

            sp.wait_ge(s["route_ready"], 2)
            sp.wait_ge(s["stage_lo"], len(B_STAGES))

            def a_load(g):
                for j in range(QS):
                    n = sp.value_load(src_i[0:1, 0, bass.ds(g * QS + j, 1)], min_val=0, max_val=B - 1)
                    sp.dma_start(xin[(j % 2) * S:(j % 2 + 1) * S, j // 2, :],
                                 x_rows[bass.ds(n, 1)].rearrange("a s d -> (a s) d")).then_inc(s["a_x_in"], 16)

            def a_store(g):
                sp.wait_ge(s["a_y"], g + 1)
                for j in range(QS):
                    n = sp.value_load(dst_i[0:1, 0, bass.ds(g * QS + j, 1)], min_val=0, max_val=ROWS - 1)
                    sp.dma_start(l0_out[bass.ds(n, 1)].rearrange("a s d -> (a s) d"),
                                 yout[(j % 2) * S:(j % 2 + 1) * S, j // 2, :]).then_inc(s["a_out"], 16)

            def a_next(g):
                sp.wait_ge(s["a_xT"], g + 1)
                sp.wait_ge(s["a_xb"], g + 1)
                a_load(g + 1)

            a_load(0)
            n_a = total(sp, 0)
            with sp.Fori(0, n_a) as g:
                a_next(g)
                a_store(g)
            a_store(n_a)

            sp.wait_ge(s["a_out"], (n_a + 1) * (16 * QS))
            sp.wait_ge(s["emb_out"], 16)

            def b_load(i):
                sp.dma_start(xin[:, :, :], l0_out[bass.ds(i * QS, QS)].rearrange("(a b) s d -> (b s) a d", b=2))\
                    .then_inc(s["b_x_in"], 16)
                for p in range(PAIRS):
                    for b2 in range(2):
                        sp.dma_start(ada[b2 * S:(b2 + 1) * S, p, :],
                                     emb_dram[bass.ds(i * QS + 2 * p + b2, 1), :].to_broadcast([S, 2 * D]))\
                            .then_inc(s["b_ada_in"], 16)

            def b_load_bias(i):
                for p in range(PAIRS):
                    for b2 in range(2):
                        sp.dma_start(bias[b2 * S:(b2 + 1) * S, p, :].rearrange("q (h k) -> q h k", h=NH),
                                     inp["fside_Bx16xSxS_0"][bass.ds(i * QS + 2 * p + b2, 1)]
                                     .rearrange("a h q k -> q (a h) k")).then_inc(s["b_bias_in"], 16)

            def b_store(i):
                sp.wait_ge(s["b_x3"], i + 1)
                sp.dma_start(l2_out[bass.ds(i * QS, QS)].rearrange("(a b) s d -> (b s) a d", b=2), yout[:, :, :])\
                    .then_inc(s["b_out"], 16)

            def b_step(i, loads=2, stores=True):
                if loads >= 1:
                    sp.wait_ge(s["b_added"], 2 * i + 2)
                    b_load_bias(i + 1)
                if loads >= 2:
                    sp.wait_ge(s["b_xm"], i + 2)
                    b_load(i + 2)
                if stores:
                    b_store(i - 1)

            b_load(0)
            b_load_bias(0)
            for n, names in enumerate(C_PARTS):
                if n == 2:
                    sp.wait_ge(s["raw_lo"], 1)
                at = 0
                for name, a, b in names:
                    sp.dma_start(raws[n][:, at:at + a * b].rearrange("p (k n) -> p k n", k=a),
                                 inp[name].rearrange("(k p) n -> p k n", p=P)).then_inc(s["raw_in"], 16)
                    at += a * b
            sp.wait_ge(s["b_xm"], 1)
            b_load(1)
            b_step(0, stores=False)
            with sp.Fori(1, NQ - 2) as i:
                b_step(i)
            b_step(NQ - 2, loads=1)
            b_step(NQ - 1, loads=0)
            b_store(NQ - 1)

            sp.wait_ge(s["b_out"], 16 * NQ)

            def c_load(g):
                for j in range(QS):
                    n = sp.value_load(src_i[0:1, 1, bass.ds(g * QS + j, 1)], min_val=0, max_val=B - 1)
                    sp.dma_start(xin[(j % 2) * S:(j % 2 + 1) * S, j // 2, :],
                                 l2_out[bass.ds(n, 1)].rearrange("a s d -> (a s) d")).then_inc(s["c_x_in"], 16)

            def c_store(g):
                sp.wait_ge(s["c_y"], g + 1)
                for j in range(QS):
                    n = sp.value_load(dst_i[0:1, 1, bass.ds(g * QS + QS + j, 1)], min_val=0, max_val=ROWS - 1)
                    sp.dma_start(out[bass.ds(n, 1)].rearrange("a s d -> (a s) d"),
                                 yout[(j % 2) * S:(j % 2 + 1) * S, j // 2, :]).then_inc(s["c_out"], 16)

            def c_next(g):
                sp.wait_ge(s["c_xT"], g + 1)
                sp.wait_ge(s["c_xb"], g + 1)
                c_load(g + 1)

            c_load(0)
            c_next(0)
            n_c = total(sp, 1)
            with sp.Fori(1, n_c) as g:
                c_next(g)
                c_store(g - 1)
            c_store(n_c - 1)
            sp.wait_ge(s["c_x_in"], apart(sp, (n_c + 1) * (16 * QS)))
            sp.wait_ge(s["c_out"], apart(sp, n_c * (16 * QS)))

        @block.tensor
        def _(pe):
            pe.wait_ge(s["const_in"], 16)
            pe.wait_ge(s["cols_in_in"], 16 * len(COLS))
            pe.transpose(ps[:, 7, 0:COLS_W], cols_in[:, :], ident[0:COLS_W, 0:COLS_W]).then_inc(s["setup_ps"], 1)

            for which in range(2):
                pe.wait_ge(s["routed_onehot"], which + 1)
                pe.matmul(ps[:, 0, 0:E], k("before"), onehot[:, which, :], start=True, stop=True)
                pe.matmul(ps[:, 1, 0:E], k("ones"), onehot[:, which, :], start=True, stop=True)\
                    .then_inc(s["routed_ps"], 1)
                pe.wait_ge(s["routed_placed"], which + 1)
                pe.matmul(ps[0:1, 2, 0:A_SLOTS], k("sample"), placed, start=True, stop=True)\
                    .then_inc(s["routed_ps"], 1)

            pe.wait_ge(s["small_in"], 16 * 11)
            for c in range(KC):
                pe.transpose(ps[:, 3, c * S:(c + 1) * S], gw1_in[:, c * P:(c + 1) * P], ident[0:S, 0:S])
            for c in range(KC):
                last = pe.transpose(ps[0:R, 5, c * P:(c + 1) * P], resp_in[:, c, :], ident)
            last.then_inc(s["setup_ps"], 1)
            for c in range(KC):
                last = pe.transpose(ps[0:2 * R, 4, c * P:(c + 1) * P], uv[:, c, :], ident)
            last.then_inc(s["setup_ps"], 1)

            pe.wait_ge(s["setup_act"], 2)
            for c in range(KC):
                last = pe.matmul(bank(6), wrap[:, c, :], w_ada[:, c, :], start=(c == 0), stop=(c == KC - 1))
            last.then_inc(s["setup_ps"], 1)

            def turn(src, dst):
                for p in range(PAIRS):
                    for c in range(KC):
                        last = pe.transpose(dst[:, c, p * P:(p + 1) * P], src[:, p, c * P:(c + 1) * P], ident)
                return last

            def hidden(o, wt, xs, f):
                n = len(xs)
                for c in range(n):
                    last = passes(pe, o, [t[:, c, f * P:(f + 1) * P] for t in wt], xs[c], c == 0, c == n - 1)
                return last

            def tokens_out(o, xs, wt, c, n):
                for p in range(PAIRS):
                    last = passes(pe, o[:, p, :], [t[:, c, p * P:(p + 1) * P] for t in xs],
                                  [t[:, c, :] for t in wt], c == 0 and p == 0, c == n - 1 and p == PAIRS - 1)
                return last

            xs = [[xh[:, c, :], xl[:, c, :]] for c in range(KC)]
            xT = bank(0, "p (c n) -> p c n", c=KC)

            def a_turn(g):
                pe.wait_ge(s["a_x_in"], g * (16 * QS) + 16 * QS)
                turn(xin, xT).then_inc(s["a_xT"], 1)

            o_ps = bank(5, "p (a n) -> p a n", a=PAIRS)
            a_turn(0)
            pe.wait_ge(s["blank_ps"], 1)
            with pe.Fori(0, E) as e:
                pe.wait_ge(s["a_w_lo"], 2 * e + 1)
                g0, g1 = bounds(pe, 0, e)
                with pe.Fori(g0, g1) as g:
                    pe.wait_ge(s["a_xl"], g + 1)
                    for f in range(FC):
                        last = hidden(ps[:, 1 + f // 2, (f % 2) * TQ:(f % 2 + 1) * TQ], wi, xs, f)
                        if f % 2 == 1:
                            last.then_inc(s["a_fc1"], 1)
                        if f == 3:
                            pe.wait_ge(s["gs_sel"], apart(pe, g + 1))
                            pe.matmul(ps[0:2 * R, 6, 0:D], sel[:, :, :], uvt[:, :], start=True, stop=True)\
                                .then_inc(s["gs_row"], 1)
                    pe.wait_ge(s["a_w_lo"], 2 * e + 2)
                    pe.wait_ge(s["a_res"], g + 1)
                    for c in range(FC):
                        if c % 2 == 0:
                            pe.wait_ge(s["a_split"], g * (FC // 2) + c // 2 + 1)
                        last = tokens_out(o_ps, [hid_h, hid_l], wo, c, FC)
                        if c == 3:
                            a_turn(g + 1)
                    last.then_inc(s["a_fc2"], 1)

            scores = ps[:, 0:4, :]
            q_ps, k_ps, v_ps = bank(0, "p (c n) -> p c n", c=KC), bank(1, "p (c n) -> p c n", c=KC), \
                bank(2, "p (a n) -> p a n", a=PAIRS)
            xT7 = bank(7, "p (c n) -> p c n", c=KC)
            pv_ps = bank(4, "p (a n) -> p a n", a=PAIRS)
            ctx_ps = bank(5, "p (c n) -> p c n", c=KC)
            wo_ps = bank(0, "p (a n) -> p a n", a=PAIRS)
            y_ps = bank(6, "p (a n) -> p a n", a=PAIRS)
            r_ps = bank(1, "p (a n) -> p a n", a=PAIRS)

            def b_qkv(i):
                pe.wait_ge(s["b_xm"], i + 1)
                turn(xm, xT7).then_inc(s["b_xT"], 1)
                pe.wait_ge(s["b_xl"], i + 1)
                for f in range(KC):
                    hidden(q_ps[:, f, :], w["L1_cond_Wq"], xs, f)
                for f in range(KC):
                    last = hidden(k_ps[:, f, :], w["L1_cond_Wk"], xs, f)
                last.then_inc(s["b_qkv"], 1)
                for c in range(KC):
                    last = tokens_out(v_ps, [xh, xl], w["L1_cond_Wv"], c, KC)
                last.then_inc(s["b_qkv"], 1)

            def b_turn_ffn(i):
                pe.wait_ge(s["b_xn"], i + 1)
                turn(xn, xT7).then_inc(s["b_xnT"], 1)

            def b_scores(i):
                pe.wait_ge(s["b_q"], 2 * i + 2)
                pe.wait_ge(s["b_v"], i + 1)
                for p in range(PAIRS):
                    for c in range(KC):
                        for par in range(2):
                            for b2 in range(2):
                                t0 = p * P + b2 * S
                                for r in range(4):
                                    last = pe.matmul(
                                        scores[b2 * S:(b2 + 1) * S, r,
                                               (p * 4 + c * 2 + par) * S:(p * 4 + c * 2 + par + 1) * S],
                                        qm[r * 32:(r + 1) * 32, c, par, t0:t0 + S],
                                        kt[r * 32:(r + 1) * 32, c, t0:t0 + S], start=True, stop=True)
                last.then_inc(s["b_score"], 1)

            def b_ffn(i):
                pe.wait_ge(s["b_htl"], i + 1)
                for f in range(FC):
                    if f % 2 == 0 and f >= 4:
                        pe.wait_ge(s["b_gelu"], i * (FC // 2) + f // 2 - 1)
                    last = hidden(ps[:, 4 + f // 2 % 2, (f % 2) * TQ:(f % 2 + 1) * TQ], w["L1_cond_W1"],
                                  [[ht_h[:, c, :], ht_l[:, c, :]] for c in range(KC)], f)
                    if f % 2 == 1:
                        last.then_inc(s["b_fc1"], 1)
                for c in range(FC):
                    if c % 2 == 0:
                        pe.wait_ge(s["b_split"], i * (FC // 2) + c // 2 + 1)
                    last = tokens_out(y_ps, [hid_h, hid_l], w["L1_cond_W2"], c, FC)
                last.then_inc(s["b_fc2"], 1)

            def b_values(i):
                pe.wait_ge(s["b_added"], 2 * i + 2)
                for p in range(PAIRS):
                    pe.wait_ge(s["b_exp"], 2 * i + p + 1)
                    for c in range(KC):
                        for r in range(4):
                            last = pe.transpose(ps[:, p * KC + c, r * P:(r + 1) * P],
                                                att[:, p, (c * 4 + r) * P:(c * 4 + r + 1) * P], ident)
                    last.then_inc(s["b_pT"], 1)
                for p in range(PAIRS):
                    pe.wait_ge(s["b_pTs"], 2 * i + p + 1)
                    for c in range(KC):
                        for b2 in range(2):
                            for r in range(4):
                                cols_of = slice(c * P + r * 32, c * P + (r + 1) * 32)
                                last = pe.matmul(pv_ps[b2 * S:(b2 + 1) * S, p, cols_of],
                                                 prob_t[:, p * KC + c, r, b2 * S:(b2 + 1) * S],
                                                 vblk[:, p, b2, cols_of], start=True, stop=True)
                last.then_inc(s["b_pv"], 1)

            def b_turn_ctx(i):
                pe.wait_ge(s["b_ctx"], i + 1)
                turn(ctxn, ctx_ps).then_inc(s["b_ctxT"], 1)

            def b_turn_l2(i):
                pe.wait_ge(s["b_x2"], i + 1)
                turn(x2, xT7).then_inc(s["b_x2T"], 1)

            def b_wo(i):
                pe.wait_ge(s["b_ctxl"], i + 1)
                for c in range(KC):
                    last = tokens_out(wo_ps, [ctx_h, ctx_l], w["L1_cond_Wo"], c, KC)
                last.then_inc(s["b_wo"], 1)

            def b_l2(i):
                pe.wait_ge(s["b_x2l"], i + 1)
                for c in range(KC):
                    last = tokens_out(r_ps, [xh, xl], [m_hi, m_lo], c, KC)
                last.then_inc(s["b_resp"], 1)

            def b_gate(i):
                pe.wait_ge(s["b_pool"], i + 1)
                for c in range(KC):
                    last = pe.matmul(ps[0:S, 7, 0:QS], gw1_t[:, c, :], pooled[:, c, :],
                                     start=(c == 0), stop=(c == KC - 1))
                last.then_inc(s["b_gate1"], 1)
                pe.wait_ge(s["b_gate1s"], i + 1)
                for p in range(PAIRS):
                    last = pe.matmul(ps[:, 2, p:p + 1], gate1[:, p * P:(p + 1) * P], gw2_t[:, :],
                                     start=True, stop=True)
                last.then_inc(s["b_gate2"], 1)

            def b_step(i, here=True, prev=True, back=True):
                if here:
                    if prev:
                        pe.wait_ge(s["b_x1"], i)
                    if back:
                        pe.wait_ge(s["b_corr"], i - 1)
                        pe.wait_ge(s["b_expz"], i - 1)
                    b_qkv(i)
                if prev:
                    b_turn_ffn(i - 1)
                if here:
                    b_scores(i)
                if prev:
                    b_ffn(i - 1)
                if here:
                    b_values(i)
                if prev:
                    b_turn_l2(i - 1)
                if here:
                    b_turn_ctx(i)
                if prev:
                    b_l2(i - 1)
                if here:
                    b_wo(i)
                if prev:
                    b_gate(i - 1)

            pe.wait_ge(s["gs_done"], 1)
            for c in range(KC):
                last = pe.matmul(ps[:, 1, c * D:(c + 1) * D], qv[:, c * P:(c + 1) * P], uvt[0:R, :],
                                 start=True, stop=True)
            last.then_inc(s["m_ps"], 1)
            pe.wait_ge(s["m_sb"], 1)
            for c in range(KC):
                last = pe.matmul(ps[0:R, 2, 0:D], basis_t[:, c, 0:R], basis_t[:, c, :],
                                 start=(c == 0), stop=(c == KC - 1))
            last.then_inc(s["m_ps"], 1)
            pe.wait_ge(s["m_sb"], 2)
            for c in range(KC):
                last = pe.matmul(ps[:, 3, c * D:(c + 1) * D], c_t[:, c * P:(c + 1) * P], resp_t,
                                 start=True, stop=True)
            last.then_inc(s["m_ps"], 1)


            n_a = total(pe, 0)
            pe.wait_ge(s["a_out"], apart(pe, (n_a + 1) * (16 * QS)))
            pe.wait_ge(s["vblk_zero"], 1)
            b_step(0, prev=False, back=False)
            b_step(1, back=False)
            with pe.Fori(2, NQ) as i:
                b_step(i)
            b_step(NQ, here=False)

            pe.wait_ge(s["raw_lo"], 3)

            def c_turn(g):
                pe.wait_ge(s["c_x_in"], g * (16 * QS) + 16 * QS)
                turn(xin, xT).then_inc(s["c_xT"], 1)

            c_turn(0)
            for c, (w1, w2, w3) in enumerate(BRANCHES):
                g0, g1 = bounds(pe, 1, c)
                n1 = w[w1][0].shape[2] // P
                with pe.Fori(0, pe.snap(g1 - g0)) as t:
                    g = g0 + t
                    pe.wait_ge(s["c_xl"], g + 1)
                    for f in range(n1):
                        last = hidden(ps[:, 1 + f // 2, (f % 2) * TQ:(f % 2 + 1) * TQ], w[w1], xs, f)
                        if f % 2 == 1:
                            last.then_inc(s[f"c_fc1_{c}"], 1)
                    c_turn(g + 1)
                    src = [hid_h, hid_l]
                    if w3:
                        for f in range(KC):
                            for kc in range(n1):
                                if f == 0 and kc % 2 == 0:
                                    pe.wait_ge(s[f"c_split_{c}"], t * (n1 // 2) + kc // 2 + 1)
                                last = passes(pe, ps[:, 4, f * TQ:(f + 1) * TQ],
                                              [u[:, kc, f * P:(f + 1) * P] for u in w[w2]],
                                              [hid_h[:, kc, :], hid_l[:, kc, :]], kc == 0, kc == n1 - 1)
                        last.then_inc(s["c_fc2"], 1)
                        src = [hid_h[:, 4:6, :], hid_l[:, 4:6, :]]
                        pe.wait_ge(s["c_split2"], t + 1)
                    else:
                        pe.wait_ge(s[f"c_split_{c}"], t * (n1 // 2) + 1)
                    pe.wait_ge(s["c_res"], g)
                    for kc in range(KC):
                        last = tokens_out(o_ps, src, w[w3 or w2], kc, KC)
                    last.then_inc(s["c_out_ps"], 1)
            g0, g1 = bounds(pe, 1, CLS - 1)
            with pe.Fori(g0, g1) as g:
                pe.wait_ge(s["c_xl"], g + 1)
                c_turn(g + 1)

        @block.scalar
        def _(act):
            act.wait_ge(s["wrap_ready"], 1)
            act.activation(wrap, wrap, ACT.Sin).then_inc(s["setup_act"], 1)
            act.wait_ge(s["setup_act"], 1)
            act.activation(wrap, wrap, ACT.Silu).then_inc(s["setup_act"], 1)
            act.wait_ge(s["small_in"], 16 * 11)
            act.activation(safety[:, :], safety[:, :], ACT.Exp, scale=-1.0).then_inc(s["setup_act"], 1)
            def split_stage(n, names, hi_v):
                act.wait_ge(s[f"stage_in_{n % 2}"], stage_dmas(n))
                width = sum(a * b for _, a, b in names)
                act.activation(hi_v, stage[:, n % 2, 0:width], ACT.Copy).then_inc(s["stage_hi"], 1)

            for n, names in enumerate(B_STAGES):
                split_stage(n, names, wb_hi[:, n * STAGE:(n + 1) * STAGE])

            def normalise_out(pre, n, stored):
                act.wait_ge(s[pre + "_out"], stored)
                act.wait_ge(s[pre + "_shift"], n + 1)
                for p in range(PAIRS):
                    last = act.activation(yout[:, p, :], res[:, p, :], ACT.Identity, scale=rstd[:, p:p + 1],
                                          bias=shift[:, p:p + 1])
                last.then_inc(s[pre + "_norm"], 1)

            def a_xhi(g):
                act.wait_ge(s["a_xT"], g + 1)
                act.activation(xh[:, :, :], bank(0, "p (c n) -> p c n", c=KC), ACT.Copy).then_inc(s["a_xh"], 1)

            a_xhi(0)
            with act.Fori(0, E) as e:
                g0, g1 = bounds(act, 0, e)
                act.wait_ge(s["a_w_in"], e * 32 + 32)
                act.wait_ge(s["a_fc1"], g0 * (FC // 2))
                act.activation(wc_hi[:, 0:STAGE], stage[:, 0, :], ACT.Copy).then_inc(s["a_w_hi"], 1)
                act.wait_ge(s["a_fc2"], g0)
                act.activation(wc_hi[:, STAGE:2 * STAGE], stage[:, 1, :], ACT.Copy).then_inc(s["a_w_hi"], 1)
                with act.Fori(g0, g1) as g:
                    for f in range(FC):
                        if f % 2 == 0:
                            act.wait_ge(s["a_fc1"], g * (FC // 2) + f // 2 + 1)
                        last = act.activation(hid[:, f, :], ps[:, 1 + f // 2, (f % 2) * TQ:(f % 2 + 1) * TQ], ACT.Gelu,
                                              bias=cols[:, bass.ds(e * FC + f, 1)])
                        if f % 2 == 1:
                            last.then_inc(s["a_gelu"], 1)
                        if f == 3:
                            act.wait_ge(s["gs_row"], g + 1)
                            act.activation(ps[0:2 * R, 7, 0:D], ps[0:2 * R, 6, 0:D], ACT.Square,
                                           accum_out=gs[:, 0:1]).then_inc(s["gs_norm2"], 1)
                    normalise_out("a", g, g * (16 * QS))
                    a_xhi(g + 1)
            n_a = total(act, 0)
            normalise_out("a", n_a, n_a * (16 * QS))

            act.wait_ge(s["m_ps"], 3)
            act.activation(m_hi[:, :, :], bank(3, "p (c n) -> p c n", c=KC), ACT.Copy).then_inc(s["m_hi_ready"], 1)
            act.wait_ge(s["a_out"], (n_a + 1) * (16 * QS))

            def raw_high(n):
                act.wait_ge(s["raw_in"], 16 * sum(len(names) for names in C_PARTS[:max(n + 1, 2)]))
                act.activation(wc_hi[:, raw_cols[n]], raws[n], ACT.Copy).then_inc(s["raw_hi"], 1)

            raw_high(0)
            raw_high(1)

            def b_act_front(i):
                act.wait_ge(s["b_xT"], i + 1)
                act.activation(xh[:, :, :], bank(7, "p (c n) -> p c n", c=KC), ACT.Copy).then_inc(s["b_xh"], 1)
                act.wait_ge(s["b_qkv"], 2 * i + 1)
                for c in range(KC):
                    for par in range(2):
                        last = act.activation(qm[:, c, par, :], ps[:, 0, c * TQ:(c + 1) * TQ], ACT.Identity,
                                              scale=k("head")[:, par:par + 1], bias=bq_head[:, c, par:par + 1])
                last.then_inc(s["b_q"], 1)
                for c in range(KC):
                    last = act.activation(kt[:, c, :], ps[:, 1, c * TQ:(c + 1) * TQ], ACT.Identity,
                                          bias=col("L1_cond_bk", c))
                last.then_inc(s["b_q"], 1)

            def b_act_exp(i):
                for p in range(PAIRS):
                    act.wait_ge(s["b_sub"], 2 * i + p + 1)
                    act.activation(att[:, p, :], att[:, p, :], ACT.Exp).then_inc(s["b_exp"], 1)

            def b_act_back(i):
                for p in range(PAIRS):
                    act.wait_ge(s["b_pT"], 2 * i + p + 1)
                    act.activation(prob_t[:, p * KC:(p + 1) * KC, :, :],
                                   ps[:, p * KC:(p + 1) * KC, :].rearrange("q c (r n) -> q c r n", r=4),
                                   ACT.Copy).then_inc(s["b_pTs"], 1)

            def b_act_ctx(i):
                act.wait_ge(s["b_ctxT"], i + 1)
                act.activation(ctx_h[:, :, :], bank(5, "p (c n) -> p c n", c=KC), ACT.Copy)\
                    .then_inc(s["b_ctxh"], 1)

            def b_act_ht(i):
                act.wait_ge(s["b_xnT"], i + 1)
                for c in range(KC):
                    last = act.activation(ht[:, c, :], ps[:, 7, c * TQ:(c + 1) * TQ], ACT.Identity,
                                          scale=col("L1_cond_g2", c), bias=col("L1_cond_beta2", c))
                last.then_inc(s["b_ht"], 1)

            def b_act_ffn(i):
                for f in range(FC):
                    if f % 2 == 0:
                        act.wait_ge(s["b_fc1"], i * (FC // 2) + f // 2 + 1)
                    last = act.activation(hid[:, f, :], ps[:, 4 + f // 2 % 2, (f % 2) * TQ:(f % 2 + 1) * TQ],
                                          ACT.Gelu_apprx_sigmoid, bias=col("L1_cond_b1", f))
                    if f % 2 == 1:
                        last.then_inc(s["b_gelu"], 1)

            def b_act_last(i):
                act.wait_ge(s["b_x2T"], i + 1)
                act.activation(xh[:, :, :], bank(7, "p (c n) -> p c n", c=KC), ACT.Copy).then_inc(s["b_x2h"], 1)

            def b_act_gate(i):
                act.wait_ge(s["b_gate1"], i + 1)
                act.activation(gate1[:, :].rearrange("n (b s) -> n b s", b=QS),
                               ps[0:S, 7, 0:QS].rearrange("n (b o) -> n b o", o=1).to_broadcast([S, QS, S]),
                               ACT.Relu, scale=1.0 / S, bias=gb1[:, 0:1]).then_inc(s["b_gate1s"], 1)
                act.wait_ge(s["b_gate2"], i + 1)
                act.activation(expz[:, :], ps[:, 2, 0:PAIRS], ACT.Exp, scale=-1.0, bias=gb2[:, 0:1])\
                    .then_inc(s["b_expz"], 1)

            def b_step(i, here=True, prev=True):
                if here:
                    b_act_front(i)
                if prev:
                    b_act_ht(i - 1)
                    b_act_ffn(i - 1)
                if here:
                    b_act_exp(i)
                    b_act_back(i)
                if prev:
                    b_act_last(i - 1)
                if here:
                    b_act_ctx(i)
                if prev:
                    b_act_gate(i - 1)

            b_step(0, prev=False)
            raw_high(2)
            with act.Fori(1, NQ) as i:
                b_step(i)
            b_step(NQ, here=False)

            def c_xhi(g):
                act.wait_ge(s["c_xT"], g + 1)
                act.activation(xh[:, :, :], bank(0, "p (c n) -> p c n", c=KC), ACT.Copy).then_inc(s["c_xh"], 1)

            c_xhi(0)
            for c, (w1, w2, w3) in enumerate(BRANCHES):
                g0, g1 = bounds(act, 1, c)
                n1 = w[w1][0].shape[2] // P
                b1 = w1.replace("w1", "b1")
                with act.Fori(0, act.snap(g1 - g0)) as t:
                    for f in range(n1):
                        if f % 2 == 0:
                            act.wait_ge(s[f"c_fc1_{c}"], t * (n1 // 2) + f // 2 + 1)
                        last = act.activation(hid[:, f, :], ps[:, 1 + f // 2, (f % 2) * TQ:(f % 2 + 1) * TQ], ACT.Gelu,
                                              bias=col(b1, f))
                        if f % 2 == 1:
                            last.then_inc(s[f"c_gelu_{c}"], 1)
                    c_xhi(g0 + t + 1)
                    if w3:
                        act.wait_ge(s["c_fc2"], t + 1)
                        for f in range(KC):
                            last = act.activation(hid[:, 4 + f, :], ps[:, 4, f * TQ:(f + 1) * TQ], ACT.Gelu,
                                                  bias=col("L3_cond_b2_sr", f))
                        last.then_inc(s["c_gelu2"], 1)
                    normalise_out("c", g0 + t, (g0 + t) * (16 * QS))
            g0, g1 = bounds(act, 1, CLS - 1)
            with act.Fori(g0, g1) as g:
                c_xhi(g + 1)
                normalise_out("c", g, g * (16 * QS))

        @block.vector
        def _(dve):
            done = [0]

            def then(ins):
                done[0] += 1
                ins.then_inc(s["setup_dve"], 1)
                dve.wait_ge(s["setup_dve"], done[0])

            dve.wait_ge(s["const_in"], 16)
            dve.wait_ge(s["idx_in"], 32)
            then(dve.tensor_copy(idxf[:, :], idx[:, :]))
            then(dve.tensor_scalar(idxf[:, 0:1], idxf[:, 0:1], 0.0, float(E - 1), ALU.max, ALU.min))
            for which in range(2):
                hot = onehot[:, which, :]
                then(dve.tensor_scalar(hot, k("class"), idxf[:, which:which + 1], None, ALU.is_equal))
                if which == 1:
                    then(dve.tensor_reduce(slot_of[:, :], hot[:, 0:CLS - 1], X, ALU.add))
                    then(dve.tensor_scalar(hot[:, CLS - 1:CLS], slot_of[:, :], -1.0, 1.0, ALU.mult, ALU.add))
                    then(dve.memset(hot[:, CLS:E], 0.0))
                dve.sem_inc(s["routed_onehot"], 1)
                dve.wait_ge(s["routed_ps"], 2 * which + 1)
                then(dve.tensor_tensor(over, ps[:, 1, 0:E].rearrange("p (e o) -> p e o", o=1).to_broadcast([P, E, NQ]),
                                       k("quads").rearrange("p (o q) -> p o q", o=1).to_broadcast([P, E, NQ]),
                                       ALU.is_gt))
                then(dve.tensor_reduce(quads[:, :], over, X, ALU.add))
                then(dve.tensor_tensor(prior, k("less").rearrange("p (e f) -> p e f", e=E),
                                       quads[:, :].rearrange("p (o f) -> p o f", o=1).to_broadcast([P, E, E]),
                                       ALU.mult))
                then(dve.tensor_reduce(start[:, :], prior, X, ALU.add))
                then(dve.tensor_tensor(end[:, :], start[:, :], quads[:, :], ALU.add))
                then(dve.scalar_tensor_tensor(slot_e[:, :], start[:, :], float(QS), ps[:, 0, 0:E], ALU.mult, ALU.add))
                then(dve.tensor_tensor(slot_e[:, :], slot_e[:, :], hot, ALU.mult))
                then(dve.tensor_reduce(slot_of[:, :], slot_e[:, :], X, ALU.add))
                dve.tensor_scalar(placed, k("slot"), slot_of[:, 0:1], None, ALU.is_equal)\
                    .then_inc(s["routed_placed"], 1)
                dve.tensor_copy(start_i[:, which, :], start[0:1, :])
                dve.tensor_copy(end_i[:, which, :], end[0:1, :])
                dve.wait_ge(s["routed_ps"], 2 * which + 2)
                then(dve.tensor_copy(srow, ps[0:1, 2, 0:A_SLOTS]))
                then(dve.tensor_scalar(sempty, srow, -0.5, None, ALU.is_gt))
                then(dve.tensor_tensor(sempty, sempty, k("slot4")[0:1, :], ALU.mult))
                dve.tensor_scalar(src_i[:, which, :], srow, float(B), float(B - 1), ALU.add, ALU.min)
                dve.tensor_scalar(dst_i[:, which, 0:QS], k("slot")[0:1, 0:QS], float(B), None, ALU.add)
                if which == 0:
                    then(dve.tensor_tensor(ended.rearrange("p (g e) -> p g e", e=E),
                                           k("slot")[0:1, 0:A_TILES + 1].rearrange("p (g o) -> p g o", o=1)
                                           .to_broadcast([1, A_TILES + 1, E]),
                                           end[0:1, :].rearrange("p (o e) -> p o e", o=1)
                                           .to_broadcast([1, A_TILES + 1, E]), ALU.is_gt))
                    then(dve.tensor_reduce(last_f, ended.rearrange("p (g e) -> p g e", e=E), X, ALU.add))
                    then(dve.tensor_scalar(last_e[:, 0, :], last_f, float(E - 1), None, ALU.min))
                dve.scalar_tensor_tensor(dst_i[:, which, QS:], srow, float(B), sempty, ALU.add, ALU.add)\
                    .then_inc(s["route_ready"], 1)

            dve.wait_ge(s["setup_ps"], 1)
            then(dve.tensor_copy(cols[:, :], ps[:, 7, 0:COLS_W]))
            dve.wait_ge(s["setup_ps"], 2)
            dve.tensor_copy(gw1_t[:, :, :], ps[:, 3, 0:KC * S].rearrange("p (c n) -> p c n", c=KC))\
                .then_inc(s["turned"], 1)
            dve.tensor_copy(resp_t, ps[0:R, 5, 0:D]).then_inc(s["turned"], 1)
            for c in range(KC):
                last = dve.tensor_scalar(bq_head[:, c, :], k("head"), col("L1_cond_bq", c), None, ALU.mult)
            last.then_inc(s["turned"], 1)
            dve.wait_ge(s["rows_in"], 16 * (len(ROWS_OF) + len(EROWS)))
            dve.tensor_tensor(resp_bias[:, :], row("L2_cond_resp_b", 1)[:, 0, :], row("L2_cond_safety_bias", 1)[:, 0, :],
                              ALU.add)
            dve.tensor_scalar(gb2[:, :], gb2[:, :], -1.0, None, ALU.mult)
            dve.wait_ge(s["small_in"], 16 * 11)
            then(dve.tensor_copy(tf, tstep[:, :]))
            then(dve.tensor_scalar(tq, tf, 0.01, None, ALU.mult))
            then(dve.scalar_tensor_tensor(tr, tq, -64.0, tf, ALU.mult, ALU.add))
            then(dve.scalar_tensor_tensor(tr, tq, -32.0, tr, ALU.mult, ALU.add))
            then(dve.scalar_tensor_tensor(tr, tq, -4.0, tr, ALU.mult, ALU.add))
            then(dve.scalar_tensor_tensor(tq, tr, 0.01, tq, ALU.mult, ALU.add))
            then(dve.tensor_scalar(tq, tq, 4000.0, None, ALU.mult))
            then(dve.tensor_scalar(ang, tq, k("freq"), None, ALU.mult))
            for half_n, shift in enumerate((0.0, 0.25)):
                n, v = turns[:, half_n, :], wrap[:, half_n, :]
                then(dve.tensor_scalar(n, ang, 0.5 / np.pi, shift, ALU.mult, ALU.add))
                then(dve.tensor_scalar(n, n, ROUNDER, None, ALU.add))
                then(dve.tensor_scalar(n, n, -ROUNDER, None, ALU.add))
                then(dve.scalar_tensor_tensor(v, n, -TURN1, ang, ALU.mult, ALU.add))
                then(dve.scalar_tensor_tensor(v, n, -TURN2, v, ALU.mult, ALU.add))
                then(dve.scalar_tensor_tensor(v, n, -TURN3, v, ALU.mult, ALU.add))
                then(dve.tensor_scalar(v, v, 2 * np.pi * shift, None, ALU.add))
                then(dve.tensor_scalar(v, v, HALF_TURN, -HALF_TURN, ALU.min, ALU.max))
            dve.sem_inc(s["wrap_ready"], 1)
            dve.wait_ge(s["setup_ps"], 4)
            then(dve.tensor_tensor(emb, bank(6), b_ada, ALU.add))
            dve.tensor_scalar(emb[:, 0:D], emb[:, 0:D], 1.0, None, ALU.add).then_inc(s["emb_done"], 1)
            dve.tensor_copy(uvt[:, :], ps[0:2 * R, 4, 0:D]).then_inc(s["turned"], 1)

            dve.wait_ge(s["setup_act"], 3)
            for b2 in range(2):
                then(dve.tensor_scalar(modden[b2 * S:(b2 + 1) * S, :],
                                       safety[b2 * S:(b2 + 1) * S, :].rearrange("p (n b) -> p n b", b=2)[:, :, b2],
                                       1.0, None, ALU.add))

            def split_lo(n, names, lo_v, hi_v):
                dve.wait_ge(s["stage_hi"], n + 1)
                width = sum(a * b for _, a, b in names)
                dve.tensor_tensor(lo_v, stage[:, n % 2, 0:width], hi_v.bitcast(F32), ALU.subtract)\
                    .then_inc(s["stage_lo"], 1)

            for n, names in enumerate(B_STAGES):
                split_lo(n, names, wb_lo[:, n * STAGE:(n + 1) * STAGE], wb_hi[:, n * STAGE:(n + 1) * STAGE])

            def low(out_t, whole, high):
                return dve.tensor_tensor(out_t, whole, high.bitcast(F32), ALU.subtract)

            def split_hidden(j, sem_hi, n_hi, sem_split, at=None):
                f = slice(2 * j, 2 * j + 2) if at is None else slice(at, at + 2)
                dve.tensor_copy(hid_h[:, f, :], hid[:, f, :]).then_inc(sem_hi, 1)
                dve.wait_ge(sem_hi, n_hi)
                low(hid_l[:, f, :], hid[:, f, :], hid_h[:, f, :]).then_inc(sem_split, 1)

            def layer_stats(src, sem_stat, n_stat, sem_var, eps, first=False):
                stats_t, mv_t, vare_t = (stats1, mv1, vare1) if first else (stats, mv, vare)
                for p in range(PAIRS):
                    last = dve.bn_stats(stats_t[:, p, :], src[:, p, :])
                last.then_inc(sem_stat, 1)
                dve.wait_ge(sem_stat, apart(dve, n_stat - 1))
                for p in range(PAIRS):
                    last = dve.bn_aggr(mv_t[:, p, :], stats_t[:, p, :])
                last.then_inc(sem_stat, 1)
                dve.wait_ge(sem_stat, n_stat)
                if src is res:
                    dve.tensor_scalar(neg_mean[:, :], mv_t[:, :, 0], -1.0, None, ALU.mult)
                dve.tensor_scalar(vare_t[:, :], mv_t[:, :, 1], eps, None, ALU.add).then_inc(sem_var, 1)

            xT_ps = bank(0, "p (c n) -> p c n", c=KC)
            o_ps = bank(5, "p (a n) -> p a n", a=PAIRS)

            def a_xlo(g):
                dve.wait_ge(s["a_xh"], g + 1)
                low(xl[:, :, :], xT_ps, xh[:, :, :]).then_inc(s["a_xl"], 1)

            def finish(pre, g, eps, has_product=True):
                dve.wait_ge(s[pre + "_xb"], g + 1 if pre == "c" else g)
                dve.wait_ge(s[pre + "_norm"], g)
                if has_product:
                    if pre == "a":
                        dve.wait_ge(s["a_fc2"], g)
                    else:
                        dve.wait_ge(s["c_out_ps"], g + 1)
                    dve.tensor_tensor(res[:, :, :], o_ps, xb[:, :, :], ALU.add).then_inc(s[pre + "_res"], 1)
                else:
                    dve.tensor_copy(res[:, :, :], xb[:, :, :]).then_inc(s[pre + "_res"], 1)
                dve.wait_ge(s[pre + "_res"], g + 1)
                layer_stats(res, s[pre + "_stat"], 2 * g + 2, s[pre + "_var"], eps)

            def gs_select(i):
                dve.tensor_copy(sel[:, :, :], k("pick")[0:2 * R, :].rearrange("p (a j) -> p a j", a=2)
                                [:, :, bass.ds(i, 1)].to_broadcast([2 * R, 2, R])).then_inc(s["gs_sel"], 1)

            def gs_dot(i):
                dve.wait_ge(s["gs_norm2"], i + 1)
                dve.tensor_tensor_reduce(junk, ps[0:2 * R, 6, 0:D], uvt, 1.0, 0.0, ALU.mult, ALU.add,
                                         gs[:, 1:2]).then_inc(s["gs_dot"], 1)

            def gs_step(i):
                dve.wait_ge(s["gs_norm"], i + 1)
                dve.tensor_scalar(gs[:, 3:4], gs[:, 2:3], 1e-8, None, ALU.add).then_inc(s["gs_chain"], 1)
                dve.wait_ge(s["gs_chain"], 4 * i + 1)
                dve.tensor_tensor(gs[:, 4:5], gs[:, 3:4], gs[:, 3:4], ALU.mult).then_inc(s["gs_chain"], 1)
                dve.wait_ge(s["gs_chain"], 4 * i + 2)
                dve.reciprocal(gs[:, 5:6], gs[:, 4:5]).then_inc(s["gs_chain"], 1)
                dve.wait_ge(s["gs_chain"], 4 * i + 3)
                dve.wait_ge(s["gs_dot"], i + 1)
                dve.scalar_tensor_tensor(gs[:, 6:7], gs[:, 1:2], gs[:, 5:6], k("later")[0:2 * R, bass.ds(i, 1)],
                                         ALU.mult, ALU.mult).then_inc(s["gs_chain"], 1)
                dve.wait_ge(s["gs_chain"], 4 * i + 4)
                dve.scalar_tensor_tensor(uvt, ps[0:2 * R, 6, 0:D], gs[:, 6:7], uvt, ALU.mult, ALU.add)\
                    .then_inc(s["gs_step"], 1)

            def a_weight_lo(e, n):
                dve.wait_ge(s["a_w_hi"], 2 * e + n + 1)
                v = slice(n * STAGE, (n + 1) * STAGE)
                low(wc_lo[:, v], stage[:, n, :], wc_hi[:, v]).then_inc(s["a_w_lo"], 1)

            def a_tile(g):
                dve.wait_ge(s["gs_step"], g)
                gs_select(g)
                finish("a", g, 1e-12)
                for j in range(FC // 2):
                    dve.wait_ge(s["a_gelu"], g * (FC // 2) + j + 1)
                    split_hidden(j, s["a_hi"], g * (FC // 2) + j + 1, s["a_split"])
                    if j == 2:
                        gs_dot(g)
                gs_step(g)
                a_xlo(g + 1)

            dve.memset(bank(5), 0.0).then_inc(s["blank_ps"], 1)
            a_xlo(0)
            dve.wait_ge(s["blank_ps"], 1)
            dve.wait_ge(s["blank_xb"], 1)
            with dve.Fori(0, E) as e:
                g0, g1 = bounds(dve, 0, e)
                a_weight_lo(e, 0)
                a_weight_lo(e, 1)
                with dve.Fori(g0, g1) as g:
                    a_tile(g)
            n_a = total(dve, 0)
            finish("a", n_a, 1e-12)
            dve.wait_ge(s["a_out"], (n_a + 1) * (16 * QS))

            dve.wait_ge(s["gs_step"], n_a)
            then(dve.tensor_tensor_reduce(junk[:, :], uvt[:, :], uvt[:, :], 1.0, 0.0, ALU.mult, ALU.add, gs[:, 0:1]))
            dve.sem_inc(s["gs_dot"], 1)
            dve.wait_ge(s["gs_norm"], n_a + 1)
            then(dve.tensor_scalar(gs[:, 3:4], gs[:, 2:3], 1e-8, None, ALU.add))
            then(dve.reciprocal(gs[:, 4:5], gs[:, 3:4]))
            then(dve.tensor_scalar(uvt[:, :], uvt[:, :], gs[:, 4:5], None, ALU.mult))
            dve.tensor_copy(qv[:, :], uvt[R:2 * R, :]).then_inc(s["gs_done"], 1)

            dve.wait_ge(s["m_ps"], 1)
            dve.tensor_copy(basis_t[:, :, :], ps[:, 1, :].rearrange("p (c n) -> p c n", c=KC)).then_inc(s["m_sb"], 1)
            dve.wait_ge(s["m_ps"], 2)
            dve.tensor_copy(c_t, ps[0:R, 2, 0:D]).then_inc(s["m_sb"], 1)
            dve.wait_ge(s["m_hi_ready"], 1)
            dve.tensor_tensor(m_lo[:, :, :], ps[:, 3, :].rearrange("p (c n) -> p c n", c=KC),
                              m_hi[:, :, :].bitcast(F32), ALU.subtract).then_inc(s["m_ready"], 1)


            dve.memset(vblk, 0.0).then_inc(s["vblk_zero"], 1)
            dve.wait_ge(s["vblk_zero"], 1)
            xT7 = bank(7, "p (c n) -> p c n", c=KC)
            heads = lambda t, n: t.rearrange("q a (h d) -> q a h d", h=n)

            def normalise(dst, src, mean, inverse):
                for p in range(PAIRS):
                    last = dve.tensor_scalar(dst[:, p, :], src[:, p, :], mean[:, p, 0:1], inverse[:, p:p + 1],
                                             ALU.subtract, ALU.mult)
                return last

            def b_ln1_stats(i):
                dve.wait_ge(s["b_x_in"], 16 * i + 16)
                layer_stats(xin, s["b_stat"], 2 * i + 2, s["b_var"], 1e-5, first=True)

            def b_ln1(i, again=True):
                dve.wait_ge(s["b_rstd"], i + 1)
                if again:
                    dve.wait_ge(s["b_xT"], i)
                    dve.wait_ge(s["b_xb"], i)
                normalise(xm, xin, mv1, rstd1).then_inc(s["b_norm"], 1)

            def b_values(i):
                dve.wait_ge(s["b_xh"], i + 1)
                low(xl[:, :, :], xT7, xh[:, :, :]).then_inc(s["b_xl"], 1)
                dve.wait_ge(s["b_qkv"], 2 * i + 2)
                bv = row("L1_cond_bv").rearrange("q a (g h d) -> q a g h d", g=NH // 2, h=2)
                vp = bank(2, "q (a g h d) -> q a g h d", a=PAIRS, g=NH // 2, h=2)
                vb = vblk.rearrange("q a b (g h d) -> q a b g h d", g=NH // 2, h=2)
                for b2 in range(2):
                    for par in range(2):
                        here, to = slice(b2 * S, (b2 + 1) * S), slice(par * S, (par + 1) * S)
                        last = dve.tensor_tensor(vb[to, :, b2, :, par, :], vp[here, :, :, par, :],
                                                 bv[here, :, :, par, :], ALU.add)
                last.then_inc(s["b_v"], 1)

            def b_softmax_in(i):
                dve.wait_ge(s["b_score"], i + 1)
                for p in range(PAIRS):
                    dve.wait_ge(s["b_bias"], 2 * i + p + 1)
                    v = lambda t: t[:, p, :].rearrange("q (c r n) -> q r c n", c=KC, r=4)
                    dve.tensor_tensor(v(att), ps[:, 0:4, p * TQ:(p + 1) * TQ].rearrange("q r (c n) -> q r c n", c=KC),
                                      v(bias), ALU.add).then_inc(s["b_added"], 1)
                    dve.wait_ge(s["b_added"], 2 * i + p + 1)
                    dve.tensor_reduce(amax[:, p, :], att[:, p, :].rearrange("q (h k) -> q h k", h=NH), X, ALU.max)\
                        .then_inc(s["b_max"], 1)

            def b_softmax_sum(i):
                for p in range(PAIRS):
                    dve.wait_ge(s["b_exp"], 2 * i + p + 1)
                    dve.tensor_reduce(asum[:, p, :], att[:, p, :].rearrange("q (h k) -> q h k", h=NH), X, ALU.add)\
                        .then_inc(s["b_sum"], 1)
                    dve.wait_ge(s["b_sum"], 2 * i + p + 1)
                    dve.reciprocal(asum[:, p, :], asum[:, p, :]).then_inc(s["b_rsum"], 1)

            def b_ctx(i):
                dve.wait_ge(s["b_pv"], i + 1)
                dve.wait_ge(s["b_rsum"], 2 * i + 2)
                dve.tensor_tensor(ctxn.rearrange("q a (h d) -> q a h d", h=NH),
                                  bank(4, "q (a h d) -> q a h d", a=PAIRS, h=NH),
                                  asum[:, :, :].rearrange("q a (h o) -> q a h o", o=1)
                                  .to_broadcast([P, PAIRS, NH, HD]), ALU.mult).then_inc(s["b_ctx"], 1)

            def b_ctx_low(i):
                dve.wait_ge(s["b_ctxh"], i + 1)
                low(ctx_l[:, :, :], bank(5, "p (c n) -> p c n", c=KC), ctx_h[:, :, :]).then_inc(s["b_ctxl"], 1)

            def b_ln2(i):
                dve.wait_ge(s["b_wo"], i + 1)
                dve.wait_ge(s["b_xb"], i + 1)
                dve.tensor_tensor(x1[:, :, :], bank(0, "p (a n) -> p a n", a=PAIRS), xb[:, :, :], ALU.add)\
                    .then_inc(s["b_x1"], 1)
                dve.wait_ge(s["b_x1"], i + 1)
                layer_stats(x1, s["b_stat2"], 2 * i + 2, s["b_var2"], 1e-5)
                dve.wait_ge(s["b_rstd2"], i + 1)
                normalise(xn, x1, mv, rstd).then_inc(s["b_xn"], 1)

            def b_ffn_in(i):
                dve.wait_ge(s["b_ht"], i + 1)
                dve.tensor_copy(ht_h[:, :, :], ht[:, :, :]).then_inc(s["b_hth"], 1)
                dve.wait_ge(s["b_hth"], i + 1)
                low(ht_l[:, :, :], ht[:, :, :], ht_h[:, :, :]).then_inc(s["b_htl"], 1)

            def b_ffn(i):
                for j in range(FC // 2):
                    dve.wait_ge(s["b_gelu"], i * (FC // 2) + j + 1)
                    split_hidden(j, s["b_hi"], i * (FC // 2) + j + 1, s["b_split"])

            def b_l2_in(i):
                dve.wait_ge(s["b_fc2"], i + 1)
                dve.wait_ge(s["b_x1b"], i + 1)
                dve.tensor_tensor(x2, bank(6, "p (a n) -> p a n", a=PAIRS), x1b, ALU.add).then_inc(s["b_x2"], 1)

            def b_l2_split(i):
                dve.wait_ge(s["b_x2h"], i + 1)
                low(xl[:, :, :], xT7, xh[:, :, :]).then_inc(s["b_x2l"], 1)
                dve.tensor_reduce(pooled[:, :, :], xT7.rearrange("p c (b s) -> p c b s", b=QS), X, ALU.add)\
                    .then_inc(s["b_pool"], 1)

            def b_l2_out(i):
                dve.wait_ge(s["b_resp"], i + 1)
                dve.wait_ge(s["b_out"], 16 * i)
                dve.tensor_tensor(yout[:, :, :], bank(1, "p (a n) -> p a n", a=PAIRS),
                                  resp_bias[:, :].rearrange("p (o d) -> p o d", o=1).to_broadcast([P, PAIRS, D]),
                                  ALU.add).then_inc(s["b_corr"], 1)
                dve.wait_ge(s["b_expz"], i + 1)
                dve.scalar_tensor_tensor(den[:, :], expz[:, :], 1.0, modden[:, bass.ds(i * PAIRS, PAIRS)],
                                         ALU.add, ALU.mult).then_inc(s["b_strength"], 1)
                dve.wait_ge(s["b_strength"], 2 * i + 1)
                dve.reciprocal(strength[:, :], den[:, :]).then_inc(s["b_strength"], 1)
                dve.wait_ge(s["b_strength"], 2 * i + 2)
                dve.wait_ge(s["b_corr"], i + 1)
                for p in range(PAIRS):
                    last = dve.scalar_tensor_tensor(yout[:, p, :], yout[:, p, :], strength[:, p:p + 1], x2[:, p, :],
                                                    ALU.mult, ALU.add)
                last.then_inc(s["b_x3"], 1)

            def b_step(i, here=True, prev=True, after=True):
                if here:
                    b_values(i)
                if prev:
                    b_ffn_in(i - 1)
                if here:
                    b_softmax_in(i)
                if after:
                    b_ln1_stats(i + 1)
                if prev:
                    b_ffn(i - 1)
                if after:
                    b_ln1(i + 1)
                if here:
                    b_softmax_sum(i)
                if prev:
                    b_l2_in(i - 1)
                if here:
                    b_ctx(i)
                if prev:
                    b_l2_split(i - 1)
                if here:
                    b_ctx_low(i)
                    b_ln2(i)
                if prev:
                    b_l2_out(i - 1)

            def raw_low(n):
                dve.wait_ge(s["raw_hi"], n + 1)
                low(wc_lo[:, raw_cols[n]], raws[n], wc_hi[:, raw_cols[n]]).then_inc(s["raw_lo"], 1)

            raw_low(0)
            raw_low(1)
            b_ln1_stats(0)
            b_ln1(0, again=False)
            b_step(0, prev=False)
            raw_low(2)
            with dve.Fori(1, NQ - 1) as i:
                b_step(i)
            b_step(NQ - 1, after=False)
            b_step(NQ, here=False, after=False)

            def c_xlo(g):
                dve.wait_ge(s["c_xh"], g + 1)
                low(xl[:, :, :], xT_ps, xh[:, :, :]).then_inc(s["c_xl"], 1)

            c_xlo(0)
            for c, (w1, w2, w3) in enumerate(BRANCHES):
                g0, g1 = bounds(dve, 1, c)
                n1 = w[w1][0].shape[2] // P
                with dve.Fori(0, dve.snap(g1 - g0)) as t:
                    g = g0 + t
                    for j in range(n1 // 2):
                        dve.wait_ge(s[f"c_gelu_{c}"], t * (n1 // 2) + j + 1)
                        split_hidden(j, s[f"c_hi_{c}"], t * (n1 // 2) + j + 1, s[f"c_split_{c}"])
                    c_xlo(g + 1)
                    if w3:
                        dve.wait_ge(s["c_gelu2"], t + 1)
                        split_hidden(0, s["c_hi2"], t + 1, s["c_split2"], at=4)
                    finish("c", g, 1e-5)
            g0, g1 = bounds(dve, 1, CLS - 1)
            with dve.Fori(g0, g1) as g:
                c_xlo(g + 1)
                finish("c", g, 1e-5, has_product=False)

        @block.gpsimd
        def _(pool):
            pool.memset(minus_half[:, :], -0.5).then_inc(s["half_ready"], 1)
            pool.memset(half[:, :], 0.5).then_inc(s["half_ready"], 1)
            pool.memset(masked[:, :, :], MASKED).then_inc(s["half_ready"], 1)
            pool.wait_ge(s["half_ready"], 3)
            def inverse_root(sem_var, n, sem_rstd, first=False):
                pool.wait_ge(sem_var, n)
                to, of = (rstd1, vare1) if first else (rstd, vare)
                pool.tensor_tensor(to[:, :], of[:, :], minus_half[:, :], ALU.pow).then_inc(sem_rstd, 1)

            def finish(pre, n, gain, offset, between=None):
                inverse_root(s[pre + "_var"], n + 1, s[pre + "_rstd"])
                pool.wait_ge(s[pre + "_rstd"], n + 1)
                pool.tensor_tensor(shift[:, :], neg_mean[:, :], rstd[:, :], ALU.mult).then_inc(s[pre + "_shift"], 1)
                if between:
                    between()
                pool.wait_ge(s[pre + "_norm"], n + 1)
                pool.tensor_tensor(yout[:, :, :], yout[:, :, :], gain, ALU.mult).then_inc(s[pre + "_gain"], 1)
                pool.wait_ge(s[pre + "_gain"], n + 1)
                pool.tensor_tensor(yout[:, :, :], yout[:, :, :], offset, ALU.add).then_inc(s[pre + "_y"], 1)

            def a_weights(e):
                pool.wait_ge(s["a_w_lo"], 2 * e)
                pool.dma_start(stage[:, 0, :].rearrange("p (k n) -> p k n", k=KC),
                               inp["L0_cond_Wi"][bass.ds(e, 1)].rearrange("a (k p) n -> p (a k) n", p=P))\
                    .then_inc(s["a_w_in"], 16)
                pool.dma_start(stage[:, 1, :].rearrange("p (k n) -> p k n", k=FC),
                               inp["L0_cond_Wo"][bass.ds(e, 1)].rearrange("a (k p) n -> p (a k) n", p=P))\
                    .then_inc(s["a_w_in"], 16)

            def a_finish(n, between=None):
                e = pool.value_load(last_e[0:1, 0, bass.ds(n, 1)], min_val=0, max_val=E - 1)
                finish("a", n, erows[:, 1, bass.ds(e, 1), :].to_broadcast([P, PAIRS, D]),
                       erows[:, 2, bass.ds(e, 1), :].to_broadcast([P, PAIRS, D]), between)

            def a_tiles(e):
                g0, g1 = bounds(pool, 0, e)
                with pool.Fori(g0, g1) as g:
                    pool.wait_ge(s["a_x_in"], g * (16 * QS) + 16 * QS)
                    pool.wait_ge(s["a_res"], g + 1)
                    pool.tensor_tensor(xb[:, :, :], xin[:, :, :],
                                       erows[:, 0, bass.ds(e, 1), :].to_broadcast([P, PAIRS, D]), ALU.add)\
                        .then_inc(s["a_xb"], 1)

                    def gs_norm():
                        pool.wait_ge(s["gs_norm2"], g + 1)
                        pool.tensor_tensor(gs[:, 2:3], gs[:, 0:1], half[0:2 * R, :], ALU.pow)\
                            .then_inc(s["gs_norm"], 1)
                    a_finish(g, gs_norm)

            pool.wait_ge(s["rows_in"], 16 * (len(ROWS_OF) + len(EROWS)))
            pool.wait_ge(s["turned"], 4)
            pool.memset(xb[:, :, :], 0.0).then_inc(s["blank_xb"], 1)
            pool.wait_ge(s["stage_lo"], len(B_STAGES))
            pool.wait_ge(s["route_ready"], 2)
            a_weights(0)
            with pool.Fori(0, E - 1) as e:
                a_weights(e + 1)
                a_tiles(e)
            a_tiles(E - 1)
            n_a = total(pool, 0)
            a_finish(n_a)
            pool.wait_ge(s["gs_dot"], n_a + 1)
            pool.tensor_tensor(gs[:, 2:3], gs[:, 0:1], half[0:2 * R, :], ALU.pow).then_inc(s["gs_norm"], 1)

            pool.wait_ge(s["a_out"], apart(pool, (n_a + 1) * (16 * QS)))
            pool.wait_ge(s["mask_in"], 32)

            def b_masks(i):
                pool.tensor_copy(maskf[:, :, :], mask8[:, bass.ds(i * PAIRS, PAIRS), :]).then_inc(s["b_mask"], 1)
                pool.wait_ge(s["b_mask"], 2 * i + 1)
                pool.tensor_tensor(maskf[:, :, :], maskf[:, :, :], masked[:, :, :].to_broadcast([P, PAIRS, S]),
                                   ALU.mult).then_inc(s["b_mask"], 1)
                pool.wait_ge(s["b_mask"], 2 * i + 2)
                pool.wait_ge(s["b_bias_in"], i * (16 * QS) + 16 * QS)
                for p in range(PAIRS):
                    v = bias[:, p, :].rearrange("q (h k) -> q h k", h=NH)
                    pool.tensor_tensor(v, v, maskf[:, p:p + 1, :].to_broadcast([P, NH, S]), ALU.add)\
                        .then_inc(s["b_bias"], 1)

            def b_modulate(i):
                inverse_root(s["b_var"], i + 1, s["b_rstd"], first=True)
                pool.wait_ge(s["b_norm"], i + 1)
                pool.wait_ge(s["b_ada_in"], i * (16 * QS) + 16 * QS)
                pool.tensor_tensor(xm[:, :, :], xm[:, :, :], ada[:, :, 0:D], ALU.mult).then_inc(s["b_scaled"], 1)
                pool.wait_ge(s["b_scaled"], i + 1)
                pool.tensor_tensor(xm[:, :, :], xm[:, :, :], ada[:, :, D:2 * D], ALU.add).then_inc(s["b_xm"], 1)

            def b_base1(i):
                pool.wait_ge(s["b_xm"], i + 1)
                pool.tensor_tensor(xb[:, :, :], xm[:, :, :], row("L1_cond_bo"), ALU.add).then_inc(s["b_xb"], 1)

            def b_subtract(i):
                for p in range(PAIRS):
                    pool.wait_ge(s["b_max"], 2 * i + p + 1)
                    v = att[:, p, :].rearrange("q (h k) -> q h k", h=NH)
                    pool.tensor_tensor(v, v, amax[:, p, :].rearrange("q (h o) -> q h o", o=1).to_broadcast([P, NH, S]),
                                       ALU.subtract).then_inc(s["b_sub"], 1)

            def b_base2(i):
                inverse_root(s["b_var2"], i + 1, s["b_rstd2"])
                pool.wait_ge(s["b_x1"], i + 1)
                pool.tensor_tensor(x1b, x1[:, :, :], row("L1_cond_b2"), ALU.add).then_inc(s["b_x1b"], 1)

            def b_step(i, after=True):
                b_subtract(i)
                if after:
                    b_modulate(i + 1)
                    b_masks(i + 1)
                b_base2(i)
                if after:
                    b_base1(i + 1)

            b_modulate(0)
            b_masks(0)
            b_base1(0)
            with pool.Fori(0, NQ - 1) as i:
                b_step(i)
            b_step(NQ - 1, after=False)

            def c_tile(g, bias_row):
                pool.wait_ge(s["c_x_in"], apart(pool, g * (16 * QS) + 16 * QS))
                pool.wait_ge(s["c_res"], g)
                if bias_row is None:
                    pool.tensor_copy(xb[:, :, :], xin[:, :, :]).then_inc(s["c_xb"], 1)
                else:
                    pool.tensor_tensor(xb[:, :, :], xin[:, :, :], bias_row, ALU.add).then_inc(s["c_xb"], 1)
                finish("c", g, row("L3_cond_gamma"), row("L3_cond_beta"))

            for c in range(CLS):
                g0, g1 = bounds(pool, 1, c)
                with pool.Fori(g0, g1) as g:
                    c_tile(g, row(OUT_BIAS[c]) if c < len(OUT_BIAS) else None)


def kernel(**inputs):
    import concourse.bacc as bacc
    from concourse.bass_utils import run_bass_kernel_spmd

    nc = bacc.Bacc("TRN2", target_bir_lowering=False, num_devices=1)
    arrays, aps = {}, {}
    for name, a in inputs.items():
        a = np.ascontiguousarray(a)
        arrays[name] = a
        aps[name] = nc.dram_tensor(name, a.shape, mybir.dt.from_np(a.dtype), kind="ExternalInput").ap()
    arrays["const"] = constants()
    const = nc.dram_tensor("const", (P, CONST_W), F32, kind="ExternalInput").ap()
    out = nc.dram_tensor("out", (ROWS, S, D), F32, kind="ExternalOutput").ap()
    build(nc, aps, const, out)
    r = run_bass_kernel_spmd(nc, [arrays], core_ids=[0])
    return r.results[0]["out"][:B]
```

```python
from contextlib import ExitStack

import numpy as np

import concourse.bass as bass
from concourse import mybir

F32 = mybir.dt.float32
F32R = mybir.dt.float32r
I32 = mybir.dt.int32
U8 = mybir.dt.uint8
ACT = mybir.ActivationFunctionType
ALU = mybir.AluOpType
X = mybir.AxisListType.X

P = 128
B, S, D = 128, 64, 256
E, FF = 8, 1024
NH, HD = 16, 16
R = 32
QS = 4
PAIRS = QS * S // P
TQ = QS * S
KC = D // P
FC = FF // P
NQ = B // QS
CLS = 4
A_TILES = NQ + E
C_TILES = NQ + CLS
A_SLOTS = QS * (A_TILES + 2)
C_SLOTS = QS * (C_TILES + 3)
ROWS = B + QS
MASKED = -1e30

CONST = {}
_n = 0
for _name, _w in (("ident", P), ("before", P), ("ones", P), ("slot", A_SLOTS), ("slot4", A_SLOTS),
                  ("quads", NQ), ("class", E), ("less", E * E), ("freq", 1), ("head", 2), ("sample", 1),
                  ("later", A_TILES), ("pick", 2 * A_TILES)):
    CONST[_name] = (_n, _n + _w)
    _n += _w
CONST_W = _n

COLS = {}
_n = 0
for _name, _w in (("L0_cond_bi", E * FC), ("L1_cond_bq", KC), ("L1_cond_bk", KC), ("L1_cond_b1", FC),
                  ("L1_cond_g2", KC), ("L1_cond_beta2", KC), ("L3_cond_b1_nr", KC), ("L3_cond_b1_tsr", KC),
                  ("L3_cond_b1_sr", 2 * KC), ("L3_cond_b2_sr", KC)):
    COLS[_name] = (_n, _n + _w)
    _n += _w
COLS_W = _n

ROWS_OF = {}
_n = 0
for _name, _w in (("L1_cond_bv", 1),
                  ("L1_cond_bo", 1), ("L1_cond_b2", 1), ("L2_cond_resp_b", 1), ("L2_cond_safety_bias", 1),
                  ("L3_cond_b2_nr", 1), ("L3_cond_b2_tsr", 1), ("L3_cond_b3_sr", 1), ("none", 1), ("L3_cond_gamma", 1),
                  ("L3_cond_beta", 1)):
    ROWS_OF[_name] = (_n, _n + _w)
    _n += _w
ROWS_W = _n

EROWS = ("L0_cond_bo", "L0_cond_gamma", "L0_cond_beta")
WB = (("L1_cond_Wq", KC, D), ("L1_cond_Wk", KC, D), ("L1_cond_Wv", KC, D), ("L1_cond_Wo", KC, D),
      ("L1_cond_W1", KC, FF), ("L1_cond_W2", FC, D))
WC = (("L3_cond_w1_nr", KC, D), ("L3_cond_w2_nr", KC, D), ("L3_cond_w1_tsr", KC, D), ("L3_cond_w2_tsr", KC, D),
      ("L3_cond_w1_sr", KC, 2 * D), ("L3_cond_w2_sr", 2 * KC, D), ("L3_cond_w3_sr", KC, D))
STAGE = 2048
WB_COLS = sum(a * b for _, a, b in WB)
WC_COLS = sum(a * b for _, a, b in WC)
PIECE = WB_COLS // NQ
RAW = WC_COLS // 3
BRANCHES = (("L3_cond_w1_nr", "L3_cond_w2_nr", None), ("L3_cond_w1_tsr", "L3_cond_w2_tsr", None),
            ("L3_cond_w1_sr", "L3_cond_w2_sr", "L3_cond_w3_sr"))
OUT_BIAS = ("L3_cond_b2_nr", "L3_cond_b2_tsr", "L3_cond_b3_sr")
HALF_TURN = float(np.nextafter(np.float32(np.pi), np.float32(0)))
TURN1 = 6.28125
TURN2 = float(np.float32(round((2 * np.pi - TURN1) * 2 ** 20) / 2 ** 20))
TURN3 = 2 * np.pi - TURN1 - TURN2
ROUNDER = 1.5 * 2 ** 23


def constants():
    c = np.zeros((P, CONST_W), np.float32)

    def put(name, a):
        c[:, CONST[name][0]:CONST[name][1]] = a

    i = np.arange(P)
    put("ident", np.eye(P))
    put("before", i[:, None] < i[None, :])
    put("ones", 1.0)
    put("slot", np.arange(A_SLOTS))
    put("slot4", np.arange(A_SLOTS) % QS)
    put("quads", [-1.0] + [QS * j for j in range(1, NQ)])
    put("class", np.arange(E))
    put("less", (np.arange(E)[None, :] < np.arange(E)[:, None]).reshape(1, -1))
    put("freq", np.exp(np.arange(P, dtype=np.float32) * np.float32(-np.log(10000.0) / (P - 1)))[:, None])
    put("head", np.stack([(i // HD) % 2 == 0, (i // HD) % 2 == 1], 1))
    put("sample", (i - B)[:, None])
    step = np.arange(A_TILES)
    put("later", np.where(((i % R)[:, None] > step[None, :]) & (step < R), -1.0, 0.0))
    put("pick", np.concatenate([(i[:, None] == a * R + step[None, :]) & (step < R) for a in range(2)], 1))
    return c


def build(nc, inp, const, out):
    ctx = ExitStack()
    with ctx:
        def sb(name, shape, dt=F32):
            return ctx.enter_context(nc.sbuf_tensor(name, shape, dt))

        def sem(name):
            return ctx.enter_context(nc.semaphore(name))

        x_rows = inp["x"]
        l0_out = nc.dram_tensor("l0_out", (QS + A_SLOTS, S, D), F32, kind="Internal").ap()
        l2_out = nc.dram_tensor("l2_out", (C_SLOTS, S, D), F32, kind="Internal").ap()
        emb_dram = nc.dram_tensor("emb_dram", (B, 2 * D), F32, kind="Internal").ap()

        cst = sb("cst", [P, CONST_W])
        idx = sb("idx", [P, 2], I32)
        idxf = sb("idxf", [P, 2])
        cols = sb("cols", [P, COLS_W])
        rows = sb("rows", [P, ROWS_W, D])
        resp_bias = sb("resp_bias", [P, D])
        bk_head = sb("bk_head", [P, KC, 2])
        bq = sb("bq", [P, KC])

        def k(name):
            return cst[:, CONST[name][0]:CONST[name][1]]

        def col(name, j):
            c0 = COLS[name][0] + j
            return cols[:, c0:c0 + 1]

        def row(name, rep=PAIRS):
            r0 = ROWS_OF[name][0]
            return rows[:, r0:r0 + 1, :].to_broadcast([P, rep, D])

        ident = k("ident")

        onehot = sb("onehot", [P, 2, E])
        quads = sb("quads", [P, E])
        start = sb("start", [P, E])
        end = sb("end", [P, E])
        slot_e = sb("slot_e", [P, E])
        slot_of = sb("slot_of", [P, 1])
        start_i = sb("start_i", [1, 2, E], I32)
        end_i = sb("end_i", [1, 2, E], I32)
        src_i = sb("src_i", [1, 1, A_SLOTS], I32)
        dst_i = sb("dst_i", [1, 1, QS + C_SLOTS], I32)
        slot_i = sb("slot_i", [1, 2, B], I32)
        piece_i = sb("piece_i", [1, 1, A_TILES + 1], I32)
        last_of = sb("last_of", [1, 2, A_TILES + 1], I32)

        wb_hi = sb("wb_hi", [P, sum(a * b for _, a, b in WB)], F32R)
        wb_lo = sb("wb_lo", [P, sum(a * b for _, a, b in WB)], F32R)
        wc_hi = sb("wc_hi", [P, sum(a * b for _, a, b in WC)], F32R)
        wc_lo = sb("wc_lo", [P, sum(a * b for _, a, b in WC)], F32R)
        stage = sb("stage", [P, 2, STAGE])
        m_hi = sb("m_hi", [P, KC, D], F32R)
        m_lo = sb("m_lo", [P, KC, D], F32R)

        def views(parts, hi, lo):
            v, n = {}, 0
            for name, a, b in parts:
                v[name] = [t[:, n:n + a * b].rearrange("p (k n) -> p k n", k=a) for t in (hi, lo)]
                n += a * b
            return v

        w = {**views(WB, wb_hi, wb_lo), **views(WC, wc_hi, wc_lo)}
        wi = [t[:, 0:STAGE].rearrange("p (k n) -> p k n", k=KC) for t in (wc_hi, wc_lo)]
        wo = [t[:, STAGE:2 * STAGE].rearrange("p (k n) -> p k n", k=FC) for t in (wc_hi, wc_lo)]

        xin = sb("xin", [P, PAIRS, D])
        xb = sb("xb", [P, PAIRS, D])
        xh = sb("xh", [P, KC, TQ], F32R)
        xl = sb("xl", [P, KC, TQ], F32R)
        hid = sb("hid", [P, FC, TQ])
        hid_h = sb("hid_h", [P, FC, TQ], F32R)
        hid_l = sb("hid_l", [P, FC, TQ], F32R)
        res = sb("res", [P, PAIRS, D])
        stats = sb("stats", [P, PAIRS, 6])
        mv = sb("mv", [P, PAIRS, 2])
        vare = sb("vare", [P, PAIRS])
        rstd = sb("rstd", [P, PAIRS])
        neg_mean = sb("neg_mean", [P, PAIRS])
        shift = sb("shift", [P, PAIRS])
        stats1 = sb("stats1", [P, PAIRS, 6])
        mv1 = sb("mv1", [P, PAIRS, 2])
        vare1 = sb("vare1", [P, PAIRS])
        rstd1 = sb("rstd1", [P, PAIRS])
        minus_half = sb("minus_half", [P, PAIRS])
        half = sb("half", [P, 1])
        masked = sb("masked", [P, 1, 1])
        yout = sb("yout", [P, PAIRS, D])

        shared = sb("shared", [P, 3 * E * D])
        erows = shared[:, :].rearrange("p (w e d) -> p w e d", w=3, e=E)
        at = [0]

        def part(n):
            at[0] += n
            return shared[:, at[0] - n:at[0]]

        prob_t = part(4 * PAIRS * KC * P).rearrange("p (n r q) -> p n r q", r=4, q=P)
        km = part(KC * 2 * TQ).rearrange("p (c h t) -> p c h t", c=KC, h=2)
        qt = part(KC * TQ).rearrange("p (c t) -> p c t", c=KC)
        vblk = part(PAIRS * 2 * D).rearrange("p (a b d) -> p a b d", a=PAIRS, b=2)
        x1b = part(PAIRS * D).rearrange("p (a d) -> p a d", a=PAIRS)
        xn = part(PAIRS * D).rearrange("p (a d) -> p a d", a=PAIRS)
        x2 = part(PAIRS * D).rearrange("p (a d) -> p a d", a=PAIRS)
        x1 = res
        ctxn = xn

        ada = sb("ada", [P, PAIRS, 2 * D])
        xm = sb("xm", [P, PAIRS, D])
        mask8 = sb("mask8", [P, B // 2, S], U8)
        maskf = sb("maskf", [P, PAIRS, S])
        bias = stage[:, 0, :].rearrange("p (a n) -> p a n", a=PAIRS)
        att = stage[:, 1, :].rearrange("p (a n) -> p a n", a=PAIRS)
        amax = sb("amax", [P, PAIRS, NH])
        asum = sb("asum", [P, PAIRS, NH])
        ctx_h = sb("ctx_h", [P, KC, TQ], F32R)
        ctx_l = sb("ctx_l", [P, KC, TQ], F32R)
        ht = sb("ht", [P, KC, TQ])
        ht_h = sb("ht_h", [P, KC, TQ], F32R)
        ht_l = sb("ht_l", [P, KC, TQ], F32R)
        pooled = sb("pooled", [P, KC, QS])
        gate1 = sb("gate1", [S, TQ])
        expz = sb("expz", [P, PAIRS])
        den = sb("den", [P, PAIRS])
        strength = sb("strength", [P, PAIRS])

        xb_ring = ada
        x_ring = stage[:, :, 0:PAIRS * D]
        y_ring = stage[:, :, PAIRS * D:2 * PAIRS * D]
        zeros = maskf

        hflat = hid[:, :, :].rearrange("p f t -> p (f t)")
        over = hflat[:, 0:E * NQ].rearrange("p (e q) -> p e q", e=E)
        prior = hflat[:, 256:256 + E * E].rearrange("p (e f) -> p e f", e=E)
        placed = hflat[:, 320:320 + A_SLOTS]
        ended = yout[0:1, :, :].rearrange("p a d -> p (a d)")[:, 0:E * (A_TILES + 1)]
        last_f = yout[0:1, :, :].rearrange("p a d -> p (a d)")[:, E * (A_TILES + 1):(E + 1) * (A_TILES + 1)]
        srow = hflat[0:1, 512:512 + A_SLOTS]
        sempty = hflat[0:1, 704:704 + A_SLOTS]
        tstep = hflat[:, 1920:1920 + P].bitcast(I32)
        tf, tq, tr = (hflat[:, 896 + n * P:896 + (n + 1) * P] for n in range(3))
        ang = hflat[:, 1280:1408]
        turns = hflat[:, 1408:1664].rearrange("p (a n) -> p a n", a=2)
        wrap = hflat[:, 1664:1920].rearrange("p (a n) -> p a n", a=2)
        w_ada = ada
        piece = ada[:, :, :].rearrange("p a d -> p (a d)")[:, 0:PIECE]
        b_ada = xm[:, :, :].rearrange("p a d -> p (a d)")
        emb = ht[:, :, :].rearrange("p a d -> p (a d)")
        uv = sb("uv", [P, KC, 2 * R])
        uvt = xm[0:2 * R, 0, :]
        sel = sb("sel", [2 * R, 2, R])
        junk = xm[0:2 * R, 1, :]
        qv = ht[0:R, 0, :]
        c_t = ht[0:R, 1, :]
        basis_t = xm
        cols_in = res[0:COLS_W, 0, 0:P]
        resp_in = res[:, 1, 0:KC * R].rearrange("p (c r) -> p c r", c=KC)
        resp_t = gate1[0:R, :]
        gs = sb("gs", [2 * R, 8])
        gw1_in = xb[0:S, 0, :]
        gw1_t = sb("gw1_t", [P, KC, S])
        gw2_t = sb("gw2_t", [S, 1])
        gb1 = sb("gb1", [S, 1])
        gb2 = sb("gb2", [P, 1])
        safety = res[:, 1, P:2 * P]
        modden = sb("modden", [P, B // 2])

        ps = ctx.enter_context(nc.psum_tensor("ps", [P, 8, 512], F32))

        def bank(n, shape=None, **kw):
            return ps[:, n, :] if shape is None else ps[:, n, :].rearrange(shape, **kw)

        names = """const_in idx_in rows_in small_in
            mask_in setup_dve setup_act routed routed_ps route_ready
            turned half_ready
            wrap_ready emb_done emb_out
            gs_sel gs_row gs_norm2 gs_dot gs_norm gs_step gs_done
            m_ps m_sb m_hi_ready m_ready vblk_zero
            a_w_in a_w_hi a_w_lo a_x_in a_xT a_xh a_xl a_xb a_fc1 a_gelu a_hi a_split a_fc2 a_res a_stat a_var
            a_rstd a_shift a_norm a_gain a_y a_out blank_xb blank_ps
            raw_in raw_hi raw_lo c_blank c_filled b_w_in b_w_hi b_w_lo a_w_last a_w_mid c_x
            b_x_in b_ada_in b_bias_in b_bias b_mask b_stat b_var b_rstd b_norm b_scaled b_xm b_xb b_xT b_xh b_xl
            b_qkv b_q b_v b_score b_added b_max b_sub b_exp b_sum b_rsum b_ctx b_ctxT b_pT b_pTs b_pv b_ctxh b_ctxl
            b_wo b_x1 b_stat2 b_var2 b_rstd2 b_xn b_x1b b_xnT b_hth b_ht b_htl b_fc1 b_gelu b_hi b_split b_fc2
            b_x2 b_x2T b_x2h b_x2l b_pool b_gate1 b_gate1s b_gate2 b_expz b_strength b_resp b_corr b_x3 b_out
            c_x_in c_xT c_xh c_xl c_xb c_out_ps c_res c_stat c_var c_rstd c_shift c_norm c_gain c_y c_out gs_chain setup_ps""".split()
        sems = {}
        for n in names:
            sems[n] = sem(n)
        for c in range(len(BRANCHES)):
            for n in ("fc1", "gelu", "hi", "split"):
                sems[f"c_{n}_{c}"] = sem(f"c_{n}_{c}")
        for n in ("fc2", "gelu2", "hi2", "split2"):
            sems[f"c_{n}"] = sem(f"c_{n}")
        s = sems
        block = ctx.enter_context(nc.Block())
        hid_flat = hid[:, :, :].rearrange("p f t -> p (f t)")
        raw_cols = [slice(n * RAW, (n + 1) * RAW) for n in range(3)]
        raws = [hid_flat[:, 0:RAW], stage[:, 1, 0:RAW], hid_flat[:, 0:RAW]]

        def apart(eng, value):
            value = eng.to_reg(value)
            eng.wait_ge(s["const_in"], 16)
            return value

        def passes(pe, o, lhs, rhs, first, last):
            pe.matmul(o, lhs[0], rhs[0], start=first, stop=False)
            pe.matmul(o, lhs[0], rhs[1], start=False, stop=False)
            return pe.matmul(o, lhs[1], rhs[0], start=False, stop=last)

        def w_piece(n):
            staged = stage[:, n // 2, :].rearrange("p (k n) -> p k n", k=(KC, FC)[n // 2])
            if n < 2:
                v = (slice(None), slice(None), slice(n * FF // 2, (n + 1) * FF // 2))
            else:
                v = (slice(None), slice((n - 2) * FC // 2, (n - 1) * FC // 2))
            hi, lo = (wi, wo)[n // 2]
            return hi[v], lo[v], staged[v]

        def bounds(eng, which, e):
            tiles = A_TILES if which == 0 else C_TILES
            a = eng.value_load(start_i[0:1, which, bass.ds(e, 1)], min_val=0, max_val=tiles - 1)
            z = eng.value_load(end_i[0:1, which, bass.ds(e, 1)], min_val=1, max_val=tiles)
            return a, z

        def total(eng, which):
            last = (E if which == 0 else CLS) - 1
            return eng.value_load(end_i[0:1, which, last:last + 1], min_val=NQ,
                                  max_val=A_TILES if which == 0 else C_TILES)

        def c_load(eng, g):
            eng.dma_start(x_ring[:, bass.ds(g % 2, 1), :].rearrange("p o (a d) -> p (o a) d", a=PAIRS),
                          l2_out[bass.ds(g * QS, QS)].rearrange("(a b) s d -> (b s) a d", b=2))\
                .then_inc(s["c_x_in"], 16)

        def c_next(eng, g):
            eng.wait_ge(s["c_x_in"], apart(eng, g * 16))
            eng.wait_ge(s["c_x"], g - 1)
            eng.wait_ge(s["c_xb"], g - 1)
            c_load(eng, g)

        @block.sync
        def _(sp):
            sp.dma_start(cst[:, :], const).then_inc(s["const_in"], 16)
            sp.dma_start(idx[:, 0:1], inp["itok_B_0_7"].rearrange("(b o) -> b o", o=1)).then_inc(s["idx_in"], 16)
            sp.dma_start(idx[:, 1:2], inp["itok_B_0_2"].rearrange("(b o) -> b o", o=1)).then_inc(s["idx_in"], 16)
            sp.dma_start(cols_in, inp["cols_packed"]).then_inc(s["idx_in"], 16)
            sp.dma_start(uv[:, :, 0:R], inp["L2_cond_U"].rearrange("(c p) r -> p c r", p=P)).then_inc(s["small_in"], 16)
            sp.dma_start(uv[:, :, R:2 * R], inp["L2_cond_V"].rearrange("(c p) r -> p c r", p=P)).then_inc(s["small_in"], 16)
            sp.dma_start(tstep[:, :], inp["itok_B_34_63"].partition_broadcast(P)).then_inc(s["small_in"], 16)
            sp.dma_start(w_ada[:, :, :], inp["L1_cond_W_ada"].rearrange("(c p) n -> p c n", p=P)).then_inc(s["small_in"], 16)
            sp.dma_start(b_ada, inp["L1_cond_b_ada"].partition_broadcast(P)).then_inc(s["small_in"], 16)
            sp.dma_start(resp_in[:, :, :], inp["L2_cond_resp_w"].rearrange("(c p) r -> p c r", p=P)).then_inc(s["small_in"], 16)
            sp.dma_start(gw1_in, inp["L2_cond_gate_w1"]).then_inc(s["small_in"], 16)
            sp.dma_start(gw2_t[:, :], inp["L2_cond_gate_w2"].rearrange("o n -> n o")).then_inc(s["small_in"], 16)
            sp.dma_start(gb1[:, :], inp["L2_cond_gate_b1"].rearrange("(n o) -> n o", o=1)).then_inc(s["small_in"], 16)
            sp.dma_start(gb2[:, :], inp["L2_cond_gate_b2"].partition_broadcast(P)).then_inc(s["small_in"], 16)
            sp.dma_start(safety, inp["condB_safetyscore"].partition_broadcast(P)).then_inc(s["small_in"], 16)
            sp.dma_start(rows[:, :, :], inp["rows_packed"].partition_broadcast(P)).then_inc(s["rows_in"], 16)
            for n in range(len(EROWS)):
                sp.dma_start(erows[:, n, :, :], inp["erows_packed"][n].partition_broadcast(P)).then_inc(s["rows_in"], 16)

            def slots(table, which, first, limit):
                return [sp.value_load(table[0:1, which, bass.ds(first + j, 1)], min_val=0, max_val=limit)
                        for j in range(QS)]

            def load_quad(src, of, sem_in):
                for j, n in enumerate(src):
                    sp.dma_start(xin[(j % 2) * S:(j % 2 + 1) * S, j // 2, :],
                                 of[bass.ds(n, 1)].rearrange("a s d -> (a s) d")).then_inc(sem_in, 16)

            def store_quad(dst, src, to, sem_out):
                for j, n in enumerate(dst):
                    sp.dma_start(to[bass.ds(n, 1)].rearrange("a s d -> (a s) d"),
                                 src[(j % 2) * S:(j % 2 + 1) * S, j // 2, :]).then_inc(sem_out, 16)

            def a_next(g):
                src = slots(src_i, 0, g * QS + QS, B - 1)
                sp.wait_ge(s["a_xT"], g + 1)
                sp.wait_ge(s["a_xb"], g + 1)
                load_quad(src, x_rows, s["a_x_in"])

            def a_store(g):
                sp.wait_ge(s["a_y"], g + 1)
                sp.dma_start(l0_out[bass.ds(g * QS, QS)].rearrange("(a b) s d -> (b s) a d", b=2), yout[:, :, :])\
                    .then_inc(s["a_out"], 16)

            sp.dma_start(stage[:, 0, :].rearrange("p (k n) -> p k n", k=KC),
                         inp["L0_cond_Wi"][0].rearrange("(k p) n -> p k n", p=P)).then_inc(s["a_w_in"], 16)
            sp.dma_start(stage[:, 1, :].rearrange("p (k n) -> p k n", k=FC),
                         inp["L0_cond_Wo"][0].rearrange("(k p) n -> p k n", p=P)).then_inc(s["a_w_in"], 16)

            sp.wait_ge(s["route_ready"], 1)
            load_quad(slots(src_i, 0, 0, B - 1), x_rows, s["a_x_in"])
            for b2 in range(2):
                sp.dma_start(mask8[b2 * S:(b2 + 1) * S, :, :],
                             inp["mask_Bx1xSxS_bk0"].rearrange("(n b) o q k -> b q (n o) k", b=2)[b2])\
                    .then_inc(s["mask_in"], 16)
            sp.wait_ge(s["emb_done"], 1)
            sp.dma_start(emb_dram, emb).then_inc(s["emb_out"], 16)
            sp.wait_ge(s["route_ready"], 2)
            ends = [sp.value_load(end_i[0:1, 1, c:c + 1], min_val=1, max_val=C_TILES) for c in range(CLS)]
            for q in [n - 1 for n in ends] + [ends[-1] + j for j in range(3)]:
                sp.dma_start(l2_out[bass.ds(q * QS, QS)].rearrange("(a b) s d -> (b s) a d", b=2),
                             cst[:, 0:PAIRS * D].rearrange("p (a d) -> p a d", a=PAIRS)).then_inc(s["c_filled"], 16)

            def piece_in(g):
                n = sp.value_load(piece_i[0:1, 0, bass.ds(g, 1)], min_val=0, max_val=NQ - 1)
                sp.wait_ge(s["b_w_lo"], g)
                sp.dma_start(piece, inp["wb"][:, bass.ds(n * PIECE, PIECE)]).then_inc(s["b_w_in"], 16)

            def a_weights(e):
                sp.dma_start(stage[:, 0, :].rearrange("p (k n) -> p k n", k=KC),
                             inp["L0_cond_Wi"][bass.ds(e, 1)].rearrange("a (k p) n -> p (a k) n", p=P))\
                    .then_inc(s["a_w_in"], 16)
                sp.dma_start(stage[:, 1, :].rearrange("p (k n) -> p k n", k=FC),
                             inp["L0_cond_Wo"][bass.ds(e, 1)].rearrange("a (k p) n -> p (a k) n", p=P))\
                    .then_inc(s["a_w_in"], 16)

            def a_tiles(e):
                g0, g1 = bounds(sp, 0, e)
                with sp.Fori(g0, g1) as g:
                    piece_in(g + 1)
                    a_store(g)
                    a_next(g + 1)

            sp.wait_ge(s["route_ready"], 3)
            piece_in(0)
            a_next(0)
            with sp.Fori(0, E - 1) as e:
                sp.wait_ge(s["a_w_lo"], e * 2 + 2)
                sp.wait_ge(s["a_w_last"], e * 2 + 2)
                a_weights(e + 1)
                a_tiles(e)
            a_tiles(E - 1)
            n_a = total(sp, 0)

            def b_load_bias(i):
                for p in range(PAIRS):
                    for b2 in range(2):
                        sp.dma_start(bias[b2 * S:(b2 + 1) * S, p, :].rearrange("q (h k) -> q h k", h=NH),
                                     inp["fside_Bx16xSxS_0"][bass.ds(i * QS + 2 * p + b2, 1)]
                                     .rearrange("a h q k -> q (a h) k")).then_inc(s["b_bias_in"], 16)

            sp.wait_ge(s["a_w_lo"], 2 * E)
            sp.wait_ge(s["a_w_last"], 2 * E)

            def load_raw(n):
                sp.dma_start(raws[n], inp["wc"][:, n * RAW:(n + 1) * RAW]).then_inc(s["raw_in"], 16)

            load_raw(1)
            sp.wait_ge(s["a_split"], apart(sp, n_a * (FC // 2)))
            load_raw(0)
            a_store(n_a)

            first = slots(slot_i, 0, 0, A_SLOTS - 1)
            sp.wait_ge(s["a_out"], apart(sp, (n_a + 1) * 16))
            sp.wait_ge(s["emb_out"], 16)
            sp.wait_ge(s["a_x_in"], apart(sp, (n_a + 2) * (16 * QS)))

            def b_load(i, src):
                load_quad([n + QS for n in src], l0_out, s["b_x_in"])
                for p in range(PAIRS):
                    for b2 in range(2):
                        sp.dma_start(ada[b2 * S:(b2 + 1) * S, p, :],
                                     emb_dram[bass.ds(i * QS + 2 * p + b2, 1), :].to_broadcast([S, 2 * D]))\
                            .then_inc(s["b_ada_in"], 16)

            def b_store(i):
                dst = slots(slot_i, 1, i * QS, C_SLOTS - 1)
                sp.wait_ge(s["b_x3"], i + 1)
                store_quad(dst, yout, l2_out, s["b_out"])

            def b_step(i, loads=2, stores=True):
                if loads >= 1:
                    sp.wait_ge(s["b_added"], 2 * i + 2)
                    b_load_bias(i + 1)
                if loads >= 2:
                    src = slots(slot_i, 0, (i + 2) * QS, A_SLOTS - 1)
                    sp.wait_ge(s["b_xm"], i + 2)
                    b_load(i + 2, src)
                if stores:
                    b_store(i - 2)

            b_load(0, first)
            b_load_bias(0)
            src = slots(slot_i, 0, QS, A_SLOTS - 1)
            sp.wait_ge(s["c_filled"], 16 * (CLS + 3))
            sp.wait_ge(s["b_xm"], 1)
            b_load(1, src)
            sp.wait_ge(s["raw_lo"], 1)
            load_raw(2)
            b_step(0, stores=False)
            b_step(1, stores=False)
            with sp.Fori(2, NQ - 2) as i:
                b_step(i)
            b_step(NQ - 2, loads=1)
            b_step(NQ - 1, loads=0)
            b_store(NQ - 2)
            b_store(NQ - 1)

            sp.wait_ge(s["b_out"], NQ * (16 * QS))

            def c_store(g):
                dst = slots(dst_i, 0, g * QS, ROWS - 1)
                sp.wait_ge(s["c_out"], apart(sp, g * (16 * QS)))
                sp.wait_ge(s["c_y"], g + 1)
                store_quad(dst, y_ring[:, bass.ds(g % 2, 1), :].rearrange("p o (a d) -> p (o a) d", a=PAIRS),
                           out, s["c_out"])

            c_load(sp, 0)
            sp.wait_ge(s["c_x_in"], 16)
            c_load(sp, 1)
            n_c = total(sp, 1)
            c_next(sp, 2)
            with sp.Fori(0, n_c) as g:
                c_store(g)
            c_store(n_c)
            sp.wait_ge(s["c_x_in"], apart(sp, (n_c + 3) * 16))
            sp.wait_ge(s["c_out"], apart(sp, (n_c + 1) * (16 * QS)))

        @block.tensor
        def _(pe):
            pe.wait_ge(s["const_in"], 16)
            pe.wait_ge(s["idx_in"], 48)
            pe.transpose(ps[:, 7, 0:COLS_W], cols_in[:, :], ident[0:COLS_W, 0:COLS_W]).then_inc(s["setup_ps"], 1)

            for which in range(2):
                pe.wait_ge(s["routed"], 2 * which + 1)
                pe.matmul(ps[:, 0, 0:E], k("before"), onehot[:, which, :], start=True, stop=True)
                pe.matmul(ps[:, 1, 0:E], k("ones"), onehot[:, which, :], start=True, stop=True)\
                    .then_inc(s["routed_ps"], 1)
                pe.wait_ge(s["routed"], 2 * which + 2)
                pe.matmul(ps[0:1, 2, 0:A_SLOTS], k("sample"), placed, start=True, stop=True)
                pe.matmul(ps[0:1, 6, 0:B], slot_of[:, :], ident, start=True, stop=True)\
                    .then_inc(s["routed_ps"], 1)

            pe.wait_ge(s["small_in"], 16 * 11)
            for c in range(KC):
                pe.transpose(ps[:, 3, c * S:(c + 1) * S], gw1_in[:, c * P:(c + 1) * P], ident[0:S, 0:S])
            for c in range(KC):
                last = pe.transpose(ps[0:R, 5, c * P:(c + 1) * P], resp_in[:, c, :], ident)
            last.then_inc(s["setup_ps"], 1)
            for c in range(KC):
                last = pe.transpose(ps[0:2 * R, 4, c * P:(c + 1) * P], uv[:, c, :], ident)
            last.then_inc(s["setup_ps"], 1)

            pe.wait_ge(s["setup_act"], 2)
            for c in range(KC):
                last = pe.matmul(bank(6), wrap[:, c, :], w_ada[:, c, :], start=(c == 0), stop=(c == KC - 1))
            last.then_inc(s["setup_ps"], 1)

            def turn(src, dst):
                for p in range(PAIRS):
                    for c in range(KC):
                        last = pe.transpose(dst[:, c, p * P:(p + 1) * P], src[:, p, c * P:(c + 1) * P], ident)
                return last

            def hidden(o, wt, xs, f):
                n = len(xs)
                for c in range(n):
                    last = passes(pe, o, [t[:, c, f * P:(f + 1) * P] for t in wt], xs[c], c == 0, c == n - 1)
                return last

            def tokens_out(o, xs, wt, c, n):
                for p in range(PAIRS):
                    last = passes(pe, o[:, p, :], [t[:, c, p * P:(p + 1) * P] for t in xs],
                                  [t[:, c, :] for t in wt], c == 0 and p == 0, c == n - 1 and p == PAIRS - 1)
                return last

            xs = [[xh[:, c, :], xl[:, c, :]] for c in range(KC)]
            xT = bank(0, "p (c n) -> p c n", c=KC)

            def a_turn(g):
                pe.wait_ge(s["a_x_in"], g * (16 * QS) + 16 * QS)
                turn(xin, xT).then_inc(s["a_xT"], 1)

            o_ps = bank(5, "p (a n) -> p a n", a=PAIRS)
            a_turn(0)
            pe.wait_ge(s["blank_ps"], 1)
            with pe.Fori(0, E) as e:
                g0, g1 = bounds(pe, 0, e)
                with pe.Fori(g0, g1) as g:
                    pe.wait_ge(s["a_xl"], g + 1)
                    for f in range(FC):
                        if f % (FC // 2) == 0:
                            pe.wait_ge(s["a_w_lo"], 2 * e + f // (FC // 2) + 1)
                        last = hidden(ps[:, 1 + f // 2, (f % 2) * TQ:(f % 2 + 1) * TQ], wi, xs, f)
                        if f % 2 == 1:
                            last.then_inc(s["a_fc1"], 1)
                        if f == 3:
                            pe.wait_ge(s["gs_sel"], apart(pe, g + 1))
                            pe.matmul(ps[0:2 * R, 6, 0:D], sel[:, :, :], uvt[:, :], start=True, stop=True)\
                                .then_inc(s["gs_row"], 1)
                    pe.wait_ge(s["a_res"], g + 1)
                    for c in range(FC):
                        if c % (FC // 2) == 0:
                            pe.wait_ge(s["a_w_last"], 2 * e + c // (FC // 2) + 1)
                        if c % 2 == 0:
                            pe.wait_ge(s["a_split"], g * (FC // 2) + c // 2 + 1)
                        last = tokens_out(o_ps, [hid_h, hid_l], wo, c, FC)
                        if c == 3:
                            a_turn(g + 1)
                    last.then_inc(s["a_fc2"], 1)

            scores = ps[:, 0:4, :]
            q_ps, k_ps, v_ps = bank(0, "p (c n) -> p c n", c=KC), bank(1, "p (c n) -> p c n", c=KC), \
                bank(2, "p (a n) -> p a n", a=PAIRS)
            xT7 = bank(7, "p (c n) -> p c n", c=KC)
            pv_ps = bank(4, "p (a n) -> p a n", a=PAIRS)
            ctx_ps = bank(5, "p (c n) -> p c n", c=KC)
            xT4 = bank(4, "p (c n) -> p c n", c=KC)
            wo_ps = bank(3, "p (a n) -> p a n", a=PAIRS)
            y_ps = bank(6, "p (a n) -> p a n", a=PAIRS)
            r_ps = bank(6, "p (a n) -> p a n", a=PAIRS)

            def b_turn_x(i):
                pe.wait_ge(s["b_xm"], i + 1)
                turn(xm, xT4).then_inc(s["b_xT"], 1)

            def b_qkv(i):
                pe.wait_ge(s["b_xl"], i + 1)
                for f in range(KC):
                    last = hidden(k_ps[:, f, :], w["L1_cond_Wk"], xs, f)
                last.then_inc(s["b_qkv"], 1)
                for f in range(KC):
                    last = hidden(q_ps[:, f, :], w["L1_cond_Wq"], xs, f)
                last.then_inc(s["b_qkv"], 1)
                for c in range(KC):
                    last = tokens_out(v_ps, [xh, xl], w["L1_cond_Wv"], c, KC)
                last.then_inc(s["b_qkv"], 1)

            def b_turn_ffn(i):
                pe.wait_ge(s["b_xn"], i + 1)
                turn(xn, xT7).then_inc(s["b_xnT"], 1)

            def b_l2(i, c):
                pe.wait_ge(s["b_x2l"], i + 1)
                last = tokens_out(r_ps, [hid_h, hid_l], [m_hi, m_lo], c, KC)
                if c == KC - 1:
                    last.then_inc(s["b_resp"], 1)

            def b_scores(i, l2=True):
                if l2:
                    b_l2(i - 2, 0)
                pe.wait_ge(s["b_q"], 2 * i + 2)
                pe.wait_ge(s["b_v"], i + 1)
                for p in range(PAIRS):
                    if p == 1 and l2:
                        b_l2(i - 2, 1)
                    for c in range(KC):
                        for b2 in range(2):
                            t0 = p * P + b2 * S
                            for r in range(4):
                                n = p * 4 + c * 2
                                last = pe.matmul(
                                    scores[b2 * S:(b2 + 1) * S, r, n * S:(n + 2) * S]
                                    .rearrange("q (h k) -> q h k", h=2),
                                    qt[r * 32:(r + 1) * 32, c, t0:t0 + S],
                                    km[r * 32:(r + 1) * 32, c, :, t0:t0 + S], start=True, stop=True)
                last.then_inc(s["b_score"], 1)

            def b_ffn(i):
                pe.wait_ge(s["b_htl"], i + 1)
                pe.wait_ge(s["b_expz"], i)
                for f in range(FC):
                    if f % 2 == 0 and f >= 4:
                        pe.wait_ge(s["b_gelu"], i * (FC // 2) + f // 2 - 1)
                    last = hidden(ps[:, 4 + f // 2 % 2, (f % 2) * TQ:(f % 2 + 1) * TQ], w["L1_cond_W1"],
                                  [[ht_h[:, c, :], ht_l[:, c, :]] for c in range(KC)], f)
                    if f % 2 == 1:
                        last.then_inc(s["b_fc1"], 1)
                pe.wait_ge(s["b_corr"], i)
                for c in range(FC):
                    if c % 2 == 0:
                        pe.wait_ge(s["b_split"], i * (FC // 2) + c // 2 + 1)
                    last = tokens_out(y_ps, [hid_h, hid_l], w["L1_cond_W2"], c, FC)
                last.then_inc(s["b_fc2"], 1)

            def b_values(i):
                pe.wait_ge(s["b_added"], 2 * i + 2)
                for p in range(PAIRS):
                    pe.wait_ge(s["b_exp"], 2 * i + p + 1)
                    for c in range(KC):
                        for r in range(4):
                            last = pe.transpose(ps[:, p * KC + c, r * P:(r + 1) * P],
                                                att[:, p, (c * 4 + r) * P:(c * 4 + r + 1) * P], ident)
                    last.then_inc(s["b_pT"], 1)
                for p in range(PAIRS):
                    pe.wait_ge(s["b_pTs"], 2 * i + p + 1)
                    for c in range(KC):
                        for b2 in range(2):
                            for r in range(4):
                                cols_of = slice(c * P + r * 32, c * P + (r + 1) * 32)
                                last = pe.matmul(pv_ps[b2 * S:(b2 + 1) * S, p, cols_of],
                                                 prob_t[:, p * KC + c, r, b2 * S:(b2 + 1) * S],
                                                 vblk[:, p, b2, cols_of], start=True, stop=True)
                last.then_inc(s["b_pv"], 1)

            def b_turn_ctx(i):
                pe.wait_ge(s["b_ctx"], i + 1)
                turn(ctxn, ctx_ps).then_inc(s["b_ctxT"], 1)

            def b_turn_l2(i):
                pe.wait_ge(s["b_x2"], i + 1)
                turn(x2, xT7).then_inc(s["b_x2T"], 1)

            def b_wo(i):
                pe.wait_ge(s["b_ctxl"], i + 1)
                for c in range(KC):
                    last = tokens_out(wo_ps, [ctx_h, ctx_l], w["L1_cond_Wo"], c, KC)
                last.then_inc(s["b_wo"], 1)

            def b_gate1(i):
                pe.wait_ge(s["b_pool"], i + 1)
                for c in range(KC):
                    last = pe.matmul(ps[0:S, 7, 0:QS], gw1_t[:, c, :], pooled[:, c, :],
                                     start=(c == 0), stop=(c == KC - 1))
                last.then_inc(s["b_gate1"], 1)

            def b_gate2(i):
                pe.wait_ge(s["b_gate1s"], i + 1)
                for p in range(PAIRS):
                    last = pe.matmul(ps[:, 5, p:p + 1], gate1[:, p * P:(p + 1) * P], gw2_t[:, :],
                                     start=True, stop=True)
                last.then_inc(s["b_gate2"], 1)

            def b_step(i, here=True, prev=True, before=True, after=True):
                if prev:
                    b_turn_ffn(i - 1)
                if here:
                    b_scores(i, before)
                elif before:
                    for c in range(KC):
                        b_l2(i - 2, c)
                if prev:
                    b_ffn(i - 1)
                if here:
                    b_values(i)
                if prev:
                    b_turn_l2(i - 1)
                if here:
                    b_turn_ctx(i)
                if after:
                    b_turn_x(i + 1)
                if here:
                    b_wo(i)
                if prev:
                    b_gate1(i - 1)
                if after:
                    b_qkv(i + 1)
                if prev:
                    b_gate2(i - 1)

            pe.wait_ge(s["gs_done"], 1)
            for c in range(KC):
                last = pe.matmul(ps[:, 1, c * D:(c + 1) * D], qv[:, c * P:(c + 1) * P], uvt[0:R, :],
                                 start=True, stop=True)
            last.then_inc(s["m_ps"], 1)
            pe.wait_ge(s["m_sb"], 1)
            for c in range(KC):
                last = pe.matmul(ps[0:R, 2, 0:D], basis_t[:, c, 0:R], basis_t[:, c, :],
                                 start=(c == 0), stop=(c == KC - 1))
            last.then_inc(s["m_ps"], 1)
            pe.wait_ge(s["m_sb"], 2)
            for c in range(KC):
                last = pe.matmul(ps[:, 3, c * D:(c + 1) * D], c_t[:, c * P:(c + 1) * P], resp_t,
                                 start=True, stop=True)
            last.then_inc(s["m_ps"], 1)

            n_a = total(pe, 0)
            pe.wait_ge(s["a_out"], apart(pe, (n_a + 1) * 16))
            pe.wait_ge(s["b_w_lo"], apart(pe, n_a))
            pe.wait_ge(s["vblk_zero"], 1)
            b_turn_x(0)
            b_qkv(0)
            b_step(0, prev=False, before=False)
            b_step(1, before=False)
            with pe.Fori(2, NQ - 1) as i:
                b_step(i)
            b_step(NQ - 1, after=False)
            b_step(NQ, here=False, after=False)
            for c in range(KC):
                b_l2(NQ - 1, c)

            pe.wait_ge(s["raw_lo"], 3)

            def c_turn(g):
                pe.wait_ge(s["c_x"], g + 1)
                turn(xin, xT).then_inc(s["c_xT"], 1)

            c_turn(0)
            pe.wait_ge(s["c_blank"], 3)
            for c, (w1, w2, w3) in enumerate(BRANCHES):
                g0, g1 = bounds(pe, 1, c)
                n1 = w[w1][0].shape[2] // P
                with pe.Fori(0, pe.snap(g1 - g0)) as t:
                    g = g0 + t
                    pe.wait_ge(s["c_xl"], g + 1)
                    for f in range(n1):
                        last = hidden(ps[:, 1 + f // 2, (f % 2) * TQ:(f % 2 + 1) * TQ], w[w1], xs, f)
                        if f % 2 == 1:
                            last.then_inc(s[f"c_fc1_{c}"], 1)
                    c_turn(g + 1)
                    src = [hid_h, hid_l]
                    if w3:
                        for f in range(KC):
                            for kc in range(n1):
                                if f == 0 and kc % 2 == 0:
                                    pe.wait_ge(s[f"c_split_{c}"], t * (n1 // 2) + kc // 2 + 1)
                                last = passes(pe, ps[:, 4, f * TQ:(f + 1) * TQ],
                                              [u[:, kc, f * P:(f + 1) * P] for u in w[w2]],
                                              [hid_h[:, kc, :], hid_l[:, kc, :]], kc == 0, kc == n1 - 1)
                        last.then_inc(s["c_fc2"], 1)
                        src = [hid_h[:, 4:6, :], hid_l[:, 4:6, :]]
                        pe.wait_ge(s["c_split2"], t + 1)
                    else:
                        pe.wait_ge(s[f"c_split_{c}"], t * (n1 // 2) + 1)
                    pe.wait_ge(s["c_res"], g + 1)
                    for kc in range(KC):
                        last = tokens_out(o_ps, src, w[w3 or w2], kc, KC)
                    last.then_inc(s["c_out_ps"], 1)
            g0, g1 = bounds(pe, 1, CLS - 1)
            with pe.Fori(g0, g1) as g:
                pe.wait_ge(s["c_xl"], g + 1)
                c_turn(g + 1)
                pe.wait_ge(s["c_res"], g + 1)
                pe.matmul(bank(5), zeros[:, :, :], hid[:, 0:2, :], start=True, stop=True).then_inc(s["c_out_ps"], 1)

        @block.scalar
        def _(act):
            act.wait_ge(s["wrap_ready"], 1)
            act.activation(wrap, wrap, ACT.Sin).then_inc(s["setup_act"], 1)
            act.wait_ge(s["setup_act"], 1)
            act.activation(wrap, wrap, ACT.Silu).then_inc(s["setup_act"], 1)
            act.wait_ge(s["small_in"], 16 * 11)
            act.activation(safety, safety, ACT.Exp, scale=-1.0).then_inc(s["setup_act"], 1)

            def normalise_out(pre, n, stored):
                act.wait_ge(s["a_out" if pre == "a" else "c_y"], stored)
                act.wait_ge(s[pre + "_shift"], n + 1)
                for p in range(PAIRS):
                    last = act.activation(yout[:, p, :], res[:, p, :], ACT.Identity, scale=rstd[:, p:p + 1],
                                          bias=shift[:, p:p + 1])
                last.then_inc(s[pre + "_norm"], 1)

            def a_xhi(g):
                act.wait_ge(s["a_xT"], g + 1)
                act.activation(xh[:, :, :], bank(0, "p (c n) -> p c n", c=KC), ACT.Copy).then_inc(s["a_xh"], 1)

            a_xhi(0)
            with act.Fori(0, E) as e:
                g0, g1 = bounds(act, 0, e)
                act.wait_ge(s["a_w_in"], e * 32 + 32)
                act.wait_ge(s["a_fc2"], g0)
                for n in (2, 3):
                    hi, _, staged = w_piece(n)
                    act.activation(hi, staged, ACT.Copy).then_inc(s["a_w_mid"], 1)
                with act.Fori(g0, g1) as g:
                    for f in range(FC):
                        if f % 2 == 0:
                            act.wait_ge(s["a_fc1"], g * (FC // 2) + f // 2 + 1)
                        last = act.activation(hid[:, f, :], ps[:, 1 + f // 2, (f % 2) * TQ:(f % 2 + 1) * TQ], ACT.Gelu,
                                              bias=cols[:, bass.ds(e * FC + f, 1)])
                        if f % 2 == 1:
                            last.then_inc(s["a_gelu"], 1)
                        if f == 3:
                            act.wait_ge(s["gs_row"], g + 1)
                            act.activation(ps[0:2 * R, 7, 0:D], ps[0:2 * R, 6, 0:D], ACT.Square,
                                           accum_out=gs[:, 0:1]).then_inc(s["gs_norm2"], 1)
                    normalise_out("a", g, g * 16)
                    a_xhi(g + 1)
            n_a = total(act, 0)
            normalise_out("a", n_a, n_a * 16)

            act.wait_ge(s["m_ps"], 3)
            act.activation(m_hi[:, :, :], bank(3, "p (c n) -> p c n", c=KC), ACT.Copy).then_inc(s["m_hi_ready"], 1)

            def raw_high(n):
                act.wait_ge(s["raw_in"], 16 * max(n + 1, 2))
                act.activation(wc_hi[:, raw_cols[n]], raws[n], ACT.Copy).then_inc(s["raw_hi"], 1)

            act.wait_ge(s["a_out"], (n_a + 1) * 16)

            def b_act_front(i):
                act.wait_ge(s["b_xT"], i + 1)
                act.activation(xh[:, :, :], bank(4, "p (c n) -> p c n", c=KC), ACT.Copy).then_inc(s["b_xh"], 1)

            def b_act_qk(i):
                act.wait_ge(s["b_qkv"], 3 * i + 1)
                for c in range(KC):
                    for par in range(2):
                        last = act.activation(km[:, c, par, :], ps[:, 1, c * TQ:(c + 1) * TQ], ACT.Identity,
                                              scale=k("head")[:, par:par + 1], bias=bk_head[:, c, par:par + 1])
                last.then_inc(s["b_q"], 1)
                act.wait_ge(s["b_qkv"], 3 * i + 2)
                for c in range(KC):
                    last = act.activation(qt[:, c, :], ps[:, 0, c * TQ:(c + 1) * TQ], ACT.Identity,
                                          scale=HD ** -0.5, bias=bq[:, c:c + 1])
                last.then_inc(s["b_q"], 1)

            def b_act_exp(i):
                for p in range(PAIRS):
                    act.wait_ge(s["b_sub"], 2 * i + p + 1)
                    act.activation(att[:, p, :], att[:, p, :], ACT.Exp).then_inc(s["b_exp"], 1)

            def b_act_back(i):
                for p in range(PAIRS):
                    act.wait_ge(s["b_pT"], 2 * i + p + 1)
                    act.activation(prob_t[:, p * KC:(p + 1) * KC, :, :],
                                   ps[:, p * KC:(p + 1) * KC, :].rearrange("q c (r n) -> q c r n", r=4),
                                   ACT.Copy).then_inc(s["b_pTs"], 1)

            def b_act_ctx(i):
                act.wait_ge(s["b_ctxT"], i + 1)
                act.activation(ctx_h[:, :, :], bank(5, "p (c n) -> p c n", c=KC), ACT.Copy)\
                    .then_inc(s["b_ctxh"], 1)

            def b_act_ht(i):
                act.wait_ge(s["b_xnT"], i + 1)
                for c in range(KC):
                    last = act.activation(ht[:, c, :], ps[:, 7, c * TQ:(c + 1) * TQ], ACT.Identity,
                                          scale=col("L1_cond_g2", c), bias=col("L1_cond_beta2", c))
                last.then_inc(s["b_ht"], 1)

            def b_act_ffn(i):
                for f in range(FC):
                    if f % 2 == 0:
                        act.wait_ge(s["b_fc1"], i * (FC // 2) + f // 2 + 1)
                    last = act.activation(hid[:, f, :], ps[:, 4 + f // 2 % 2, (f % 2) * TQ:(f % 2 + 1) * TQ],
                                          ACT.Gelu_apprx_sigmoid, bias=col("L1_cond_b1", f))
                    if f % 2 == 1:
                        last.then_inc(s["b_gelu"], 1)

            def b_act_last(i):
                act.wait_ge(s["b_x2T"], i + 1)
                act.activation(hid_h[:, 0:KC, :], bank(7, "p (c n) -> p c n", c=KC), ACT.Copy)\
                    .then_inc(s["b_x2h"], 1)

            def b_act_gate(i):
                act.wait_ge(s["b_gate1"], i + 1)
                act.activation(gate1[:, :].rearrange("n (b s) -> n b s", b=QS),
                               ps[0:S, 7, 0:QS].rearrange("n (b o) -> n b o", o=1).to_broadcast([S, QS, S]),
                               ACT.Relu, scale=1.0 / S, bias=gb1[:, 0:1]).then_inc(s["b_gate1s"], 1)

            def b_act_gate2(i):
                act.wait_ge(s["b_gate2"], i + 1)
                act.activation(expz[:, :], ps[:, 5, 0:PAIRS], ACT.Exp, scale=-1.0, bias=gb2[:, 0:1])\
                    .then_inc(s["b_expz"], 1)

            def b_step(i, here=True, prev=True, after=True):
                if prev:
                    b_act_ht(i - 1)
                    b_act_ffn(i - 1)
                if here:
                    b_act_exp(i)
                    b_act_back(i)
                if prev:
                    b_act_last(i - 1)
                if here:
                    b_act_ctx(i)
                if after:
                    b_act_front(i + 1)
                if prev:
                    b_act_gate(i - 1)
                if after:
                    b_act_qk(i + 1)
                if prev:
                    b_act_gate2(i - 1)

            b_act_front(0)
            raw_high(0)
            raw_high(1)
            b_act_qk(0)
            b_step(0, prev=False)
            raw_high(2)
            with act.Fori(1, NQ - 1) as i:
                b_step(i)
            b_step(NQ - 1, after=False)
            b_step(NQ, here=False, after=False)

            def c_xhi(g):
                act.wait_ge(s["c_xT"], g + 1)
                act.activation(xh[:, :, :], bank(0, "p (c n) -> p c n", c=KC), ACT.Copy).then_inc(s["c_xh"], 1)

            c_xhi(0)
            for c, (w1, w2, w3) in enumerate(BRANCHES):
                g0, g1 = bounds(act, 1, c)
                n1 = w[w1][0].shape[2] // P
                b1 = w1.replace("w1", "b1")
                with act.Fori(0, act.snap(g1 - g0)) as t:
                    for f in range(n1):
                        if f % 2 == 0:
                            act.wait_ge(s[f"c_fc1_{c}"], t * (n1 // 2) + f // 2 + 1)
                        last = act.activation(hid[:, f, :], ps[:, 1 + f // 2, (f % 2) * TQ:(f % 2 + 1) * TQ], ACT.Gelu,
                                              bias=col(b1, f))
                        if f % 2 == 1:
                            last.then_inc(s[f"c_gelu_{c}"], 1)
                    c_xhi(g0 + t + 1)
                    normalise_out("c", g0 + t, g0 + t)
                    c_next(act, nc.s_assert_within(g0 + t + 3, 3, C_TILES + 2,
                           skip_runtime_bounds_check_because="g0 + t is below the class's end"))
                    if w3:
                        act.wait_ge(s["c_fc2"], t + 1)
                        for f in range(KC):
                            last = act.activation(hid[:, 4 + f, :], ps[:, 4, f * TQ:(f + 1) * TQ], ACT.Gelu,
                                                  bias=col("L3_cond_b2_sr", f))
                        last.then_inc(s["c_gelu2"], 1)
            g0, g1 = bounds(act, 1, CLS - 1)
            with act.Fori(g0, g1) as g:
                c_xhi(g + 1)
                normalise_out("c", g, g)
                c_next(act, g + 3)
            normalise_out("c", g1, g1)

        @block.vector
        def _(dve):
            done = [0]

            def then(ins):
                done[0] += 1
                ins.then_inc(s["setup_dve"], 1)
                dve.wait_ge(s["setup_dve"], done[0])

            dve.wait_ge(s["const_in"], 16)
            dve.wait_ge(s["idx_in"], 48)
            then(dve.tensor_copy(idxf[:, :], idx[:, :]))
            then(dve.tensor_scalar(idxf[:, 0:1], idxf[:, 0:1], 0.0, float(E - 1), ALU.max, ALU.min))
            for which in range(2):
                hot = onehot[:, which, :]
                then(dve.tensor_scalar(hot, k("class"), idxf[:, which:which + 1], None, ALU.is_equal))
                if which == 1:
                    then(dve.tensor_reduce(slot_of[:, :], hot[:, 0:CLS - 1], X, ALU.add))
                    then(dve.tensor_scalar(hot[:, CLS - 1:CLS], slot_of[:, :], -1.0, 1.0, ALU.mult, ALU.add))
                    then(dve.memset(hot[:, CLS:E], 0.0))
                dve.sem_inc(s["routed"], 1)
                dve.wait_ge(s["routed_ps"], 2 * which + 1)
                then(dve.tensor_tensor(over, ps[:, 1, 0:E].rearrange("p (e o) -> p e o", o=1).to_broadcast([P, E, NQ]),
                                       k("quads").rearrange("p (o q) -> p o q", o=1).to_broadcast([P, E, NQ]),
                                       ALU.is_gt))
                then(dve.tensor_reduce(quads[:, :], over, X, ALU.add))
                then(dve.tensor_tensor(prior, k("less").rearrange("p (e f) -> p e f", e=E),
                                       quads[:, :].rearrange("p (o f) -> p o f", o=1).to_broadcast([P, E, E]),
                                       ALU.mult))
                then(dve.tensor_reduce(start[:, :], prior, X, ALU.add))
                then(dve.tensor_tensor(end[:, :], start[:, :], quads[:, :], ALU.add))
                then(dve.scalar_tensor_tensor(slot_e[:, :], start[:, :], float(QS), ps[:, 0, 0:E], ALU.mult, ALU.add))
                then(dve.tensor_tensor(slot_e[:, :], slot_e[:, :], hot, ALU.mult))
                then(dve.tensor_reduce(slot_of[:, :], slot_e[:, :], X, ALU.add))
                dve.tensor_scalar(placed, k("slot"), slot_of[:, 0:1], None, ALU.is_equal)\
                    .then_inc(s["routed"], 1)
                dve.tensor_copy(start_i[:, which, :], start[0:1, :])
                dve.tensor_copy(end_i[:, which, :], end[0:1, :])
                dve.wait_ge(s["routed_ps"], 2 * which + 2)
                then(dve.tensor_copy(slot_i[:, which, :], ps[0:1, 6, 0:B]))
                then(dve.tensor_copy(srow, ps[0:1, 2, 0:A_SLOTS]))
                if which == 0:
                    then(dve.tensor_scalar(src_i[:, 0, :], srow, float(B), float(B - 1), ALU.add, ALU.min))
                else:
                    then(dve.tensor_scalar(sempty, srow, -0.5, None, ALU.is_gt))
                    then(dve.tensor_tensor(sempty, sempty, k("slot4")[0:1, :], ALU.mult))
                    then(dve.tensor_scalar(dst_i[:, 0, 0:QS], k("slot")[0:1, 0:QS], float(B), None, ALU.add))
                    then(dve.scalar_tensor_tensor(dst_i[:, 0, QS:], srow[:, 0:C_SLOTS], float(B),
                                                  sempty[:, 0:C_SLOTS], ALU.add, ALU.add))
                then(dve.tensor_tensor(ended.rearrange("p (g e) -> p g e", e=E),
                                       k("slot")[0:1, 0:A_TILES + 1].rearrange("p (g o) -> p g o", o=1)
                                       .to_broadcast([1, A_TILES + 1, E]),
                                       end[0:1, :].rearrange("p (o e) -> p o e", o=1)
                                       .to_broadcast([1, A_TILES + 1, E]), ALU.is_gt))
                then(dve.tensor_reduce(last_f, ended.rearrange("p (g e) -> p g e", e=E), X, ALU.add))
                then(dve.tensor_scalar(last_of[:, which, :], last_f, float((E, CLS)[which] - 1), None, ALU.min))
                dve.sem_inc(s["route_ready"], 1)

            dve.tensor_scalar(piece_i[:, 0, :], k("slot")[0:1, 0:A_TILES + 1], float(NQ - 1), None, ALU.min)\
                .then_inc(s["route_ready"], 1)

            dve.wait_ge(s["setup_ps"], 1)
            then(dve.tensor_copy(cols[:, :], ps[:, 7, 0:COLS_W]))
            dve.wait_ge(s["setup_ps"], 2)
            dve.tensor_copy(gw1_t[:, :, :], ps[:, 3, 0:KC * S].rearrange("p (c n) -> p c n", c=KC))\
                .then_inc(s["turned"], 1)
            dve.tensor_copy(resp_t, ps[0:R, 5, 0:D]).then_inc(s["turned"], 1)
            a, z = COLS["L1_cond_bq"]
            dve.tensor_scalar(bq[:, :], cols[:, a:z], HD ** -0.5, None, ALU.mult)
            for c in range(KC):
                last = dve.tensor_scalar(bk_head[:, c, :], k("head"), col("L1_cond_bk", c), None, ALU.mult)
            last.then_inc(s["turned"], 1)
            dve.wait_ge(s["rows_in"], 16 * (1 + len(EROWS)))
            dve.tensor_tensor(resp_bias[:, :], row("L2_cond_resp_b", 1)[:, 0, :], row("L2_cond_safety_bias", 1)[:, 0, :],
                              ALU.add)
            dve.tensor_scalar(gb2[:, :], gb2[:, :], -1.0, None, ALU.mult)
            dve.wait_ge(s["small_in"], 16 * 11)
            then(dve.tensor_copy(tf, tstep[:, :]))
            then(dve.tensor_scalar(tq, tf, 0.01, None, ALU.mult))
            then(dve.scalar_tensor_tensor(tr, tq, -64.0, tf, ALU.mult, ALU.add))
            then(dve.scalar_tensor_tensor(tr, tq, -32.0, tr, ALU.mult, ALU.add))
            then(dve.scalar_tensor_tensor(tr, tq, -4.0, tr, ALU.mult, ALU.add))
            then(dve.scalar_tensor_tensor(tq, tr, 0.01, tq, ALU.mult, ALU.add))
            then(dve.tensor_scalar(tq, tq, 4000.0, None, ALU.mult))
            then(dve.tensor_scalar(ang, tq, k("freq"), None, ALU.mult))
            for half_n, shift in enumerate((0.0, 0.25)):
                n, v = turns[:, half_n, :], wrap[:, half_n, :]
                then(dve.tensor_scalar(n, ang, 0.5 / np.pi, shift, ALU.mult, ALU.add))
                then(dve.tensor_scalar(n, n, ROUNDER, None, ALU.add))
                then(dve.tensor_scalar(n, n, -ROUNDER, None, ALU.add))
                then(dve.scalar_tensor_tensor(v, n, -TURN1, ang, ALU.mult, ALU.add))
                then(dve.scalar_tensor_tensor(v, n, -TURN2, v, ALU.mult, ALU.add))
                then(dve.scalar_tensor_tensor(v, n, -TURN3, v, ALU.mult, ALU.add))
                then(dve.tensor_scalar(v, v, 2 * np.pi * shift, None, ALU.add))
                then(dve.tensor_scalar(v, v, HALF_TURN, -HALF_TURN, ALU.min, ALU.max))
            dve.sem_inc(s["wrap_ready"], 1)
            dve.wait_ge(s["setup_ps"], 4)
            then(dve.tensor_tensor(emb, bank(6), b_ada, ALU.add))
            dve.tensor_scalar(emb[:, 0:D], emb[:, 0:D], 1.0, None, ALU.add).then_inc(s["emb_done"], 1)
            dve.tensor_copy(uvt[:, :], ps[0:2 * R, 4, 0:D]).then_inc(s["turned"], 1)

            dve.wait_ge(s["setup_act"], 3)
            for b2 in range(2):
                then(dve.tensor_scalar(modden[b2 * S:(b2 + 1) * S, :],
                                       safety[b2 * S:(b2 + 1) * S, :].rearrange("p (n b) -> p n b", b=2)[:, :, b2],
                                       1.0, None, ALU.add))

            def low(out_t, whole, high):
                return dve.tensor_tensor(out_t, whole, high.bitcast(F32), ALU.subtract)

            def split_hidden(j, sem_hi, n_hi, sem_split, at=None):
                f = slice(2 * j, 2 * j + 2) if at is None else slice(at, at + 2)
                dve.tensor_copy(hid_h[:, f, :], hid[:, f, :]).then_inc(sem_hi, 1)
                dve.wait_ge(sem_hi, n_hi)
                low(hid_l[:, f, :], hid[:, f, :], hid_h[:, f, :]).then_inc(sem_split, 1)

            def layer_stats(src, sem_stat, n_stat, sem_var, eps, first=False):
                stats_t, mv_t, vare_t = (stats1, mv1, vare1) if first else (stats, mv, vare)
                for p in range(PAIRS):
                    last = dve.bn_stats(stats_t[:, p, :], src[:, p, :])
                last.then_inc(sem_stat, 1)
                dve.wait_ge(sem_stat, apart(dve, n_stat - 1))
                for p in range(PAIRS):
                    last = dve.bn_aggr(mv_t[:, p, :], stats_t[:, p, :])
                last.then_inc(sem_stat, 1)
                dve.wait_ge(sem_stat, n_stat)
                if src is res:
                    dve.tensor_scalar(neg_mean[:, :], mv_t[:, :, 0], -1.0, None, ALU.mult)
                dve.tensor_scalar(vare_t[:, :], mv_t[:, :, 1], eps, None, ALU.add).then_inc(sem_var, 1)

            xT_ps = bank(0, "p (c n) -> p c n", c=KC)
            o_ps = bank(5, "p (a n) -> p a n", a=PAIRS)

            def a_xlo(g):
                dve.wait_ge(s["a_xh"], g + 1)
                low(xl[:, :, :], xT_ps, xh[:, :, :]).then_inc(s["a_xl"], 1)

            def finish(pre, g, base, eps):
                dve.wait_ge(s[pre + "_xb"], g)
                dve.wait_ge(s[pre + "_norm"], g)
                dve.wait_ge(s["a_fc2" if pre == "a" else "c_out_ps"], g)
                dve.tensor_tensor(res[:, :, :], o_ps, base, ALU.add).then_inc(s[pre + "_res"], 1)
                dve.wait_ge(s[pre + "_res"], g + 1)
                layer_stats(res, s[pre + "_stat"], 2 * g + 2, s[pre + "_var"], eps)

            def gs_select(i):
                dve.tensor_copy(sel[:, :, :], k("pick")[0:2 * R, :].rearrange("p (a j) -> p a j", a=2)
                                [:, :, bass.ds(i, 1)].to_broadcast([2 * R, 2, R])).then_inc(s["gs_sel"], 1)

            def gs_dot(i):
                dve.wait_ge(s["gs_norm2"], i + 1)
                dve.tensor_tensor_reduce(junk, ps[0:2 * R, 6, 0:D], uvt, 1.0, 0.0, ALU.mult, ALU.add,
                                         gs[:, 1:2]).then_inc(s["gs_dot"], 1)

            def gs_step(i):
                dve.wait_ge(s["gs_norm"], i + 1)
                dve.tensor_scalar(gs[:, 3:4], gs[:, 2:3], 1e-8, None, ALU.add).then_inc(s["gs_chain"], 1)
                dve.wait_ge(s["gs_chain"], 4 * i + 1)
                dve.tensor_tensor(gs[:, 4:5], gs[:, 3:4], gs[:, 3:4], ALU.mult).then_inc(s["gs_chain"], 1)
                dve.wait_ge(s["gs_chain"], 4 * i + 2)
                dve.reciprocal(gs[:, 5:6], gs[:, 4:5]).then_inc(s["gs_chain"], 1)
                dve.wait_ge(s["gs_chain"], 4 * i + 3)
                dve.wait_ge(s["gs_dot"], i + 1)
                dve.scalar_tensor_tensor(gs[:, 6:7], gs[:, 1:2], gs[:, 5:6], k("later")[0:2 * R, bass.ds(i, 1)],
                                         ALU.mult, ALU.mult).then_inc(s["gs_chain"], 1)
                dve.wait_ge(s["gs_chain"], 4 * i + 4)
                dve.scalar_tensor_tensor(uvt, ps[0:2 * R, 6, 0:D], gs[:, 6:7], uvt, ALU.mult, ALU.add)\
                    .then_inc(s["gs_step"], 1)

            def a_weight(e, n):
                hi, lo, staged = w_piece(n)
                dve.tensor_copy(hi, staged).then_inc(s["a_w_hi"], 1)
                dve.wait_ge(s["a_w_hi"], 2 * e + n + 1)
                low(lo, staged, hi).then_inc(s["a_w_lo"], 1)

            def a_tile(g):
                dve.wait_ge(s["gs_step"], g)
                gs_select(g)
                finish("a", g, xb[:, :, :], 1e-12)
                for j in range(FC // 2):
                    dve.wait_ge(s["a_gelu"], g * (FC // 2) + j + 1)
                    split_hidden(j, s["a_hi"], g * (FC // 2) + j + 1, s["a_split"])
                    if j == 2:
                        gs_dot(g)
                gs_step(g)
                a_xlo(g + 1)

            dve.memset(bank(5), 0.0).then_inc(s["blank_ps"], 1)
            a_xlo(0)
            dve.wait_ge(s["blank_ps"], 1)
            dve.wait_ge(s["blank_xb"], 1)
            with dve.Fori(0, E) as e:
                dve.wait_ge(s["a_w_in"], e * 32 + 32)
                a_weight(e, 0)
                a_weight(e, 1)
                g0, g1 = bounds(dve, 0, e)
                with dve.Fori(g0, g1) as g:
                    a_tile(g)
            n_a = total(dve, 0)
            finish("a", n_a, xb[:, :, :], 1e-12)
            dve.wait_ge(s["emb_out"], 16)

            dve.wait_ge(s["gs_step"], n_a)
            then(dve.tensor_tensor_reduce(junk[:, :], uvt[:, :], uvt[:, :], 1.0, 0.0, ALU.mult, ALU.add, gs[:, 0:1]))
            dve.sem_inc(s["gs_dot"], 1)
            dve.wait_ge(s["gs_norm"], n_a + 1)
            then(dve.tensor_scalar(gs[:, 3:4], gs[:, 2:3], 1e-8, None, ALU.add))
            then(dve.reciprocal(gs[:, 4:5], gs[:, 3:4]))
            then(dve.tensor_scalar(uvt[:, :], uvt[:, :], gs[:, 4:5], None, ALU.mult))
            dve.tensor_copy(qv[:, :], uvt[R:2 * R, :]).then_inc(s["gs_done"], 1)

            dve.wait_ge(s["m_ps"], 1)
            dve.tensor_copy(basis_t[:, :, :], ps[:, 1, :].rearrange("p (c n) -> p c n", c=KC)).then_inc(s["m_sb"], 1)
            dve.wait_ge(s["m_ps"], 2)
            dve.tensor_copy(c_t, ps[0:R, 2, 0:D]).then_inc(s["m_sb"], 1)
            dve.wait_ge(s["m_hi_ready"], 1)
            dve.tensor_tensor(m_lo[:, :, :], ps[:, 3, :].rearrange("p (c n) -> p c n", c=KC),
                              m_hi[:, :, :].bitcast(F32), ALU.subtract).then_inc(s["m_ready"], 1)

            def raw_low(n):
                dve.wait_ge(s["raw_hi"], n + 1)
                low(wc_lo[:, raw_cols[n]], raws[n], wc_hi[:, raw_cols[n]]).then_inc(s["raw_lo"], 1)

            dve.wait_ge(s["a_out"], (n_a + 1) * 16)
            dve.memset(vblk, 0.0).then_inc(s["vblk_zero"], 1)
            dve.wait_ge(s["vblk_zero"], 1)
            xT7 = bank(7, "p (c n) -> p c n", c=KC)

            def normalise(dst, src, mean, inverse):
                for p in range(PAIRS):
                    last = dve.tensor_scalar(dst[:, p, :], src[:, p, :], mean[:, p, 0:1], inverse[:, p:p + 1],
                                             ALU.subtract, ALU.mult)
                return last

            def b_ln1_stats(i):
                dve.wait_ge(s["b_x_in"], i * (16 * QS) + 16 * QS)
                layer_stats(xin, s["b_stat"], 2 * i + 2, s["b_var"], 1e-5, first=True)

            def b_ln1(i, again=True):
                dve.wait_ge(s["b_rstd"], i + 1)
                if again:
                    dve.wait_ge(s["b_xT"], i)
                    dve.wait_ge(s["b_xb"], i)
                normalise(xm, xin, mv1, rstd1).then_inc(s["b_norm"], 1)

            def b_xlo(i):
                dve.wait_ge(s["b_xh"], i + 1)
                low(xl[:, :, :], bank(4, "p (c n) -> p c n", c=KC), xh[:, :, :]).then_inc(s["b_xl"], 1)

            def b_values(i):
                dve.wait_ge(s["b_qkv"], 3 * i + 3)
                bv = row("L1_cond_bv").rearrange("q a (g h d) -> q a g h d", g=NH // 2, h=2)
                vp = bank(2, "q (a g h d) -> q a g h d", a=PAIRS, g=NH // 2, h=2)
                vb = vblk.rearrange("q a b (g h d) -> q a b g h d", g=NH // 2, h=2)
                for b2 in range(2):
                    for par in range(2):
                        here, to = slice(b2 * S, (b2 + 1) * S), slice(par * S, (par + 1) * S)
                        last = dve.tensor_tensor(vb[to, :, b2, :, par, :], vp[here, :, :, par, :],
                                                 bv[here, :, :, par, :], ALU.add)
                last.then_inc(s["b_v"], 1)

            def b_add(i, p):
                if p == 0:
                    dve.wait_ge(s["b_score"], i + 1)
                dve.wait_ge(s["b_bias"], 2 * i + p + 1)
                v = lambda t: t[:, p, :].rearrange("q (c r n) -> q r c n", c=KC, r=4)
                dve.tensor_tensor(v(att), ps[:, 0:4, p * TQ:(p + 1) * TQ].rearrange("q r (c n) -> q r c n", c=KC),
                                  v(bias), ALU.add).then_inc(s["b_added"], 1)

            def b_maximum(i, p):
                dve.wait_ge(s["b_added"], 2 * i + p + 1)
                dve.tensor_reduce(amax[:, p, :], att[:, p, :].rearrange("q (h k) -> q h k", h=NH), X, ALU.max)\
                    .then_inc(s["b_max"], 1)

            def b_softmax_sum(i):
                for p in range(PAIRS):
                    dve.wait_ge(s["b_exp"], 2 * i + p + 1)
                    dve.tensor_reduce(asum[:, p, :], att[:, p, :].rearrange("q (h k) -> q h k", h=NH), X, ALU.add)\
                        .then_inc(s["b_sum"], 1)
                    dve.wait_ge(s["b_sum"], 2 * i + p + 1)
                    dve.reciprocal(asum[:, p, :], asum[:, p, :]).then_inc(s["b_rsum"], 1)

            def b_ctx(i):
                dve.wait_ge(s["b_pv"], i + 1)
                dve.wait_ge(s["b_rsum"], 2 * i + 2)
                dve.tensor_tensor(ctxn.rearrange("q a (h d) -> q a h d", h=NH),
                                  bank(4, "q (a h d) -> q a h d", a=PAIRS, h=NH),
                                  asum[:, :, :].rearrange("q a (h o) -> q a h o", o=1)
                                  .to_broadcast([P, PAIRS, NH, HD]), ALU.mult).then_inc(s["b_ctx"], 1)

            def b_ctx_low(i):
                dve.wait_ge(s["b_ctxh"], i + 1)
                low(ctx_l[:, :, :], bank(5, "p (c n) -> p c n", c=KC), ctx_h[:, :, :]).then_inc(s["b_ctxl"], 1)

            def b_ln2(i):
                dve.wait_ge(s["b_wo"], i + 1)
                dve.wait_ge(s["b_xb"], i + 1)
                dve.tensor_tensor(x1[:, :, :], bank(3, "p (a n) -> p a n", a=PAIRS), xb[:, :, :], ALU.add)\
                    .then_inc(s["b_x1"], 1)
                dve.wait_ge(s["b_x1"], i + 1)
                layer_stats(x1, s["b_stat2"], 2 * i + 2, s["b_var2"], 1e-5)
                dve.wait_ge(s["b_rstd2"], i + 1)
                normalise(xn, x1, mv, rstd).then_inc(s["b_xn"], 1)

            def b_ffn_in(i):
                dve.wait_ge(s["b_ht"], i + 1)
                dve.tensor_copy(ht_h[:, :, :], ht[:, :, :]).then_inc(s["b_hth"], 1)
                dve.wait_ge(s["b_hth"], i + 1)
                low(ht_l[:, :, :], ht[:, :, :], ht_h[:, :, :]).then_inc(s["b_htl"], 1)

            def b_ffn(i, j):
                dve.wait_ge(s["b_gelu"], i * (FC // 2) + j + 1)
                split_hidden(j, s["b_hi"], i * (FC // 2) + j + 1, s["b_split"])

            def b_l2_in(i):
                dve.wait_ge(s["b_fc2"], i + 1)
                dve.wait_ge(s["b_x1b"], i + 1)
                dve.wait_ge(s["b_x3"], i)
                dve.tensor_tensor(x2, bank(6, "p (a n) -> p a n", a=PAIRS), x1b, ALU.add).then_inc(s["b_x2"], 1)

            def b_l2_split(i):
                dve.wait_ge(s["b_x2h"], i + 1)
                low(hid_l[:, 0:KC, :], xT7, hid_h[:, 0:KC, :]).then_inc(s["b_x2l"], 1)

            def b_pooled(i):
                dve.tensor_reduce(pooled[:, :, :], xT7.rearrange("p c (b s) -> p c b s", b=QS), X, ALU.add)\
                    .then_inc(s["b_pool"], 1)

            def b_correct(i):
                dve.wait_ge(s["b_resp"], i + 1)
                dve.wait_ge(s["b_out"], i * (16 * QS))
                dve.tensor_tensor(yout[:, :, :], bank(6, "p (a n) -> p a n", a=PAIRS),
                                  resp_bias[:, :].rearrange("p (o d) -> p o d", o=1).to_broadcast([P, PAIRS, D]),
                                  ALU.add).then_inc(s["b_corr"], 1)

            def b_l2_out(i):
                dve.wait_ge(s["b_expz"], i + 1)
                dve.scalar_tensor_tensor(den[:, :], expz[:, :], 1.0, modden[:, bass.ds(i * PAIRS, PAIRS)],
                                         ALU.add, ALU.mult).then_inc(s["b_strength"], 1)
                dve.wait_ge(s["b_strength"], 2 * i + 1)
                dve.reciprocal(strength[:, :], den[:, :]).then_inc(s["b_strength"], 1)
                dve.wait_ge(s["b_strength"], 2 * i + 2)
                dve.wait_ge(s["b_corr"], i + 1)
                for p in range(PAIRS):
                    last = dve.scalar_tensor_tensor(yout[:, p, :], yout[:, p, :], strength[:, p:p + 1], x2[:, p, :],
                                                    ALU.mult, ALU.add)
                last.then_inc(s["b_x3"], 1)

            def b_step(i, here=True, prev=True, before=True, after=True):
                if prev:
                    b_ffn_in(i - 1)
                if before:
                    b_correct(i - 2)
                if here:
                    b_add(i, 0)
                    b_maximum(i, 0)
                    b_add(i, 1)
                if prev:
                    b_ffn(i - 1, 0)
                if here:
                    b_maximum(i, 1)
                if prev:
                    for j in range(1, FC // 2):
                        b_ffn(i - 1, j)
                if before:
                    b_l2_out(i - 2)
                if after:
                    b_ln1_stats(i + 1)
                if after:
                    b_ln1(i + 1)
                if here:
                    b_softmax_sum(i)
                if prev:
                    b_l2_in(i - 1)
                if here:
                    b_ctx(i)
                if prev:
                    b_l2_split(i - 1)
                if here:
                    b_ctx_low(i)
                if after:
                    b_xlo(i + 1)
                if prev:
                    b_pooled(i - 1)
                if here:
                    b_ln2(i)
                if after:
                    b_values(i + 1)

            b_ln1_stats(0)
            b_ln1(0, again=False)
            b_xlo(0)
            raw_low(0)
            raw_low(1)
            b_values(0)
            b_step(0, prev=False, before=False)
            raw_low(2)
            b_step(1, before=False)
            with dve.Fori(2, NQ - 1) as i:
                b_step(i)
            b_step(NQ - 1, after=False)
            b_step(NQ, here=False, after=False)
            b_correct(NQ - 1)
            b_l2_out(NQ - 1)

            def c_xlo(g):
                dve.wait_ge(s["c_xh"], g + 1)
                low(xl[:, :, :], xT_ps, xh[:, :, :]).then_inc(s["c_xl"], 1)

            def c_take(g):
                dve.wait_ge(s["c_x_in"], g * 16 + 16)
                dve.wait_ge(s["c_xT"], g)
                dve.tensor_copy(xin[:, :, :], x_ring[:, bass.ds(g % 2, 1), :]
                                .rearrange("p o (a d) -> p (o a) d", a=PAIRS)).then_inc(s["c_x"], 1)

            def c_finish(g):
                finish("c", g, xb_ring[:, bass.ds((g + 1) % 2, 1), :].rearrange("p o (a d) -> p (o a) d", a=PAIRS),
                       1e-5)

            dve.memset(bank(5), 0.0).then_inc(s["c_blank"], 1)
            dve.memset(zeros[:, :, :], 0.0).then_inc(s["c_blank"], 1)
            dve.memset(xb_ring[:, 1, :], 0.0).then_inc(s["c_blank"], 1)
            c_take(0)
            c_xlo(0)
            dve.wait_ge(s["c_blank"], 3)
            for c, (w1, w2, w3) in enumerate(BRANCHES):
                g0, g1 = bounds(dve, 1, c)
                n1 = w[w1][0].shape[2] // P
                with dve.Fori(0, dve.snap(g1 - g0)) as t:
                    g = g0 + t
                    c_take(g + 1)
                    c_finish(g)
                    for j in range(n1 // 2):
                        dve.wait_ge(s[f"c_gelu_{c}"], t * (n1 // 2) + j + 1)
                        split_hidden(j, s[f"c_hi_{c}"], t * (n1 // 2) + j + 1, s[f"c_split_{c}"])
                    c_xlo(g + 1)
                    if w3:
                        dve.wait_ge(s["c_gelu2"], t + 1)
                        split_hidden(0, s["c_hi2"], t + 1, s["c_split2"], at=4)
            g0, g1 = bounds(dve, 1, CLS - 1)
            with dve.Fori(g0, g1) as g:
                c_take(g + 1)
                c_finish(g)
                c_xlo(g + 1)
            c_finish(g1)

        @block.gpsimd
        def _(pool):
            pool.memset(minus_half[:, :], -0.5).then_inc(s["half_ready"], 1)
            pool.memset(half[:, :], 0.5).then_inc(s["half_ready"], 1)
            pool.memset(masked[:, :, :], MASKED).then_inc(s["half_ready"], 1)
            pool.wait_ge(s["half_ready"], 3)

            def inverse_root(sem_var, n, sem_rstd, first=False):
                pool.wait_ge(sem_var, n)
                to, of = (rstd1, vare1) if first else (rstd, vare)
                pool.tensor_tensor(to[:, :], of[:, :], minus_half[:, :], ALU.pow).then_inc(sem_rstd, 1)

            def finish(pre, n, gain, offset, between=None, to=None, stored=None):
                inverse_root(s[pre + "_var"], n + 1, s[pre + "_rstd"])
                pool.wait_ge(s[pre + "_rstd"], n + 1)
                pool.tensor_tensor(shift[:, :], neg_mean[:, :], rstd[:, :], ALU.mult).then_inc(s[pre + "_shift"], 1)
                if between:
                    between()
                pool.wait_ge(s[pre + "_norm"], n + 1)
                pool.tensor_tensor(yout[:, :, :], yout[:, :, :], gain, ALU.mult).then_inc(s[pre + "_gain"], 1)
                pool.wait_ge(s[pre + "_gain"], n + 1 if stored is None else apart(pool, n + 1))
                if stored is not None:
                    pool.wait_ge(s[pre + "_out"], stored)
                pool.tensor_tensor(yout[:, :, :] if to is None else to, yout[:, :, :], offset, ALU.add)\
                    .then_inc(s[pre + "_y"], 1)

            def a_finish(n, between=None):
                e = pool.value_load(last_of[0:1, 0, bass.ds(n, 1)], min_val=0, max_val=E - 1)
                finish("a", n, erows[:, 1, bass.ds(e, 1), :].to_broadcast([P, PAIRS, D]),
                       erows[:, 2, bass.ds(e, 1), :].to_broadcast([P, PAIRS, D]), between)

            def a_tiles(e):
                g0, g1 = bounds(pool, 0, e)
                with pool.Fori(g0, g1) as g:
                    pool.wait_ge(s["a_x_in"], g * (16 * QS) + 16 * QS)
                    pool.wait_ge(s["a_res"], g + 1)
                    pool.tensor_tensor(xb[:, :, :], xin[:, :, :],
                                       erows[:, 0, bass.ds(e, 1), :].to_broadcast([P, PAIRS, D]), ALU.add)\
                        .then_inc(s["a_xb"], 1)

                    def gs_norm():
                        pool.wait_ge(s["gs_norm2"], g + 1)
                        pool.tensor_tensor(gs[:, 2:3], gs[:, 0:1], half[0:2 * R, :], ALU.pow)\
                            .then_inc(s["gs_norm"], 1)
                    a_finish(g, gs_norm)
                    n = pool.value_load(piece_i[0:1, 0, bass.ds(g, 1)], min_val=0, max_val=NQ - 1)
                    v = bass.ds(n * PIECE, PIECE)
                    pool.wait_ge(s["b_w_in"], apart(pool, g * 16 + 16))
                    pool.tensor_copy(wb_hi[:, v], piece).then_inc(s["b_w_hi"], 1)
                    pool.wait_ge(s["b_w_hi"], apart(pool, g + 1))
                    pool.tensor_tensor(wb_lo[:, v], piece, wb_hi[:, v].bitcast(F32), ALU.subtract)\
                        .then_inc(s["b_w_lo"], 1)

            def a_weight_lo(e, n):
                hi, lo, staged = w_piece(n)
                pool.wait_ge(s["a_w_mid"], apart(pool, 2 * e + n - 1))
                pool.tensor_tensor(lo, staged, hi.bitcast(F32), ALU.subtract).then_inc(s["a_w_last"], 1)

            pool.wait_ge(s["rows_in"], 16 * (1 + len(EROWS)))
            pool.wait_ge(s["turned"], 4)
            pool.memset(xb[:, :, :], 0.0).then_inc(s["blank_xb"], 1)
            pool.wait_ge(s["route_ready"], 3)
            with pool.Fori(0, E) as e:
                a_weight_lo(e, 2)
                a_weight_lo(e, 3)
                a_tiles(e)
            n_a = total(pool, 0)
            pool.wait_ge(s["a_res"], apart(pool, n_a + 1))
            pool.memset(xb[:, :, :], 0.0).then_inc(s["a_xb"], 1)
            a_finish(n_a)
            pool.wait_ge(s["gs_dot"], n_a + 1)
            pool.tensor_tensor(gs[:, 2:3], gs[:, 0:1], half[0:2 * R, :], ALU.pow).then_inc(s["gs_norm"], 1)

            pool.wait_ge(s["a_out"], apart(pool, (n_a + 1) * 16))
            pool.wait_ge(s["mask_in"], 32)

            def b_masks(i):
                pool.tensor_copy(maskf[:, :, :], mask8[:, bass.ds(i * PAIRS, PAIRS), :]).then_inc(s["b_mask"], 1)
                pool.wait_ge(s["b_mask"], 2 * i + 1)
                pool.tensor_tensor(maskf[:, :, :], maskf[:, :, :], masked[:, :, :].to_broadcast([P, PAIRS, S]),
                                   ALU.mult).then_inc(s["b_mask"], 1)
                pool.wait_ge(s["b_mask"], 2 * i + 2)
                pool.wait_ge(s["b_bias_in"], i * (16 * QS) + 16 * QS)
                for p in range(PAIRS):
                    v = bias[:, p, :].rearrange("q (h k) -> q h k", h=NH)
                    pool.tensor_tensor(v, v, maskf[:, p:p + 1, :].to_broadcast([P, NH, S]), ALU.add)\
                        .then_inc(s["b_bias"], 1)

            def b_modulate(i):
                inverse_root(s["b_var"], i + 1, s["b_rstd"], first=True)
                pool.wait_ge(s["b_norm"], i + 1)
                pool.wait_ge(s["b_ada_in"], i * (16 * QS) + 16 * QS)
                pool.tensor_tensor(xm[:, :, :], xm[:, :, :], ada[:, :, 0:D], ALU.mult).then_inc(s["b_scaled"], 1)
                pool.wait_ge(s["b_scaled"], i + 1)
                pool.tensor_tensor(xm[:, :, :], xm[:, :, :], ada[:, :, D:2 * D], ALU.add).then_inc(s["b_xm"], 1)

            def b_base1(i):
                pool.wait_ge(s["b_xm"], i + 1)
                pool.tensor_tensor(xb[:, :, :], xm[:, :, :], row("L1_cond_bo"), ALU.add).then_inc(s["b_xb"], 1)

            def b_subtract(i):
                for p in range(PAIRS):
                    pool.wait_ge(s["b_max"], 2 * i + p + 1)
                    v = att[:, p, :].rearrange("q (h k) -> q h k", h=NH)
                    pool.tensor_tensor(v, v, amax[:, p, :].rearrange("q (h o) -> q h o", o=1).to_broadcast([P, NH, S]),
                                       ALU.subtract).then_inc(s["b_sub"], 1)

            def b_base2(i):
                inverse_root(s["b_var2"], i + 1, s["b_rstd2"])
                pool.wait_ge(s["b_x1"], i + 1)
                pool.tensor_tensor(x1b, x1[:, :, :], row("L1_cond_b2"), ALU.add).then_inc(s["b_x1b"], 1)

            def b_step(i, after=True):
                b_subtract(i)
                if after:
                    b_modulate(i + 1)
                    b_masks(i + 1)
                b_base2(i)
                if after:
                    b_base1(i + 1)

            b_modulate(0)
            b_masks(0)
            b_base1(0)
            with pool.Fori(0, NQ - 1) as i:
                b_step(i)
            b_step(NQ - 1, after=False)

            def c_base(g):
                c = pool.value_load(last_of[0:1, 1, bass.ds(g + 1, 1)], min_val=0, max_val=CLS - 1)
                pool.wait_ge(s["c_x_in"], g * 16 + 16)
                pool.tensor_tensor(xb_ring[:, bass.ds(g % 2, 1), :].rearrange("p o (a d) -> p (o a) d", a=PAIRS),
                                   x_ring[:, bass.ds(g % 2, 1), :].rearrange("p o (a d) -> p (o a) d", a=PAIRS),
                                   rows[:, bass.ds(c + ROWS_OF[OUT_BIAS[0]][0], 1), :].to_broadcast([P, PAIRS, D]),
                                   ALU.add).then_inc(s["c_xb"], 1)

            n_c = total(pool, 1)
            pool.wait_ge(s["c_blank"], 3)

            def c_tile(g, stored):
                finish("c", g, row("L3_cond_gamma"), row("L3_cond_beta"),
                       lambda: c_base(g + 1),
                       y_ring[:, bass.ds(g % 2, 1), :].rearrange("p o (a d) -> p (o a) d", a=PAIRS), stored)

            c_base(0)
            c_tile(0, None)
            with pool.Fori(0, n_c) as t:
                c_tile(t + 1, t * (16 * QS))


PACKED = {name for name, _, _ in WB + WC} | set(COLS) | (set(ROWS_OF) - {"none"}) | set(EROWS)


def pack(inputs):

    def chunks(names):
        return np.concatenate([np.asarray(inputs[n]).reshape(k, P, w).transpose(1, 0, 2).reshape(P, k * w)
                               for n, k, w in names], 1)

    return {"wb": chunks(WB), "wc": chunks(WC),
            "cols_packed": np.concatenate([np.asarray(inputs[n]).reshape(-1, P) for n in COLS]),
            "rows_packed": np.concatenate([np.zeros((1, D), np.float32) if n == "none"
                                           else np.asarray(inputs[n]).reshape(1, D) for n in ROWS_OF]),
            "erows_packed": np.stack([np.asarray(inputs[n]) for n in EROWS])}


def kernel(**inputs):
    import concourse.bacc as bacc
    from concourse.bass_utils import run_bass_kernel_spmd

    nc = bacc.Bacc("TRN2", target_bir_lowering=False, num_devices=1)
    arrays, aps = {}, {}
    packed = pack(inputs)
    for name, a in list(packed.items()) + [(n, a) for n, a in inputs.items() if n not in PACKED]:
        a = np.ascontiguousarray(a)
        arrays[name] = a
        aps[name] = nc.dram_tensor(name, a.shape, mybir.dt.from_np(a.dtype), kind="ExternalInput").ap()
    arrays["const"] = constants()
    const = nc.dram_tensor("const", (P, CONST_W), F32, kind="ExternalInput").ap()
    out = nc.dram_tensor("out", (ROWS, S, D), F32, kind="ExternalOutput").ap()
    build(nc, aps, const, out)
    r = run_bass_kernel_spmd(nc, [arrays], core_ids=[0])
    return r.results[0]["out"][:B]
```
